# Optimizing a Trainium2 kernel written in Bass

```python
import numpy as np
import jax
import jax.numpy as jnp

def _softmax(x, axis=-1):
    return jax.nn.softmax(x, axis=axis)

def _gelu(x):
    return jax.nn.gelu(x, approximate=True)

def _silu(x):
    return jax.nn.silu(x)

def _sigmoid(x):
    return jax.nn.sigmoid(x)

def _layernorm(x, axis=-1, eps=1e-05):
    m = jnp.mean(x, axis=axis, keepdims=True)
    v = jnp.var(x, axis=axis, keepdims=True)
    return (x - m) / jnp.sqrt(v + eps)

def _scatter_add(tgt, idx, src, axis=0):
    return tgt.at[idx].add(src)

def _segment_sum(src, seg, n):
    return jax.ops.segment_sum(src, seg, n)
kernel_name = 'mk_lm_tower_d2_tok_ids768_r4_989aa0'

def setup_inputs(seed: int=0):
    np.random.seed(seed)
    _w = jnp.asarray

    def _rec_inputs():
        import jax
        import jax.numpy as jnp
        _rk = jax.random.key(seed)
        x = jax.random.randint(jax.random.fold_in(_rk, 1), (4, 512), 0, 12564, jnp.int32)
        return x
    x = _rec_inputs()

    def _L0_tok_setup():
        import jax, jax.numpy as jnp
        import numpy as np
        VOCAB = 50257
        EMBED_DIM = 192
        NUM_TUNE = 256
        key = jax.random.key(seed)
        k_ids, k_tune, k_base, k_train = jax.random.split(key, 4)
        input_ids = jax.random.randint(k_ids, (8, 1024), 0, VOCAB, dtype=jnp.int64)
        tune_ids = jnp.sort(jax.random.randint(k_tune, (NUM_TUNE,), 0, VOCAB, dtype=jnp.int64))
        base_weight = jax.random.normal(k_base, (VOCAB, EMBED_DIM), dtype=jnp.float32)
        train_weight = jax.random.normal(k_train, (NUM_TUNE, EMBED_DIM), dtype=jnp.float32)
        return {'input_ids': input_ids, 'tune_ids': tune_ids, 'base_weight': base_weight, 'train_weight': train_weight}
    _L0_tok_all = _L0_tok_setup()
    _L0_tok_in = {k: v for k, v in _L0_tok_all.items() if k in ('tune_ids', 'base_weight', 'train_weight')}
    del _L0_tok_all

    def _L0_attn_setup():
        import jax, jax.numpy as jnp
        import numpy as np
        DIM = 192
        NUM_HEADS = 12
        HEAD_DIM = DIM // NUM_HEADS
        SCALE = HEAD_DIM ** (-0.5)
        B, N = (4, 512)
        key = jax.random.key(seed)
        k1, k2, k3, k4 = jax.random.split(key, 4)
        x = jax.random.normal(k1, (B, N, DIM), dtype=jnp.float32)
        Wq = jax.random.normal(k2, (DIM, DIM), dtype=jnp.float32) * DIM ** (-0.5)
        Wkv = jax.random.normal(k3, (2 * DIM, DIM), dtype=jnp.float32) * DIM ** (-0.5)
        Wproj = jax.random.normal(k4, (DIM, DIM), dtype=jnp.float32) * DIM ** (-0.5)
        return {'x': x, 'Wq': Wq, 'Wkv': Wkv, 'Wproj': Wproj}
    _L0_attn_all = _L0_attn_setup()
    _L0_attn_in = {k: v for k, v in _L0_attn_all.items() if k in ('Wq', 'Wkv', 'Wproj')}
    del _L0_attn_all

    def _L0_ffn_setup():
        import jax, jax.numpy as jnp
        import numpy as np
        H = 192
        R = 64
        E = 8
        B, S = (8, 512)
        key = jax.random.key(seed)
        ks = jax.random.split(key, 10)
        s_in = 1.0 / np.sqrt(H)
        s_r = 1.0 / np.sqrt(R)
        return {'x': jax.random.normal(ks[0], (B, S, H), dtype=jnp.float32), 'enc_w': jax.random.uniform(ks[1], (H, R), jnp.float32, -s_in, s_in), 'enc_b': jax.random.uniform(ks[2], (R,), jnp.float32, -s_in, s_in), 'sw_w': jax.random.uniform(ks[3], (R, E), jnp.float32, -s_r, s_r), 'sw_b': jax.random.uniform(ks[4], (E,), jnp.float32, -s_r, s_r), 'w1': jax.random.uniform(ks[5], (E, H, R), jnp.float32, -s_in, s_in), 'b1': jax.random.uniform(ks[6], (E, R), jnp.float32, -s_in, s_in), 'w2': jax.random.uniform(ks[7], (E, R, H), jnp.float32, -s_r, s_r), 'b2': jax.random.uniform(ks[8], (E, H), jnp.float32, -s_r, s_r)}
    _L0_ffn_all = _L0_ffn_setup()
    _L0_ffn_in = {k: v for k, v in _L0_ffn_all.items() if k in ('enc_w', 'enc_b', 'sw_w', 'sw_b', 'w1', 'b1', 'w2', 'b2')}
    del _L0_ffn_all

    def _L1_attn_setup():
        import jax, jax.numpy as jnp
        import numpy as np
        B, S, HID = (4, 2048, 192)
        H, D, K = (12, 64, 16)
        KW = 4
        TTT_BASE_LR = 1.0
        ROPE_THETA = 10000.0
        ETA_DECAY_RATE = 0.0
        LN_EPS = 1e-05

        def causal_dwconv(x, w, b):
            S_ = x.shape[1]
            xp = jnp.pad(x, ((0, 0), (KW, 0), (0, 0)))
            out = b
            for k in range(KW):
                out = out + w[k] * xp[:, k:k + S_]
            return out

        def rope(x, cos, sin):
            xr = x.reshape(*x.shape[:-1], D // 2, 2)
            x1, x2 = (xr[..., 0], xr[..., 1])
            c = cos[None, :, None, :]
            s = sin[None, :, None, :]
            return jnp.stack([x1 * c - x2 * s, x1 * s + x2 * c], axis=-1).reshape(x.shape)

        def ln_fwd(x, g, b):
            mu = x.mean(-1, keepdims=True)
            var = x.var(-1, keepdims=True)
            return (x - mu) * jax.lax.rsqrt(var + LN_EPS) * g + b

        def ln_l2_bwd(x, target, g, b):
            mu = x.mean(-1, keepdims=True)
            var = x.var(-1, keepdims=True)
            std = jnp.sqrt(var + LN_EPS)
            xh = (x - mu) / std
            gx = (xh * g + b - target) * g
            return (gx - gx.mean(-1, keepdims=True) - xh * (gx * xh).mean(-1, keepdims=True)) / std

        def ttt_forward(x, wq, wv, wo, wg, conv_q_w, conv_q_b, conv_k_w, conv_k_b, lr_w, lr_b, learnable_token_idx, ttt_norm_scale, ttt_norm_bias, post_norm_scale, post_norm_bias, W1, b1):
            Bx, Sx, _ = x.shape
            n_mb = Sx // K
            xqk = x @ wq
            XQ = causal_dwconv(xqk, conv_q_w, conv_q_b).reshape(Bx, Sx, H, D)
            XK = causal_dwconv(xqk, conv_k_w, conv_k_b).reshape(Bx, Sx, H, D)
            XV = (x @ wv).reshape(Bx, Sx, H, D)
            inv_freq = 1.0 / ROPE_THETA ** (jnp.arange(0, D, 2, dtype=jnp.float32) / D)
            freqs = jnp.arange(Sx, dtype=jnp.float32)[:, None] * inv_freq[None, :]
            cos, sin = (jnp.cos(freqs), jnp.sin(freqs))
            XQ = rope(XQ, cos, sin)
            XK = rope(XK, cos, sin)
            token_idx = jnp.maximum(1.0 / jnp.arange(1, K + 1, dtype=jnp.float32) + learnable_token_idx, 0.0)
            ttt_lr = jax.nn.sigmoid(jnp.einsum('bsd,hd->bhs', x, lr_w) + lr_b[None, :, None])
            ttt_lr_eta = TTT_BASE_LR / D * ttt_lr
            decay = jnp.exp(ETA_DECAY_RATE * (jnp.arange(K, dtype=jnp.float32) - (K - 1)))
            eta = token_idx[None, None, None, :, None] * (ttt_lr_eta.reshape(Bx, H, n_mb, 1, K) * decay)
            to_mb = lambda t: t.reshape(Bx, n_mb, K, H, D).transpose(1, 0, 3, 2, 4)
            xs = (to_mb(XQ), to_mb(XK), to_mb(XV), eta.transpose(2, 0, 1, 3, 4))
            W1_0 = jnp.broadcast_to(W1[None], (Bx, H, D, D)) + 0.0
            b1_0 = jnp.broadcast_to(b1[None], (Bx, H, 1, D)) + 0.0
            tril = jnp.tril(jnp.ones((K, K), jnp.float32))

            def step(carry, inp):
                W1c, b1c = carry
                q, k, v, e = inp
                Z1 = jnp.einsum('bhkd,bhde->bhke', k, W1c) + b1c
                grad = ln_l2_bwd(Z1, v - k, ttt_norm_scale, ttt_norm_bias)
                Attn = jnp.einsum('bhid,bhjd->bhij', q, k) * tril
                b1_bar = b1c - jnp.einsum('bhij,bhjd->bhid', e * tril, grad)
                Z1_bar = jnp.einsum('bhkd,bhde->bhke', q, W1c) - jnp.einsum('bhij,bhjd->bhid', e * Attn, grad) + b1_bar
                last_e = e[..., -1, :, None]
                W1n = W1c - jnp.einsum('bhkd,bhke->bhde', last_e * k, grad)
                b1n = b1c - jnp.sum(last_e * grad, axis=-2, keepdims=True)
                out = q + ln_fwd(Z1_bar, ttt_norm_scale, ttt_norm_bias)
                return ((W1n, b1n), out)
            _, Z = jax.lax.scan(step, (W1_0, b1_0), xs)
            Z = Z.transpose(1, 0, 3, 2, 4).reshape(Bx, Sx, H * D)
            mu = Z.mean(-1, keepdims=True)
            var = Z.var(-1, keepdims=True)
            Zn = (Z - mu) * jax.lax.rsqrt(var + LN_EPS) * post_norm_scale + post_norm_bias
            gate = jax.nn.gelu(x @ wg)
            return Zn * gate @ wo
        key = jax.random.key(seed)
        ks = jax.random.split(key, 12)

        def randn(k, shape, scale):
            return jax.random.normal(k, shape, jnp.float32) * scale

        def lecun(k, fan_in, shape):
            return jax.random.normal(k, shape, jnp.float32) / np.sqrt(fan_in).astype(np.float32)
        return {'x': randn(ks[0], (B, S, HID), 1.0), 'wq': lecun(ks[1], HID, (HID, H * D)), 'wv': lecun(ks[2], HID, (HID, H * D)), 'wo': lecun(ks[3], H * D, (H * D, HID)), 'wg': lecun(ks[4], HID, (HID, H * D)), 'conv_q_w': randn(ks[5], (KW, H * D), 0.1), 'conv_q_b': jnp.zeros((H * D,), jnp.float32), 'conv_k_w': randn(ks[6], (KW, H * D), 0.1), 'conv_k_b': jnp.zeros((H * D,), jnp.float32), 'lr_w': randn(ks[7], (H, HID), 0.02), 'lr_b': jnp.zeros((H,), jnp.float32), 'learnable_token_idx': jnp.zeros((K,), jnp.float32), 'ttt_norm_scale': jnp.ones((H, 1, D), jnp.float32), 'ttt_norm_bias': jnp.zeros((H, 1, D), jnp.float32), 'post_norm_scale': jnp.ones((H * D,), jnp.float32), 'post_norm_bias': jnp.zeros((H * D,), jnp.float32), 'W1': randn(ks[8], (H, D, D), 0.02), 'b1': jnp.zeros((H, 1, D), jnp.float32)}
    _L1_attn_all = _L1_attn_setup()
    _L1_attn_in = {k: v for k, v in _L1_attn_all.items() if k in ('wq', 'wv', 'wo', 'wg', 'conv_q_w', 'conv_q_b', 'conv_k_w', 'conv_k_b', 'lr_w', 'lr_b', 'learnable_token_idx', 'ttt_norm_scale', 'ttt_norm_bias', 'post_norm_scale', 'post_norm_bias', 'W1', 'b1')}
    del _L1_attn_all

    def _L1_ffn_setup():
        import jax, jax.numpy as jnp
        import numpy as np
        B, L, D = (4, 256, 192)
        E, S, H = (32, 32, 768)
        EPS = 1e-12

        def _l2norm(v, axis):
            n = jnp.sqrt(jnp.sum(v * v, axis=axis, keepdims=True))
            return v / jnp.maximum(n, EPS)
        key = jax.random.key(seed)
        ks = jax.random.split(key, 6)
        x = jax.random.normal(ks[0], (B, L, D), dtype=jnp.float32)
        phi = jax.random.normal(ks[1], (D, E, S), dtype=jnp.float32) / np.sqrt(D)
        scale = jnp.ones((1,), dtype=jnp.float32)
        w1 = jax.random.normal(ks[2], (E, D, H), dtype=jnp.float32) / np.sqrt(D)
        b1 = jax.random.normal(ks[3], (E, H), dtype=jnp.float32) * 0.01
        w2 = jax.random.normal(ks[4], (E, H, D), dtype=jnp.float32) / np.sqrt(H)
        b2 = jax.random.normal(ks[5], (E, D), dtype=jnp.float32) * 0.01
        return {'x': x, 'phi': phi, 'scale': scale, 'w1': w1, 'b1': b1, 'w2': w2, 'b2': b2}
    _L1_ffn_all = _L1_ffn_setup()
    _L1_ffn_in = {k: v for k, v in _L1_ffn_all.items() if k in ('phi', 'scale', 'w1', 'b1', 'w2', 'b2')}
    del _L1_ffn_all
    return {'x': x, 'L0_tok_tune_ids': _L0_tok_in['tune_ids'], 'L0_tok_base_weight': _L0_tok_in['base_weight'], 'L0_tok_train_weight': _L0_tok_in['train_weight'], 'L0_attn_Wq': _L0_attn_in['Wq'], 'L0_attn_Wkv': _L0_attn_in['Wkv'], 'L0_attn_Wproj': _L0_attn_in['Wproj'], 'L0_ffn_enc_w': _L0_ffn_in['enc_w'], 'L0_ffn_enc_b': _L0_ffn_in['enc_b'], 'L0_ffn_sw_w': _L0_ffn_in['sw_w'], 'L0_ffn_sw_b': _L0_ffn_in['sw_b'], 'L0_ffn_w1': _L0_ffn_in['w1'], 'L0_ffn_b1': _L0_ffn_in['b1'], 'L0_ffn_w2': _L0_ffn_in['w2'], 'L0_ffn_b2': _L0_ffn_in['b2'], 'L1_attn_wq': _L1_attn_in['wq'], 'L1_attn_wv': _L1_attn_in['wv'], 'L1_attn_wo': _L1_attn_in['wo'], 'L1_attn_wg': _L1_attn_in['wg'], 'L1_attn_conv_q_w': _L1_attn_in['conv_q_w'], 'L1_attn_conv_q_b': _L1_attn_in['conv_q_b'], 'L1_attn_conv_k_w': _L1_attn_in['conv_k_w'], 'L1_attn_conv_k_b': _L1_attn_in['conv_k_b'], 'L1_attn_lr_w': _L1_attn_in['lr_w'], 'L1_attn_lr_b': _L1_attn_in['lr_b'], 'L1_attn_learnable_token_idx': _L1_attn_in['learnable_token_idx'], 'L1_attn_ttt_norm_scale': _L1_attn_in['ttt_norm_scale'], 'L1_attn_ttt_norm_bias': _L1_attn_in['ttt_norm_bias'], 'L1_attn_post_norm_scale': _L1_attn_in['post_norm_scale'], 'L1_attn_post_norm_bias': _L1_attn_in['post_norm_bias'], 'L1_attn_W1': _L1_attn_in['W1'], 'L1_attn_b1': _L1_attn_in['b1'], 'L1_ffn_phi': _L1_ffn_in['phi'], 'L1_ffn_scale': _L1_ffn_in['scale'], 'L1_ffn_w1': _L1_ffn_in['w1'], 'L1_ffn_b1': _L1_ffn_in['b1'], 'L1_ffn_w2': _L1_ffn_in['w2'], 'L1_ffn_b2': _L1_ffn_in['b2']}

def reference(x, L0_tok_tune_ids, L0_tok_base_weight, L0_tok_train_weight, L0_attn_Wq, L0_attn_Wkv, L0_attn_Wproj, L0_ffn_enc_w, L0_ffn_enc_b, L0_ffn_sw_w, L0_ffn_sw_b, L0_ffn_w1, L0_ffn_b1, L0_ffn_w2, L0_ffn_b2, L1_attn_wq, L1_attn_wv, L1_attn_wo, L1_attn_wg, L1_attn_conv_q_w, L1_attn_conv_q_b, L1_attn_conv_k_w, L1_attn_conv_k_b, L1_attn_lr_w, L1_attn_lr_b, L1_attn_learnable_token_idx, L1_attn_ttt_norm_scale, L1_attn_ttt_norm_bias, L1_attn_post_norm_scale, L1_attn_post_norm_bias, L1_attn_W1, L1_attn_b1, L1_ffn_phi, L1_ffn_scale, L1_ffn_w1, L1_ffn_b1, L1_ffn_w2, L1_ffn_b2):
    import jax
    import jax.numpy as jnp

    def _L0_tok_ref(input_ids, tune_ids, base_weight, train_weight):
        import jax, jax.numpy as jnp
        import numpy as np
        VOCAB = 50257
        EMBED_DIM = 192
        NUM_TUNE = 256
        id2row = jnp.full((VOCAB,), -1, dtype=jnp.int32)
        id2row = id2row.at[tune_ids].set(jnp.arange(NUM_TUNE, dtype=jnp.int32))
        out = base_weight[input_ids]
        rows = id2row[input_ids]
        mask = rows >= 0
        override = train_weight[jnp.maximum(rows, 0)]
        return jnp.where(mask[..., None], override, out)

    def _L0_attn_ref(x, Wq, Wkv, Wproj):
        import jax, jax.numpy as jnp
        import numpy as np
        DIM = 192
        NUM_HEADS = 12
        HEAD_DIM = DIM // NUM_HEADS
        SCALE = HEAD_DIM ** (-0.5)
        B, N = (4, 512)
        b, n, c = x.shape
        h, d = (NUM_HEADS, HEAD_DIM)
        q = (x @ Wq.T).reshape(b, n, h, d)
        kv = (x @ Wkv.T).reshape(b, n, h, 2 * d)
        k, v = (kv[..., :d], kv[..., d:])
        attn = jnp.einsum('bnhd,bmhd->bhnm', q, k) * SCALE
        neg_inf = jnp.finfo(attn.dtype).min
        attn = attn.at[..., 1:, 0].set(neg_inf)
        attn = jax.nn.softmax(attn, axis=-1)
        out = jnp.einsum('bhnm,bmhd->bnhd', attn, v).reshape(b, n, c)
        out = out @ Wproj.T
        return out

    def _L0_ffn_ref(x, enc_w, enc_b, sw_w, sw_b, w1, b1, w2, b2):
        import jax, jax.numpy as jnp
        import numpy as np
        H = 192
        R = 64
        E = 8
        B, S = (8, 512)
        b, s, d = x.shape
        xt = x.reshape(-1, d)
        x_enc = xt @ enc_w + enc_b
        route_prob = jax.nn.softmax(x_enc @ sw_w + sw_b, axis=-1)
        route_prob_max = jnp.max(route_prob, axis=-1)
        routes = jnp.argmax(route_prob, axis=-1)
        onehot = jax.nn.one_hot(routes, E, dtype=xt.dtype)
        h = jnp.einsum('td,edr->ter', xt, w1) + b1[None]
        h = jax.nn.gelu(h, approximate=False)
        h = h * onehot[..., None]
        out = jnp.einsum('ter,erd->td', h, w2) + onehot @ b2
        out = out * route_prob_max[:, None]
        return out.reshape(b, s, d)

    def _L1_attn_ref(x, wq, wv, wo, wg, conv_q_w, conv_q_b, conv_k_w, conv_k_b, lr_w, lr_b, learnable_token_idx, ttt_norm_scale, ttt_norm_bias, post_norm_scale, post_norm_bias, W1, b1):
        import jax, jax.numpy as jnp
        import numpy as np
        B, S, HID = (4, 2048, 192)
        H, D, K = (12, 64, 16)
        KW = 4
        TTT_BASE_LR = 1.0
        ROPE_THETA = 10000.0
        ETA_DECAY_RATE = 0.0
        LN_EPS = 1e-05

        def causal_dwconv(x, w, b):
            S_ = x.shape[1]
            xp = jnp.pad(x, ((0, 0), (KW, 0), (0, 0)))
            out = b
            for k in range(KW):
                out = out + w[k] * xp[:, k:k + S_]
            return out

        def rope(x, cos, sin):
            xr = x.reshape(*x.shape[:-1], D // 2, 2)
            x1, x2 = (xr[..., 0], xr[..., 1])
            c = cos[None, :, None, :]
            s = sin[None, :, None, :]
            return jnp.stack([x1 * c - x2 * s, x1 * s + x2 * c], axis=-1).reshape(x.shape)

        def ln_fwd(x, g, b):
            mu = x.mean(-1, keepdims=True)
            var = x.var(-1, keepdims=True)
            return (x - mu) * jax.lax.rsqrt(var + LN_EPS) * g + b

        def ln_l2_bwd(x, target, g, b):
            mu = x.mean(-1, keepdims=True)
            var = x.var(-1, keepdims=True)
            std = jnp.sqrt(var + LN_EPS)
            xh = (x - mu) / std
            gx = (xh * g + b - target) * g
            return (gx - gx.mean(-1, keepdims=True) - xh * (gx * xh).mean(-1, keepdims=True)) / std

        def ttt_forward(x, wq, wv, wo, wg, conv_q_w, conv_q_b, conv_k_w, conv_k_b, lr_w, lr_b, learnable_token_idx, ttt_norm_scale, ttt_norm_bias, post_norm_scale, post_norm_bias, W1, b1):
            Bx, Sx, _ = x.shape
            n_mb = Sx // K
            xqk = x @ wq
            XQ = causal_dwconv(xqk, conv_q_w, conv_q_b).reshape(Bx, Sx, H, D)
            XK = causal_dwconv(xqk, conv_k_w, conv_k_b).reshape(Bx, Sx, H, D)
            XV = (x @ wv).reshape(Bx, Sx, H, D)
            inv_freq = 1.0 / ROPE_THETA ** (jnp.arange(0, D, 2, dtype=jnp.float32) / D)
            freqs = jnp.arange(Sx, dtype=jnp.float32)[:, None] * inv_freq[None, :]
            cos, sin = (jnp.cos(freqs), jnp.sin(freqs))
            XQ = rope(XQ, cos, sin)
            XK = rope(XK, cos, sin)
            token_idx = jnp.maximum(1.0 / jnp.arange(1, K + 1, dtype=jnp.float32) + learnable_token_idx, 0.0)
            ttt_lr = jax.nn.sigmoid(jnp.einsum('bsd,hd->bhs', x, lr_w) + lr_b[None, :, None])
            ttt_lr_eta = TTT_BASE_LR / D * ttt_lr
            decay = jnp.exp(ETA_DECAY_RATE * (jnp.arange(K, dtype=jnp.float32) - (K - 1)))
            eta = token_idx[None, None, None, :, None] * (ttt_lr_eta.reshape(Bx, H, n_mb, 1, K) * decay)
            to_mb = lambda t: t.reshape(Bx, n_mb, K, H, D).transpose(1, 0, 3, 2, 4)
            xs = (to_mb(XQ), to_mb(XK), to_mb(XV), eta.transpose(2, 0, 1, 3, 4))
            W1_0 = jnp.broadcast_to(W1[None], (Bx, H, D, D)) + 0.0
            b1_0 = jnp.broadcast_to(b1[None], (Bx, H, 1, D)) + 0.0
            tril = jnp.tril(jnp.ones((K, K), jnp.float32))

            def step(carry, inp):
                W1c, b1c = carry
                q, k, v, e = inp
                Z1 = jnp.einsum('bhkd,bhde->bhke', k, W1c) + b1c
                grad = ln_l2_bwd(Z1, v - k, ttt_norm_scale, ttt_norm_bias)
                Attn = jnp.einsum('bhid,bhjd->bhij', q, k) * tril
                b1_bar = b1c - jnp.einsum('bhij,bhjd->bhid', e * tril, grad)
                Z1_bar = jnp.einsum('bhkd,bhde->bhke', q, W1c) - jnp.einsum('bhij,bhjd->bhid', e * Attn, grad) + b1_bar
                last_e = e[..., -1, :, None]
                W1n = W1c - jnp.einsum('bhkd,bhke->bhde', last_e * k, grad)
                b1n = b1c - jnp.sum(last_e * grad, axis=-2, keepdims=True)
                out = q + ln_fwd(Z1_bar, ttt_norm_scale, ttt_norm_bias)
                return ((W1n, b1n), out)
            _, Z = jax.lax.scan(step, (W1_0, b1_0), xs)
            Z = Z.transpose(1, 0, 3, 2, 4).reshape(Bx, Sx, H * D)
            mu = Z.mean(-1, keepdims=True)
            var = Z.var(-1, keepdims=True)
            Zn = (Z - mu) * jax.lax.rsqrt(var + LN_EPS) * post_norm_scale + post_norm_bias
            gate = jax.nn.gelu(x @ wg)
            return Zn * gate @ wo
        return ttt_forward(x, wq, wv, wo, wg, conv_q_w, conv_q_b, conv_k_w, conv_k_b, lr_w, lr_b, learnable_token_idx, ttt_norm_scale, ttt_norm_bias, post_norm_scale, post_norm_bias, W1, b1)

    def _L1_ffn_ref(x, phi, scale, w1, b1, w2, b2):
        import jax, jax.numpy as jnp
        import numpy as np
        B, L, D = (4, 256, 192)
        E, S, H = (32, 32, 768)
        EPS = 1e-12

        def _l2norm(v, axis):
            n = jnp.sqrt(jnp.sum(v * v, axis=axis, keepdims=True))
            return v / jnp.maximum(n, EPS)
        b, l, d = x.shape
        xn = _l2norm(x, axis=2)
        phin = scale * _l2norm(phi, axis=0)
        logits = jnp.einsum('bld,des->bles', xn, phin)
        d_w = jax.nn.softmax(logits, axis=-1)
        c_w = jax.nn.softmax(logits.reshape(b, l, E * S), axis=-1)
        slots = jnp.einsum('bld,bles->besd', xn, d_w)
        h = jax.nn.gelu(jnp.einsum('besd,edh->besh', slots, w1) + b1[:, None, :], approximate=False)
        eo = jnp.einsum('besh,ehd->besd', h, w2) + b2[:, None, :]
        eo = eo.reshape(b, E * S, d)
        return jnp.einsum('bkd,blk->bld', eo, c_w)
    h = _L0_tok_ref(x, L0_tok_tune_ids, L0_tok_base_weight, L0_tok_train_weight)
    h = h + _L0_attn_ref(_layernorm(h, axis=-1), L0_attn_Wq, L0_attn_Wkv, L0_attn_Wproj)
    h = h + _L0_ffn_ref(_layernorm(h, axis=-1), L0_ffn_enc_w, L0_ffn_enc_b, L0_ffn_sw_w, L0_ffn_sw_b, L0_ffn_w1, L0_ffn_b1, L0_ffn_w2, L0_ffn_b2)
    h = h + _L1_attn_ref(_layernorm(h, axis=-1), L1_attn_wq, L1_attn_wv, L1_attn_wo, L1_attn_wg, L1_attn_conv_q_w, L1_attn_conv_q_b, L1_attn_conv_k_w, L1_attn_conv_k_b, L1_attn_lr_w, L1_attn_lr_b, L1_attn_learnable_token_idx, L1_attn_ttt_norm_scale, L1_attn_ttt_norm_bias, L1_attn_post_norm_scale, L1_attn_post_norm_bias, L1_attn_W1, L1_attn_b1)
    h = h + _L1_ffn_ref(_layernorm(h, axis=-1), L1_ffn_phi, L1_ffn_scale, L1_ffn_w1, L1_ffn_b1, L1_ffn_w2, L1_ffn_b2)
    return h

_drawn_inputs = setup_inputs


def setup_inputs(seed=0):
    import zlib

    import numpy as np

    out = dict(_drawn_inputs(seed))
    spreads = {'L1_attn_conv_q_b': (0.0, 0.1),
     'L1_attn_conv_k_b': (0.0, 0.1),
     'L1_attn_lr_b': (0.0, 0.682),
     'L1_attn_learnable_token_idx': (0.0, 0.1),
     'L1_attn_ttt_norm_scale': (1.0, 0.2),
     'L1_attn_ttt_norm_bias': (0.0, 0.1),
     'L1_attn_post_norm_scale': (1.0, 0.2),
     'L1_attn_post_norm_bias': (0.0, 0.1),
     'L1_attn_b1': (0.0, 0.1)}
    factors = {'L0_ffn_enc_b': 7.083,
     'L0_ffn_b1': 8.0,
     'L0_ffn_b2': 3.646,
     'L1_ffn_phi': 64.0,
     'L1_ffn_w1': 3.526,
     'L1_ffn_b1': 8.0,
     'L1_ffn_w2': 3.167,
     'L1_ffn_b2': 40.238}
    for name, (base, spread) in spreads.items():
        noise = np.random.default_rng([zlib.crc32(name.encode()), seed]).standard_normal(out[name].shape)
        drawn = base * np.exp(spread * noise) if base else spread * noise
        out[name] = jnp.asarray(drawn.astype(out[name].dtype))
    for name, factor in factors.items():
        out[name] = (out[name] * factor).astype(out[name].dtype)
    return out
```

```python
from contextlib import ExitStack

import numpy as np

import concourse.bass as bass
from concourse import mybir

F32 = mybir.dt.float32
BF16 = mybir.dt.bfloat16
I32 = mybir.dt.int32
U32 = mybir.dt.uint32
ALU = mybir.AluOpType
ACT = mybir.ActivationFunctionType
AX = mybir.AxisListType

P = 128
B, N, D = 4, 512, 192
TILES = B * N // P
TB = N // P
KC, DC = 2, 96
LN_EPS = 1e-5

HA, DH = 12, 16
VP = 32
QUADS = HA // 4
SPLIT = 3
PAIRS = [(0, 0), (0, 1), (1, 0), (0, 2), (2, 0), (1, 1)]
MASK_ROW = len(PAIRS) * DH
MAX_ROW = MASK_ROW + 1
NEG = -3.0e38


class Steps:

    def __init__(self, sem, names):
        self.sem, self.names, self.k, self.pos = sem, list(names), len(names), 0
        assert len(set(self.names)) == self.k

    def open(self, eng):
        eng.sem_inc(self.sem, self.k)

    def did(self, name):
        assert self.names[self.pos % self.k] == name, (name, self.names[self.pos % self.k])
        self.pos += 1
        return self.sem, 1

    def at(self, name, turn=0, back=0):
        return self.sem, turn * self.k + (self.k * (1 - back) + self.names.index(name) + 1)


def row(ap, i):
    return ap[:, bass.ds(i, 1), :].rearrange("p a n -> p (a n)")


def rows(ap, i, n):
    return ap[:, bass.ds(i, n), :]


def embed(nc, M, ins):
    NT = ins["tune_ids"].shape[0]
    with ExitStack() as ctx:
        sb = lambda n, s, d=F32: ctx.enter_context(nc.sbuf_tensor(n, s, d))
        sem = lambda n: ctx.enter_context(nc.semaphore(n))
        ids16, ids16f = sb("ids16", [TILES, P], I32), sb("ids16f", [TILES, P])
        tune_i, tune_f = sb("tune_i", [P, NT], I32), sb("tune_f", [P, NT])
        rank_i, rank_f = sb("rank_i", [P, NT], I32), sb("rank_f", [P, NT])
        ids_f, ids_u = sb("ids_f", [P, TILES]), sb("ids_u", [P, TILES], U32)
        hit = sb("hit", [P, TILES, NT])
        best, none = sb("best", [P, TILES]), sb("none", [P, TILES])
        tuned_u = sb("tuned_u", [P, TILES], U32)
        h, ident, psT = M["h"], M["ident"], M["ps"][0]
        loaded, consts, gathered, laid = sem("e_loaded"), sem("e_consts"), sem("e_gathered"), sem("e_laid")
        dve = Steps(sem("e_dve"), ["idsf", "ids", "tune", "rank", "hits", "best", "none", "tuned"])
        turned, ranked = sem("e_turned"), sem("e_ranked")

        with nc.Block() as block:
            @block.sync
            def _(sp):
                sp.dma_start(ids16[:, :], ins["x"].rearrange("b (t p) -> (b t) p", p=P)).then_inc(loaded, 16)
                sp.dma_start(tune_i[:, :], ins["tune_ids"].rearrange("(a n) -> a n", a=1).to_broadcast([P, NT]))\
                    .then_inc(loaded, 16)
                sp.dma_start(M["ident"][:, :], ins["c_ident"]).then_inc(consts, 16)
                sp.dma_start(M["pair"][:, :], ins["c_pair"]).then_inc(consts, 16)
                sp.dma_start(M["blk"][:, :], ins["c_blk"]).then_inc(consts, 16)
                sp.wait_ge(consts, 48)

            @block.tensor
            def _(pe):
                pe.wait_ge(consts, 48)
                pe.wait_ge(*dve.at("idsf"))
                pe.transpose(psT[:, 0:TILES], ids16f[:, :], ident[0:TILES, 0:TILES]).then_inc(turned, 1)

            @block.vector
            def _(v):
                dve.open(v)
                v.wait_ge(loaded, 32)
                v.tensor_copy(ids16f[:, :], ids16[:, :]).then_inc(*dve.did("idsf"))
                v.wait_ge(turned, 1)
                v.tensor_copy(ids_f[:, :], psT[:, 0:TILES])
                v.tensor_copy(ids_u[:, :], psT[:, 0:TILES]).then_inc(*dve.did("ids"))
                v.tensor_copy(tune_f[:, :], tune_i[:, :]).then_inc(*dve.did("tune"))
                v.wait_ge(ranked, 1)
                v.tensor_copy(rank_f[:, :], rank_i[:, :]).then_inc(*dve.did("rank"))
                v.wait_ge(*dve.at("rank"))
                for t in range(TILES):
                    last = v.scalar_tensor_tensor(hit[:, t, :], tune_f[:, :], ids_f[:, t:t + 1], rank_f[:, :],
                                                  ALU.is_equal, ALU.mult)
                last.then_inc(*dve.did("hits"))
                v.wait_ge(*dve.at("hits"))
                v.tensor_reduce(best[:, :], hit[:, :, :], AX.X, ALU.max).then_inc(*dve.did("best"))
                v.wait_ge(*dve.at("best"))
                v.tensor_scalar(none[:, :], best[:, :], 0.0, 70000.0, ALU.is_equal, ALU.mult)\
                    .then_inc(*dve.did("none"))
                v.wait_ge(*dve.at("none"))
                v.scalar_tensor_tensor(tuned_u[:, :], best[:, :], 1.0, none[:, :], ALU.subtract, ALU.add,)\
                    .then_inc(*dve.did("tuned"))

            @block.gpsimd
            def _(g):
                g.iota(rank_i[:, :], pattern=[[1, NT]], base=1, channel_multiplier=0).then_inc(ranked, 1)
                g.wait_ge(*dve.at("ids"))
                for t in range(TILES):
                    g.indirect_dma_start(out=h[:, t, :], out_offset=None, in_=ins["base_weight"],
                                         in_offset=bass.IndirectOffsetOnAxis(ap=ids_u[:, t:t + 1], axis=0))\
                        .then_inc(gathered, 16)
                g.wait_ge(gathered, 16 * TILES)
                g.wait_ge(*dve.at("tuned"))
                for t in range(TILES):
                    g.indirect_dma_start(out=h[:, t, :], out_offset=None, in_=ins["train_weight"],
                                         in_offset=bass.IndirectOffsetOnAxis(ap=tuned_u[:, t:t + 1], axis=0),
                                         bounds_check=NT - 1, oob_is_err=False).then_inc(laid, 16)
                g.wait_ge(laid, 16 * TILES)


LN_DVE = ["stats", "aggr", "rstd", "xn0", "xn1", "xn2", "xn3"]


def ln_buffers(sb, pre=""):
    return {"stats": sb(pre + "ln_stats", [P, TB, 6]), "mv": sb(pre + "ln_mv", [P, TB, 2]), "std": sb(pre + "ln_std", [P, TB]),
            "rstd": sb(pre + "ln_rstd", [P, TB]), "xn": sb(pre + "ln_xn", [P, TB, D]), "eps": sb(pre + "ln_eps", [P, 1]),
            "gate": sb(pre + "ln_gate", [P, 1])}


def ln_dve(v, L, h, b, dve, act, pe):
    v.wait_ge(*dve.at("xn3", b, 1))
    for t in range(TB):
        last = v.bn_stats(L["stats"][:, t, :], row(h, b * TB + t))
    last.then_inc(*dve.did("stats"))
    v.wait_ge(*dve.at("stats", b))
    v.memset(L["gate"][:, :], 0.0)
    for t in range(TB):
        last = v.bn_aggr(L["mv"][:, t, :], L["stats"][:, t, :])
    last.then_inc(*dve.did("aggr"))
    v.wait_ge(*act.at("std", b))
    v.reciprocal(L["rstd"][:, :], L["std"][:, :]).then_inc(*dve.did("rstd"))
    v.wait_ge(*dve.at("rstd", b))
    v.wait_ge(*pe.at("T1", b, 1))
    for t in range(TB):
        v.tensor_scalar(L["xn"][:, t, :], row(h, b * TB + t), L["mv"][:, t, 0:1], L["rstd"][:, t:t + 1],
                        ALU.subtract, ALU.mult).then_inc(*dve.did(f"xn{t}"))


def ln_std(a, L, b, dve, act):
    a.wait_ge(*dve.at("aggr", b))
    a.activation(L["std"][:, :], L["mv"][:, :, 1], ACT.Sqrt, bias=L["eps"][:, 0:1]).then_inc(*act.did("std"))


def ln_turn(t_, L, ident, banks, b, dve, act, pe):
    for c in range(KC):
        t_.wait_ge(*act.at(f"xT{c}", b, 1))
        for t in range(TB):
            if c == 0:
                t_.wait_ge(*dve.at(f"xn{t}", b))
            last = t_.transpose(banks[c][0:DC, t * P:(t + 1) * P], L["xn"][:, t, c * DC:(c + 1) * DC], ident[:, :])
        last.then_inc(*pe.did(f"T{c}"))


def qkv(nc, M, ins):
    with ExitStack() as ctx:
        sb = lambda n, s, d=F32: ctx.enter_context(nc.sbuf_tensor(n, s, d))
        sem = lambda n: ctx.enter_context(nc.semaphore(n))
        L = ln_buffers(sb, "a_")
        w = [sb("wq_a", [DC, KC, D]), sb("wk_a", [DC, KC, D]), sb("wv_a", [DC, KC, D])]
        xT = sb("a_xT", [DC, KC, N])
        parts = sb("qk_parts", [DC, 2, KC, SPLIT, N], BF16)
        rest = sb("qk_rest", [DC, 2, KC, N])
        h, ident, ps, V1 = M["h"], M["ident"], M["ps"], M["V1"]
        loaded, ones, stored = sem("a_loaded"), sem("a_ones"), sem("a_stored")
        WC = [(w_, c) for w_ in range(2) for c in range(KC)]
        dve = Steps(sem("a_dve"), LN_DVE + [f"rest{w_}{c}" for w_, c in WC])
        pe = Steps(sem("a_pe"), ["T0", "T1"] + [f"qk{w_}{c}" for w_, c in WC] + ["v0", "v1"])
        act = Steps(sem("a_act"), ["std", "xT0", "xT1"] + [f"hi{w_}{c}" for w_, c in WC] + ["v0", "v1"]
                    + [f"mid{w_}{c}" for w_, c in WC])
        pool = Steps(sem("a_pool"), [f"lo{w_}{c}" for w_, c in WC])
        qk_d = M["qk_d"]
        PER = 16 * 8

        with nc.Block() as block:
            @block.sync
            def _(sp):
                sp.sem_inc(stored, 1)
                for t, name in zip(w, ("WqT", "WkT", "WvT")):
                    sp.dma_start(t[:, :, :], ins[name].rearrange("(k p) n -> p k n", p=DC)).then_inc(loaded, 16)
                with sp.Fori(0, B) as b:
                    for w_, c in WC:
                        sp.wait_ge(*pool.at(f"lo{w_}{c}", b))
                        for r0, r1, q, d0 in ([(0, 64, 0, 0), (64, 96, 1, 0)], [(0, 32, 1, 32), (32, 96, 2, 0)])[c]:
                            sp.dma_start(
                                qk_d[bass.ds(b, 1), q, w_, :, d0:d0 + r1 - r0, :].rearrange("a s r n -> r (a s) n"),
                                parts[r0:r1, w_, c, :, :]).then_inc(stored, 16)
                sp.wait_ge(stored, PER * B + 1)

            @block.tensor
            def _(t_):
                pe.open(t_)
                t_.wait_ge(loaded, 48)
                with t_.Fori(0, B) as b:
                    ln_turn(t_, L, ident, ps[0:2], b, dve, act, pe)
                    t_.wait_ge(*act.at("xT1", b))
                    for w_, c in WC:
                        bank = ps[2 + 2 * w_ + c]
                        t_.wait_ge(*dve.at(f"rest{w_}{c}", b, 1))
                        for kc in range(KC):
                            last = t_.matmul(bank[0:DC, :], w[w_][:, kc, c * DC:(c + 1) * DC], xT[:, kc, :],
                                             start=(kc == 0), stop=(kc == KC - 1))
                        last.then_inc(*pe.did(f"qk{w_}{c}"))
                    for t in range(TB):
                        if t % 2 == 0:
                            t_.wait_ge(*act.at(f"v{t // 2}", b, 1))
                        for kc in range(KC):
                            last = t_.matmul(ps[6 + t // 2][:, (t % 2) * D:(t % 2 + 1) * D], xT[:, kc, t * P:(t + 1) * P],
                                             w[2][:, kc, :], start=(kc == 0), stop=(kc == KC - 1))
                        if t % 2:
                            last.then_inc(*pe.did(f"v{t // 2}"))

            @block.vector
            def _(v):
                dve.open(v)
                v.memset(L["eps"][:, :], LN_EPS)
                with v.Fori(0, B) as b:
                    ln_dve(v, L, h, b, dve, act, pe)
                    for w_, c in WC:
                        v.wait_ge(*act.at(f"hi{w_}{c}", b))
                        v.wait_ge(*pool.at(f"lo{w_}{c}", b, 1))
                        v.tensor_tensor(rest[:, w_, c, :], ps[2 + 2 * w_ + c][0:DC, :], parts[:, w_, c, 0, :],
                                        ALU.subtract).then_inc(*dve.did(f"rest{w_}{c}"))

            @block.scalar
            def _(a):
                act.open(a)
                with a.Fori(0, B) as b:
                    ln_std(a, L, b, dve, act)
                    for c in range(KC):
                        a.wait_ge(*pe.at(f"T{c}", b))
                        a.wait_ge(*pe.at("v1", b, 1))
                        a.activation(xT[:, c, :], ps[c][0:DC, :], ACT.Copy).then_inc(*act.did(f"xT{c}"))
                    for w_, c in WC:
                        a.wait_ge(*pe.at(f"qk{w_}{c}", b))
                        a.wait_ge(stored, b * PER + 1)
                        a.activation(parts[:, w_, c, 0, :], ps[2 + 2 * w_ + c][0:DC, :], ACT.Copy)\
                            .then_inc(*act.did(f"hi{w_}{c}"))
                    for j in range(2):
                        a.wait_ge(*pe.at(f"v{j}", b))
                        a.wait_ge(ones, 2)
                        a.activation(V1[:, bass.ds(b * TB + 2 * j, 2), :, 0:DH],
                                     ps[6 + j][:, 0:2 * D].rearrange("p (t h d) -> p t h d", t=2, h=HA), ACT.Copy)\
                            .then_inc(*act.did(f"v{j}"))
                    for w_, c in WC:
                        a.wait_ge(*dve.at(f"rest{w_}{c}", b))
                        a.activation(parts[:, w_, c, 1, :], rest[:, w_, c, :], ACT.Copy).then_inc(*act.did(f"mid{w_}{c}"))

            @block.gpsimd
            def _(g):
                pool.open(g)
                g.memset(V1[:, :, :, DH:DH + 1], 1.0).then_inc(ones, 1)
                g.memset(V1[:, :, :, DH + 1:VP], 0.0).then_inc(ones, 1)
                with g.Fori(0, B) as b:
                    for w_, c in WC:
                        g.wait_ge(*act.at(f"mid{w_}{c}", b))
                        g.tensor_tensor(parts[:, w_, c, 2, :], rest[:, w_, c, :], parts[:, w_, c, 1, :], ALU.subtract)\
                            .then_inc(*pool.did(f"lo{w_}{c}"))


def attention(nc, M, ins):
    with ExitStack() as ctx:
        sb = lambda n, s, d=F32: ctx.enter_context(nc.sbuf_tensor(n, s, d))
        sem = lambda n: ctx.enter_context(nc.semaphore(n))
        RA, RB = MASK_ROW + 1, MAX_ROW + 2
        Q = [sb(f"Q{r}", [RB, 4, N], BF16) for r in range(QUADS)]
        K = [sb(f"K{r}", [RB, 4, N], BF16) for r in range(QUADS)]
        PT = [sb(f"PT{r}", [P, 2, N]) for r in range(2)]
        mx = sb("mx", [P, 4, TB])
        mparts, mrest = sb("mparts", [16, 2, P], BF16), sb("mrest", [16, P])
        rec, AO = sb("rec", [P, TB, 4]), sb("AO", [P, TB, D])
        AOT = sb("AOT", [DC, KC, N])
        OT = sb("OT", [P, N])
        Vb = sb("Vb", [P, TB, HA * VP])
        wp = sb("wp", [DC, KC, D])
        h, ident, V1, qk_d = M["h"], M["ident"], M["V1"], M["qk_d"]
        ps = M["ps"]
        AB, STB = M["ps2"][0], [M["ps2"][1], M["ps2"][2]]
        OB, XB = ps[6], ps[7]
        O = XB.rearrange("p (t h e) -> p t h e", t=TB, h=4)
        WHEN = {0: [0, 1], 1: [2], 2: [3, 4], 3: [5], 4: [6, 7]}
        loaded = [sem(f"t_loaded{r}") for r in range(QUADS)]
        consts, rowed = sem("t_consts"), sem("t_rowed")
        UQ = range(QUADS)
        MXS = [f"max{j}" for j in range(8)]
        dve = Steps(sem("t_dve"), [f"{s}/{q}" for q in UQ for s in MXS + ["m0", "m0r", "m1", "rec", "AO"]]
                    + ["res0", "res1", "Vb"])
        act = Steps(sem("t_act"), [f"exp{s}/{q}" for q in UQ for s in list(range(8)) + ["O"]] + ["AOT0", "AOT1"])
        pe = Steps(sem("t_pe"), [x for q in UQ for x in
                                 [y for s in range(8) for y in [f"ST{s}/{q}"] + [f"A{j}/{q}" for j in WHEN.get(s, [])]
                                  + ([f"mxT/{q}"] if s == 5 else []) + ([f"PV{s - 1}/{q}"] if s else [])]
                                 + [f"PV7/{q}", f"Oq/{q}"]] + ["OT0", "OT1", "proj0", "proj1"])
        first_pe, first_dve = sem("t_first_pe"), sem("t_first_dve")
        masks, laid = sem("t_masks"), sem("t_laid")
        NL = 12

        def load(sp, r, b, q):
            for g, pq in enumerate(PAIRS):
                for w_, dst in ((0, Q[r]), (1, K[r])):
                    sp.dma_start(dst[g * DH:(g + 1) * DH, :, :],
                                 qk_d[bass.ds(b, 1), q, w_, pq[w_], :, :].rearrange("a (h d) n -> (a d) h n", d=DH))\
                        .then_inc(loaded[r], 16)

        def max_scores(t_, r, j):
            hd, qt = j // 2, 2 * (j % 2)
            for i in range(2):
                last = t_.matmul(AB[:, i, :], Q[r][0:RA, hd, (qt + i) * P:(qt + i + 1) * P], K[r][0:RA, hd, :],
                                 start=True, stop=True)
            return last

        def take_max(v, j):
            hd, qt = j // 2, 2 * (j % 2)
            return v.tensor_reduce(mx[:, hd, qt:qt + 2], AB[:, :, :], AX.X, ALU.max)

        MXT = AB[0:16, 0, 0:P]

        def neg_max(v, wait, done):
            v.tensor_scalar(mparts[:, 0, :], MXT, -1.0, None, ALU.mult).then_inc(*done("m0"))
            wait("m0")
            v.scalar_tensor_tensor(mrest[:, :], MXT, -1.0, mparts[:, 0, :], ALU.mult, ALU.subtract)\
                .then_inc(*done("m0r"))
            wait("m0r")
            v.tensor_copy(mparts[:, 1, :], mrest[:, :]).then_inc(*done("m1"))

        def store_rows(sp, r):
            for j in range(2):
                sp.dma_start(Q[r][MAX_ROW + j:MAX_ROW + j + 1, :, :].rearrange("a h (t n) -> a (h t) n", t=TB),
                             mparts[:, j, :]).then_inc(rowed, 16)

        with nc.Block() as block:
            @block.sync
            def _(sp):
                sp.dma_start(wp[:, :, :], ins["WprojT"].rearrange("(k p) n -> p k n", p=DC)).then_inc(consts, 16)
                for r in UQ:
                    load(sp, r, 0, r)
                sp.wait_ge(first_dve, 11)
                store_rows(sp, 0)
                with sp.Fori(0, B) as b:
                    for q in UQ:
                        sp.wait_ge(*dve.at(f"m1/{q}", b))
                        store_rows(sp, (q + 1) % 3)
                        sp.wait_ge(*pe.at(f"PV7/{q}", b))
                        load(sp, q, (b + 1) % B, q)
                for r in UQ:
                    sp.wait_ge(loaded[r], 16 * NL * (B + 1))
                sp.wait_ge(rowed, 32 * (QUADS * B + 1))

            @block.tensor
            def _(t_):
                pe.open(t_)
                t_.wait_ge(consts, 16)
                t_.wait_ge(masks, QUADS)
                t_.wait_ge(loaded[0], 16 * NL)
                for j in range(8):
                    if j:
                        t_.wait_ge(first_dve, j)
                    max_scores(t_, 0, j).then_inc(first_pe, 1)
                t_.wait_ge(first_dve, 8)
                t_.transpose(MXT, mx[:, :, :].rearrange("p h t -> p (h t)"), ident[:, :]).then_inc(first_pe, 1)
                with t_.Fori(0, B) as b:
                    for q in UQ:
                        nxt = (q + 1) % 3
                        t_.wait_ge(rowed, b * (32 * QUADS) + 32 * (q + 1))

                        def pv(s):
                            t_.wait_ge(*act.at(f"exp{s}/{q}", b))
                            for i in range(2):
                                hd, kt = s // 2, 2 * (s % 2) + i
                                last = t_.matmul(OB[hd * VP:(hd + 1) * VP, :], Vb[:, kt, (4 * q + hd) * VP:(4 * q + hd + 1) * VP],
                                                 PT[s % 2][:, i, :], start=(kt == 0), stop=(kt == TB - 1))
                            last.then_inc(*pe.did(f"PV{s}/{q}"))

                        for s in range(8):
                            hd, kt = s // 2, 2 * (s % 2)
                            if s >= 2:
                                t_.wait_ge(*act.at(f"exp{s - 2}/{q}", b))
                            elif q:
                                t_.wait_ge(*act.at(f"exp{6 + s}/{q - 1}", b))
                            else:
                                t_.wait_ge(*act.at(f"exp{6 + s}/2", b, 1))
                            for i in range(2):
                                last = t_.matmul(STB[s % 2][:, i, :], K[q][0:RB, hd, (kt + i) * P:(kt + i + 1) * P],
                                                 Q[q][0:RB, hd, :], start=True, stop=True)
                            last.then_inc(*pe.did(f"ST{s}/{q}"))
                            for j in WHEN.get(s, []):
                                if j:
                                    t_.wait_ge(*dve.at(f"max{j - 1}/{q}", b))
                                else:
                                    t_.wait_ge(*dve.at(f"m0r/{(q - 1) % 3}", b, 1 if q == 0 else 0))
                                    t_.wait_ge(loaded[nxt], b * (16 * NL) + 16 * NL * (2 if q == 2 else 1))
                                    if q == 0:
                                        t_.wait_ge(*act.at("AOT1", b, 1))
                                        t_.wait_ge(*dve.at("res1", b, 1))
                                max_scores(t_, nxt, j).then_inc(*pe.did(f"A{j}/{q}"))
                            if s == 5:
                                t_.wait_ge(*dve.at(f"max7/{q}", b))
                                t_.transpose(MXT, mx[:, :, :].rearrange("p h t -> p (h t)"), ident[:, :])\
                                    .then_inc(*pe.did(f"mxT/{q}"))
                            if s:
                                if s == 1 and q == 0:
                                    t_.wait_ge(first_dve, 12)
                                    t_.wait_ge(*dve.at("Vb", b, 1))
                                pv(s - 1)
                        pv(7)
                        t_.wait_ge(*act.at(f"expO/{q}", b))
                        t_.wait_ge(*dve.at("res1", b, 1) if q == 0 else dve.at(f"AO/{q - 1}", b))
                        for t in range(TB):
                            last = t_.transpose(XB[:, t * P:(t + 1) * P], OT[:, t * P:(t + 1) * P], ident[:, :])
                        last.then_inc(*pe.did(f"Oq/{q}"))
                    t_.wait_ge(*dve.at("AO/2", b))
                    for c in range(KC):
                        for t in range(TB):
                            last = t_.transpose(AB[0:DC, c, t * P:(t + 1) * P], AO[:, t, c * DC:(c + 1) * DC], ident[:, :])
                        last.then_inc(*pe.did(f"OT{c}"))
                    t_.wait_ge(*act.at("AOT1", b))
                    for t in range(TB):
                        bank = XB if t < 2 else AB[:, 0, :]
                        for kc in range(KC):
                            last = t_.matmul(bank[:, (t % 2) * D:(t % 2 + 1) * D], AOT[:, kc, t * P:(t + 1) * P],
                                             wp[:, kc, :], start=(kc == 0), stop=(kc == KC - 1))
                        if t % 2:
                            last.then_inc(*pe.did(f"proj{t // 2}"))

            @block.vector
            def _(v):
                dve.open(v)
                def stage_values(b):
                    return v.tensor_copy(Vb[:, :, :], V1[:, bass.ds(b * TB, TB), :, :].rearrange("p t h e -> p t (h e)"))

                for j in range(8):
                    v.wait_ge(first_pe, j + 1)
                    take_max(v, j).then_inc(first_dve, 1)
                v.wait_ge(first_pe, 9)
                neg_max(v, lambda n: v.wait_ge(first_dve, {"m0": 9, "m0r": 10}[n]), lambda n: (first_dve, 1))
                stage_values(0).then_inc(first_dve, 1)
                with v.Fori(0, B) as b:
                    for q in UQ:
                        for j in range(8):
                            if j == 0:
                                v.wait_ge(*pe.at(f"mxT/{(q - 1) % 3}", b, 1 if q == 0 else 0))
                            v.wait_ge(*pe.at(f"A{j}/{q}", b))
                            take_max(v, j).then_inc(*dve.did(f"max{j}/{q}"))
                        v.wait_ge(*pe.at(f"mxT/{q}", b))
                        v.wait_ge(rowed, b * (32 * QUADS) + 32 * (q + 1))
                        neg_max(v, lambda n: v.wait_ge(*dve.at(f"{n}/{q}", b)), lambda n: dve.did(f"{n}/{q}"))
                        v.wait_ge(*pe.at(f"Oq/{q}", b))
                        v.wait_ge(*dve.at(f"AO/{(q - 1) % 3}", b, 1 if q == 0 else 0))
                        v.reciprocal(rec[:, :, :], O[:, :, :, DH]).then_inc(*dve.did(f"rec/{q}"))
                        v.wait_ge(*dve.at(f"rec/{q}", b))
                        if q == 0:
                            v.wait_ge(*pe.at("OT1", b, 1))
                        v.tensor_tensor(AO[:, :, q * 64:(q + 1) * 64].rearrange("p t (h d) -> p t h d", d=DH),
                                        O[:, :, :, 0:DH], rec[:, :, :].unsqueeze(3).to_broadcast([P, TB, 4, DH]),
                                        ALU.mult).then_inc(*dve.did(f"AO/{q}"))
                    for j in range(2):
                        v.wait_ge(*pe.at(f"proj{j}", b))
                        bank = XB if j == 0 else AB[:, 0, :]
                        v.tensor_tensor(rows(h, b * TB + 2 * j, 2), rows(h, b * TB + 2 * j, 2),
                                        bank[:, 0:2 * D].rearrange("p (t n) -> p t n", t=2), ALU.add)\
                            .then_inc(*dve.did(f"res{j}"))
                    stage_values((b + 1) % B).then_inc(*dve.did("Vb"))

            @block.scalar
            def _(a):
                act.open(a)
                with a.Fori(0, B) as b:
                    for q in UQ:
                        for s in range(8):
                            a.wait_ge(*pe.at(f"ST{s}/{q}", b))
                            if s >= 2:
                                a.wait_ge(*pe.at(f"PV{s - 2}/{q}", b))
                            elif q:
                                a.wait_ge(*pe.at(f"PV{6 + s}/{q - 1}", b))
                            else:
                                a.wait_ge(*pe.at(f"PV{6 + s}/2", b, 1))
                            a.activation(PT[s % 2][:, :, :], STB[s % 2][:, :, :], ACT.Exp, scale=DH ** -0.5)\
                                .then_inc(*act.did(f"exp{s}/{q}"))
                        a.wait_ge(*pe.at(f"PV7/{q}", b))
                        a.wait_ge(*pe.at(f"Oq/{(q - 1) % 3}", b, 1 if q == 0 else 0))
                        a.activation(OT[:, :], OB, ACT.Copy).then_inc(*act.did(f"expO/{q}"))
                    for c in range(KC):
                        a.wait_ge(*pe.at(f"OT{c}", b))
                        a.wait_ge(*pe.at("proj1", b, 1))
                        a.activation(AOT[:, c, :], AB[0:DC, c, :], ACT.Copy).then_inc(*act.did(f"AOT{c}"))

            @block.gpsimd
            def _(g):
                for n, r in enumerate(UQ):
                    g.memset(Q[r][MASK_ROW:MASK_ROW + 1, :, :], NEG)
                    g.memset(K[r][MASK_ROW:RB, :, :], 1.0).then_inc(laid, 1)
                    g.wait_ge(laid, n + 1)
                    g.memset(Q[r][MASK_ROW:MASK_ROW + 1, :, 0:1], 0.0)
                    g.memset(K[r][MASK_ROW:MASK_ROW + 1, :, 1:N], 0.0).then_inc(masks, 1)


E0, R0 = 8, 64
CE = E0 * R0 // P


def switch_ffn(nc, M, ins):
    with ExitStack() as ctx:
        sb = lambda n, s, d=F32: ctx.enter_context(nc.sbuf_tensor(n, s, d))
        sem = lambda n: ctx.enter_context(nc.semaphore(n))
        L = ln_buffers(sb, "f_")
        xT = sb("f_xT", [DC, KC, N])
        enc_w, enc_b = sb("enc_w", [DC, KC, R0]), sb("enc_b", [R0, 1])
        sw = sb("sw", [R0 + 1, E0])
        w1, b1 = sb("f_w1", [DC, KC, E0 * R0]), sb("f_b1", [P, CE])
        w2, b2 = sb("f_w2", [P, CE, D]), sb("f_b2", [E0, D])
        spread, rank = sb("f_spread", [E0, CE, P]), sb("f_rank", [P, TB, E0])
        xe = sb("f_xe", [R0 + 1, N])
        top, lg, ex = sb("f_top", [P, TB]), sb("f_lg", [P, TB, E0]), sb("f_ex", [P, TB, E0])
        den, prob = sb("f_den", [P, TB]), sb("f_prob", [P, TB])
        ranked, first, hot = sb("f_ranked", [P, TB, E0]), sb("f_first", [P, TB]), sb("f_hot", [P, TB, E0])
        spreadb = sb("f_spreadb", [E0, CE, P], BF16)
        hotT, hotTb = sb("f_hotT", [E0, N]), sb("f_hotTb", [E0, N], BF16)
        act_h, hid = sb("f_act", [P, 2, N]), sb("f_hid", [P, CE, N])
        h, ident, ps = M["h"], M["ident"], M["ps"]
        loaded, cast = sem("f_loaded"), sem("f_cast")
        dve = Steps(sem("f_dve"), LN_DVE + ["top", "lg", "ranked", "first", "hot", "den", "prob"]
                    + [f"hid{c}" for c in range(CE)] + ["res0", "res1"])
        act = Steps(sem("f_act_s"), ["std", "xT0", "xT1", "xe", "ex", "hotT", "hotTb"] + [f"gelu{c}" for c in range(CE)])
        pe = Steps(sem("f_pe"), ["T0", "T1", "enc", "logits"] + ["hotT"]
                   + [f"{x}{c}" for c in range(CE) for x in ("mask", "h")] + ["y0", "y1"])
        lg_ps = ps[3][:, 0:TB * E0].rearrange("p (t e) -> p t e", t=TB)

        def bc(ap, n):
            return ap.unsqueeze(2).to_broadcast([P, ap.shape[1], n])

        with nc.Block() as block:
            @block.sync
            def _(sp):
                for dst, src in ((enc_w[:, :, :], ins["enc_w"].rearrange("(k p) n -> p k n", p=DC)),
                                 (enc_b[:, :], ins["enc_b"].rearrange("(p a) -> p a", a=1)),
                                 (sw[0:R0, :], ins["sw_w"]), (sw[R0:R0 + 1, :], ins["sw_b"].rearrange("(a e) -> a e", a=1)),
                                 (w1[:, :, :], ins["f_w1"].rearrange("(k p) n -> p k n", p=DC)),
                                 (b1[:, :], ins["f_b1"]), (w2[:, :, :], ins["f_w2"].rearrange("(c p) d -> p c d", p=P)),
                                 (b2[:, :], ins["f_b2"]), (spread[:, :, :], ins["c_spread"].rearrange("e (c p) -> e c p", p=P)),
                                 (rank[:, :, :], ins["c_rank8"].rearrange("p (t e) -> p t e", e=E0))):
                    sp.dma_start(dst, src).then_inc(loaded, 16)
                sp.wait_ge(loaded, 160)

            @block.tensor
            def _(t_):
                pe.open(t_)
                t_.wait_ge(loaded, 160)
                t_.wait_ge(cast, 1)
                with t_.Fori(0, B) as b:
                    t_.wait_ge(*dve.at("res1", b, 1))
                    ln_turn(t_, L, ident, ps[0:2], b, dve, act, pe)
                    t_.wait_ge(*act.at("xT1", b))
                    t_.wait_ge(*act.at("hotTb", b, 1))
                    for kc in range(KC):
                        last = t_.matmul(ps[2][0:R0, :], enc_w[:, kc, :], xT[:, kc, :], start=(kc == 0), stop=(kc == 1))
                    last.then_inc(*pe.did("enc"))
                    t_.wait_ge(*act.at("xe", b))
                    t_.wait_ge(*dve.at("lg", b, 1))
                    for t in range(TB):
                        last = t_.matmul(lg_ps[:, t, :], xe[:, t * P:(t + 1) * P], sw[:, :], start=True, stop=True)
                    last.then_inc(*pe.did("logits"))
                    t_.wait_ge(*dve.at("hot", b))
                    for t in range(TB):
                        last = t_.transpose(ps[2][0:E0, t * P:(t + 1) * P], hot[:, t, :], ident[:, :])
                    last.then_inc(*pe.did("hotT"))
                    t_.wait_ge(*act.at("hotTb", b))
                    for c in range(CE):
                        t_.wait_ge(*dve.at(f"hid{(c - 2) % CE}", b, 1 if c < 2 else 0))
                        t_.matmul(ps[6 + c % 2], spreadb[:, c, :], hotTb[:, :], start=True, stop=True)\
                            .then_inc(*pe.did(f"mask{c}"))
                        for kc in range(KC):
                            last = t_.matmul(ps[4 + c % 2], w1[:, kc, c * P:(c + 1) * P], xT[:, kc, :],
                                             start=(kc == 0), stop=(kc == 1))
                        last.then_inc(*pe.did(f"h{c}"))
                    t_.wait_ge(*dve.at(f"hid{CE - 1}", b))
                    for t in range(TB):
                        y = ps[t // 2][:, (t % 2) * D:(t % 2 + 1) * D]
                        for c in range(CE):
                            t_.matmul(y, hid[:, c, t * P:(t + 1) * P], w2[:, c, :], start=(c == 0), stop=False)
                        last = t_.matmul(y, hotT[:, t * P:(t + 1) * P], b2[:, :], start=False, stop=True)
                        if t % 2:
                            last.then_inc(*pe.did(f"y{t // 2}"))

            @block.vector
            def _(v):
                dve.open(v)
                v.memset(L["eps"][:, :], LN_EPS)
                v.memset(xe[R0:R0 + 1, :], 1.0)
                v.wait_ge(loaded, 160)
                v.tensor_copy(spreadb[:, :, :], spread[:, :, :]).then_inc(cast, 1)
                with v.Fori(0, B) as b:
                    ln_dve(v, L, h, b, dve, act, pe)
                    v.wait_ge(*pe.at("logits", b))
                    v.tensor_reduce(top[:, :], lg_ps, AX.X, ALU.max).then_inc(*dve.did("top"))
                    v.wait_ge(*dve.at("top", b))
                    v.wait_ge(*act.at("ex", b, 1))
                    v.tensor_tensor(lg[:, :, :], lg_ps, bc(top[:, :], E0), ALU.subtract).then_inc(*dve.did("lg"))
                    v.wait_ge(*dve.at("lg", b))
                    v.scalar_tensor_tensor(ranked[:, :, :], lg[:, :, :], 0.0, rank[:, :, :], ALU.is_equal, ALU.mult)\
                        .then_inc(*dve.did("ranked"))
                    v.wait_ge(*dve.at("ranked", b))
                    v.tensor_reduce(first[:, :], ranked[:, :, :], AX.X, ALU.max).then_inc(*dve.did("first"))
                    v.wait_ge(*dve.at("first", b))
                    v.wait_ge(*pe.at("hotT", b, 1))
                    v.tensor_tensor(hot[:, :, :], rank[:, :, :], bc(first[:, :], E0), ALU.is_equal)\
                        .then_inc(*dve.did("hot"))
                    v.wait_ge(*act.at("ex", b))
                    v.wait_ge(*dve.at("res1", b, 1))
                    v.tensor_reduce(den[:, :], ex[:, :, :], AX.X, ALU.add).then_inc(*dve.did("den"))
                    v.wait_ge(*dve.at("den", b))
                    v.reciprocal(prob[:, :], den[:, :]).then_inc(*dve.did("prob"))
                    for c in range(CE):
                        v.wait_ge(*act.at(f"gelu{c}", b))
                        if c == 0:
                            v.wait_ge(*pe.at("y1", b, 1))
                        v.tensor_tensor(hid[:, c, :], ps[6 + c % 2], act_h[:, c % 2, :], ALU.mult)\
                            .then_inc(*dve.did(f"hid{c}"))
                    for j in range(2):
                        v.wait_ge(*pe.at(f"y{j}", b))
                        for t in (2 * j, 2 * j + 1):
                            last = v.scalar_tensor_tensor(row(h, b * TB + t), ps[j][:, (t % 2) * D:(t % 2 + 1) * D],
                                                          prob[:, t:t + 1], row(h, b * TB + t), ALU.mult, ALU.add)
                        last.then_inc(*dve.did(f"res{j}"))

            @block.scalar
            def _(a):
                act.open(a)
                a.wait_ge(loaded, 160)
                with a.Fori(0, B) as b:
                    ln_std(a, L, b, dve, act)
                    for c in range(KC):
                        a.wait_ge(*pe.at(f"T{c}", b))
                        a.activation(xT[:, c, :], ps[c][0:DC, :], ACT.Copy).then_inc(*act.did(f"xT{c}"))
                    a.wait_ge(*pe.at("enc", b))
                    a.wait_ge(*dve.at("xn0", b))
                    a.activation(xe[0:R0, :], ps[2][0:R0, :], ACT.Identity, bias=enc_b[:, 0:1]).then_inc(*act.did("xe"))
                    a.wait_ge(*dve.at("lg", b))
                    a.wait_ge(*dve.at("den", b, 1))
                    a.activation(ex[:, :, :], lg[:, :, :], ACT.Exp).then_inc(*act.did("ex"))
                    a.wait_ge(*pe.at("hotT", b))
                    a.activation(hotT[:, :], ps[2][0:E0, :], ACT.Copy).then_inc(*act.did("hotT"))
                    a.activation(hotTb[:, :], ps[2][0:E0, :], ACT.Copy).then_inc(*act.did("hotTb"))
                    for c in range(CE):
                        a.wait_ge(*pe.at(f"h{c}", b))
                        a.wait_ge(*dve.at(f"hid{(c - 2) % CE}", b, 1 if c < 2 else 0))
                        a.activation(act_h[:, c % 2, :], ps[4 + c % 2], ACT.Gelu, bias=b1[:, c:c + 1])\
                            .then_inc(*act.did(f"gelu{c}"))

            @block.gpsimd
            def _(g):
                g.wait_ge(loaded, 160)


H1, E1, MB, KW = 12, 64, 16, 4
HP = H1 // 2
CH = H1 * E1
HALF = CH // 2
STEPS = N // MB
SPT = P // MB
CL = HALF + 8


def ttt_prepare(nc, M, ins):
    with ExitStack() as ctx:
        sb = lambda n, s, d=F32: ctx.enter_context(nc.sbuf_tensor(n, s, d))
        sem = lambda n: ctx.enter_context(nc.semaphore(n))
        L = ln_buffers(sb, "p_")
        xT = sb("p_xT", [DC, KC, N])
        wq, wv = sb("p_wq", [DC, KC, CH]), sb("p_wv", [DC, KC, CH])
        wvn = sb("p_wvn", [DC, KC, CH])
        lrw, lrb = sb("p_lrw", [DC, KC, H1]), sb("p_lrb", [P, H1])
        cw, cb = [sb("cw_q", [P, HP, KW]), sb("cw_k", [P, HP, KW])], [sb("cb_q", [P, HP]), sb("cb_k", [P, HP])]
        rope = sb("rope", [P, 2, N])
        gB, bB = sb("gB", [P, CH]), sb("bB", [P, CH])
        XP = sb("XP", [P, 2, KW + N])
        y = sb("cy", [P, 2, N])
        r1, r2 = sb("rope_c", [P, 2, N]), sb("rope_s", [P, 2, N])
        kT, qT = sb("p_kT", [P, HP, N]), sb("p_qT", [P, HP, N])
        tg, rows_ = sb("p_tg", [P, 2, CH]), sb("p_rows", [P, TB, 2, CL])
        lg = sb("p_lr", [P, TB, H1])
        h, ident, pair, ps, ps2, kT_all = M["h"], M["ident"], M["pair"], M["ps"], M["ps2"], M["kT_all"]
        loaded, kept, padded = sem("p_loaded"), sem("p_kept"), sem("p_padded")
        kst, cst = sem("p_kstored"), sem("p_cstored")
        WP = [(w_, p) for p in range(HP) for w_ in (1, 0)]
        nm = lambda x: [f"{x}{w_}{p}" for w_, p in WP]
        dve = Steps(sem("p_dve"), LN_DVE + [n for w_, p in WP for n in (f"c1{w_}{p}", f"c2{w_}{p}", f"c3{w_}{p}", f"s{w_}{p}")]
                    + [f"tg{t}" for t in range(TB)] + ["lr", "lr64"])
        act = Steps(sem("p_act"), ["std", "xT0", "xT1"] + [n for p in range(HP) for n in (f"XP{p}", f"y1{p}", f"y0{p}")] + ["sig"])
        pe = Steps(sem("p_pe"), ["T0", "T1"] + [n for p in range(HP) for n in (f"x{p}", f"r1{p}", f"r0{p}")]
                   + [f"v{t}" for t in range(TB)] + ["lr"])
        pool = Steps(sem("p_pool"), [n for w_, p in WP for n in (f"c{w_}{p}", f"z{w_}{p}")]
                     + [f"rows{t}" for t in range(TB)])
        lr_ps = ps[0][:, 0:TB * H1].rearrange("p (t h) -> p t h", t=TB)

        with nc.Block() as block:
            @block.sync
            def _(sp):
                for stores in (kept, kst, cst):
                    sp.sem_inc(stores, 1)
                for dst, src in ((wq[:, :, :], ins["t_wq"].rearrange("(k p) n -> p k n", p=DC)),
                                 (wv[:, :, :], ins["t_wv"].rearrange("(k p) n -> p k n", p=DC)),
                                 (lrw[:, :, :], ins["t_lrw"].rearrange("(k p) n -> p k n", p=DC)),
                                 (lrb[:, :], ins["t_lrb"].rearrange("(a n) -> a n", a=1).to_broadcast([P, H1])),
                                 (cw[0][:, :, :], ins["t_cwq"]), (cw[1][:, :, :], ins["t_cwk"]),
                                 (cb[0][:, :], ins["t_cbq"]), (cb[1][:, :], ins["t_cbk"]),
                                 (rope[:, :, :], ins["c_rope"]),
                                 (gB[:, :], ins["t_g"].rearrange("(a n) -> a n", a=1).to_broadcast([P, CH])),
                                 (bB[:, :], ins["t_b"].rearrange("(a n) -> a n", a=1).to_broadcast([P, CH]))):
                    sp.dma_start(dst, src).then_inc(loaded, 16)
                with sp.Fori(0, B) as b:
                    sp.wait_ge(*act.at("xT1", b))
                    sp.dma_start(M["xT_d"][bass.ds(b, 1)].rearrange("a p k n -> (a p) k n"), xT[:, :, :]).then_inc(kept, 16)
                    sp.wait_ge(*pool.at(f"z1{HP - 1}", b))
                    sp.dma_start(kT_all[:, :, bass.ds(b, 1), :].rearrange("p h a n -> p (h a) n"), kT[:, :, :]).then_inc(kst, 16)
                    sp.wait_ge(*pool.at(f"z0{HP - 1}", b))
                    for t in range(TB):
                        for w_, src in ((0, qT), (1, kT)):
                            sp.dma_start(M["qk1_d"][bass.ds(b * TB + t, 1), w_].rearrange("a p h n -> (a p) h n"),
                                         src[:, :, t * P:(t + 1) * P]).then_inc(kst, 16)
                    sp.wait_ge(*pool.at(f"rows{TB - 1}", b))
                    sp.wait_ge(*dve.at("lr64", b))
                    for t in range(TB):
                        for hh in range(2):
                            sp.dma_start(M["c_d"][bass.ds(b, 1), hh, t * P:(t + 1) * P, :].rearrange("a k n -> (a k) n"),
                                         rows_[:, t, hh, :]).then_inc(cst, 16)
                sp.wait_ge(kept, 16 * B + 1)
                sp.wait_ge(kst, 16 * 9 * B + 1)
                sp.wait_ge(cst, 16 * 8 * B + 1)
                sp.wait_ge(loaded, 16 * 11)

            @block.tensor
            def _(t_):
                pe.open(t_)
                t_.wait_ge(loaded, 16 * 11)
                with t_.Fori(0, B) as b:
                    ln_turn(t_, L, ident, ps[0:2], b, dve, act, pe)
                    t_.wait_ge(*act.at("xT1", b))
                    for p in range(HP):
                        t_.wait_ge(*act.at(f"XP{(p - 2) % HP}", b, 1 if p < 2 else 0))
                        if p < 2:
                            t_.wait_ge(*dve.at(f"tg{TB - 1}", b, 1))
                        for kc in range(KC):
                            last = t_.matmul(ps[2 + p % 2], wq[:, kc, p * P:(p + 1) * P], xT[:, kc, :],
                                             start=(kc == 0), stop=(kc == 1))
                        last.then_inc(*pe.did(f"x{p}"))
                        for w_ in (1, 0):
                            t_.wait_ge(*dve.at(f"c3{w_}{p}", b))
                            t_.matmul(ps[4 + 2 * w_ + p % 2], pair[:, :], y[:, w_, :], start=True, stop=True)\
                                .then_inc(*pe.did(f"r{w_}{p}"))
                    t_.wait_ge(*pool.at(f"z1{HP - 1}", b))
                    for t in range(TB):
                        bank = ps2[1 + t % 2]
                        if t >= 2:
                            t_.wait_ge(*dve.at(f"tg{t - 2}", b))
                        elif t == 0:
                            t_.wait_ge(*act.at(f"XP{HP - 1}", b))
                        else:
                            t_.wait_ge(*dve.at(f"s0{HP - 1}", b))
                        for hh in range(2):
                            for kc in range(KC):
                                t_.matmul(bank[:, hh, 0:HALF], xT[:, kc, t * P:(t + 1) * P],
                                          wvn[:, kc, hh * HALF:(hh + 1) * HALF], start=(kc == 0), stop=False,
                                          skip_group_check=True)
                            for p in range(HP):
                                last = t_.matmul(bank[:, hh, p * E1:(p + 1) * E1], kT[:, p, t * P:(t + 1) * P],
                                                 ident[:, hh * E1:(hh + 1) * E1], start=False, stop=(p == HP - 1),
                                                 skip_group_check=True)
                        last.then_inc(*pe.did(f"v{t}"))
                    for t in range(TB):
                        for kc in range(KC):
                            last = t_.matmul(lr_ps[:, t, :], xT[:, kc, t * P:(t + 1) * P], lrw[:, kc, :],
                                             start=(kc == 0), stop=(kc == 1))
                    last.then_inc(*pe.did("lr"))

            @block.vector
            def _(v):
                dve.open(v)
                v.memset(L["eps"][:, :], LN_EPS)
                v.wait_ge(loaded, 16 * 11)
                v.tensor_scalar(wvn[:, :, :], wv[:, :, :], -1.0, None, ALU.mult)
                with v.Fori(0, B) as b:
                    ln_dve(v, L, h, b, dve, act, pe)
                    for w_, p in WP:
                        for k in range(1, KW):
                            if k == 1:
                                v.wait_ge(*act.at(f"y{w_}{p}", b))
                            else:
                                v.wait_ge(*dve.at(f"c{k - 1}{w_}{p}", b))
                            v.scalar_tensor_tensor(y[:, w_, :], XP[:, p % 2, k:k + N], cw[w_][:, p, k:k + 1], y[:, w_, :],
                                                   ALU.mult, ALU.add).then_inc(*dve.did(f"c{k}{w_}{p}"))
                        v.wait_ge(*pe.at(f"r{w_}{p}", b))
                        v.wait_ge(*pool.at(f"z{w_}{(p - 1) % HP}", b, 1 if p == 0 else 0))
                        v.tensor_tensor(r2[:, w_, :], ps[4 + 2 * w_ + p % 2], rope[:, 1, :], ALU.mult)\
                            .then_inc(*dve.did(f"s{w_}{p}"))
                    for t in range(TB):
                        v.wait_ge(*pe.at(f"v{t}", b))
                        v.wait_ge(*pool.at(f"rows{(t - 2) % TB}", b, 1 if t < 2 else 0))
                        v.tensor_tensor(tg[:, t % 2, :].rearrange("p (a n) -> p a n", a=2), ps2[1 + t % 2][:, :, 0:HALF],
                                        bB[:, :].rearrange("p (a n) -> p a n", a=2), ALU.add).then_inc(*dve.did(f"tg{t}"))
                    v.wait_ge(*pe.at("lr", b))
                    v.wait_ge(*dve.at("lr64", b, 1))
                    v.tensor_tensor(lg[:, :, :], lr_ps, lrb[:, :].unsqueeze(1).to_broadcast([P, TB, H1]), ALU.add)\
                        .then_inc(*dve.did("lr"))
                    v.wait_ge(*act.at("sig", b))
                    v.wait_ge(cst, b * (16 * 8) + 1)
                    v.tensor_scalar(rows_[:, :, :, HALF:HALF + HP], lg[:, :, :].rearrange("p t (a h) -> p t a h", a=2),
                                    1.0 / E1, None, ALU.mult).then_inc(*dve.did("lr64"))

            @block.scalar
            def _(a):
                act.open(a)
                a.wait_ge(loaded, 16 * 11)
                a.wait_ge(padded, 1)
                with a.Fori(0, B) as b:
                    ln_std(a, L, b, dve, act)
                    for c in range(KC):
                        a.wait_ge(*pe.at(f"T{c}", b))
                        a.wait_ge(*pe.at("lr", b, 1))
                        a.wait_ge(kept, b * 16 + 1)
                        a.activation(xT[:, c, :], ps[c][0:DC, :], ACT.Copy).then_inc(*act.did(f"xT{c}"))
                    for p in range(HP):
                        a.wait_ge(*pe.at(f"x{p}", b))
                        a.wait_ge(*dve.at(f"c30{(p - 2) % HP}", b, 1 if p < 2 else 0))
                        a.activation(XP[:, p % 2, KW:KW + N], ps[2 + p % 2], ACT.Copy).then_inc(*act.did(f"XP{p}"))
                        a.wait_ge(*act.at(f"XP{p}", b))
                        for w_ in (1, 0):
                            a.wait_ge(*pe.at(f"r{w_}{(p - 1) % HP}", b, 1 if p == 0 else 0))
                            a.wait_ge(*pool.at(f"c{w_}{(p - 1) % HP}", b, 1 if p == 0 else 0))
                            a.activation(y[:, w_, :], XP[:, p % 2, 0:N], ACT.Identity, bias=cb[w_][:, p:p + 1],
                                         scale=cw[w_][:, p, 0:1]).then_inc(*act.did(f"y{w_}{p}"))
                    a.wait_ge(*dve.at("lr", b))
                    a.activation(lg[:, :, :], lg[:, :, :], ACT.Sigmoid).then_inc(*act.did("sig"))

            @block.gpsimd
            def _(g):
                pool.open(g)
                g.memset(XP[:, :, 0:KW], 0.0)
                g.memset(rows_[:, :, :, HALF + HP:CL], 0.0).then_inc(padded, 1)
                g.wait_ge(loaded, 16 * 11)
                with g.Fori(0, B) as b:
                    for w_, p in WP:
                        g.wait_ge(*dve.at(f"c3{w_}{p}", b))
                        g.tensor_tensor(r1[:, w_, :], y[:, w_, :], rope[:, 0, :], ALU.mult).then_inc(*pool.did(f"c{w_}{p}"))
                        g.wait_ge(*pool.at(f"c{w_}{p}", b))
                        g.wait_ge(*dve.at(f"s{w_}{p}", b))
                        if p == 0:
                            g.wait_ge(kst, b * (16 * 9) + 1)
                            g.wait_ge(*pe.at("lr", b, 1))
                        g.tensor_tensor((qT, kT)[w_][:, p, :], r1[:, w_, :], r2[:, w_, :], ALU.add)\
                            .then_inc(*pool.did(f"z{w_}{p}"))
                    for t in range(TB):
                        g.wait_ge(*dve.at(f"tg{t}", b))
                        if t == 0:
                            g.wait_ge(cst, b * (16 * 8) + 1)
                        g.tensor_tensor(rows_[:, t, :, 0:HALF], tg[:, t % 2, :].rearrange("p (a n) -> p a n", a=2),
                                        gB[:, :].rearrange("p (a n) -> p a n", a=2), ALU.mult).then_inc(*pool.did(f"rows{t}"))


def ttt_recur(nc, M, ins):
    with ExitStack() as ctx:
        sb = lambda n, s, d=F32: ctx.enter_context(nc.sbuf_tensor(n, s, d))
        sem = lambda n: ctx.enter_context(nc.semaphore(n))
        G = 2
        GP, GC = HP // G, HALF // G
        Wsb, Bsb = sb("Wsb", [P, HP, B, E1]), sb("Bsb", [P, HALF])
        W0, B0 = sb("W0", [P, HALF]), sb("B0", [P, HALF])
        mean0 = sb("mean0", [P, 2, HP])
        KTz, ek = sb("KTz", [P, HP, B, 2, MB]), sb("ek", [P, HP, P])
        tgt, g2 = sb("tgt", [P, CL]), sb("g2", [P, HALF])
        t15, lastb = sb("t15", [P, 1]), sb("lastb", [P, P])
        eps = sb("r_eps", [P, 1])
        z, sq, xh, u, gx, pr = ([sb(f"{n}{g}", [P, GC]) for g in range(G)] for n in ("z_", "sq_", "xh_", "u_", "gx_", "pr_"))
        var, std, rs, rl, mm = ([sb(f"{n}{g}", [P, GP]) for g in range(G)] for n in ("var", "std_", "rs", "rl", "mm_"))
        sums = [sb(f"sums{g}", [P, 2, GP]) for g in range(G)]
        neg = [sb(f"neg{g}", [P, GP]) for g in range(G)]
        gr = sb("gr", [P, HALF])
        grD = sb("grD", [P, HP, B, E1])
        ident, blk, ps, ps2, kT_all = M["ident"], M["blk"], M["ps"], M["ps2"], M["kT_all"]
        BZ, Zps, TK = ps[3], ps[4:6], ps[6:8]
        loaded, primed_d, primed_p, primed_a, primed_g, primed_s = (sem("r_" + n) for n in ("loaded", "pr_d", "pr_p", "pr_a", "pr_g", "pr_s"))
        tgt_in, gr_out, snapped = sem("r_tgt"), sem("r_gr"), sem("r_snap")
        OPS = ["z", "sq", "var", "rs", "rl", "xh", "u", "gx", "m1", "pr", "m2", "neg", "t", "g", "d"]
        ORDER = [(o, g) for g in range(G) for o in OPS]
        dve = Steps(sem("r_dve"), [f"{o}{g}" for o, g in ORDER])
        act = Steps(sem("r_act"), ["std0", "W1", "B1", "ek0", "ek1", "kz0", "kz1", "d0", "std1", "W0", "B0", "d1"])
        pe = Steps(sem("r_pe"), ["T0", "T1", "Z1", "upd0", "bz0", "Z0", "upd1", "bz1"])
        b3 = lambda ap: ap.rearrange("p (h e) -> p h e", e=E1)
        bc = lambda ap: ap.unsqueeze(2).to_broadcast([P, ap.shape[1], E1])
        wps = [ps[p // 2][:, (p % 2) * B * E1:(p % 2 + 1) * B * E1] for p in range(HP)]

        def diagonal(g, b):
            r = slice(32 * b, 32 * b + 32)
            return grD[r, g * GP:(g + 1) * GP, b, :], b3(gr[r, g * GC:(g + 1) * GC])

        with nc.Block() as block:
            @block.sync
            def _(sp):
                sp.sem_inc(gr_out, 1)
                sp.dma_start(W0[:, :], ins["t_W1"]).then_inc(loaded, 16)
                for b in range(B):
                    for hh in range(2):
                        r0 = 32 * b + 16 * hh
                        for dst, src in ((B0, "t_b1"), (g2, "t_g")):
                            sp.dma_start(dst[r0:r0 + MB, :], ins[src][hh * HALF:(hh + 1) * HALF]
                                         .rearrange("(a n) -> a n", a=1).to_broadcast([MB, HALF])).then_inc(loaded, 16)
                sp.dma_start(t15[:, :], ins["t_idx"][MB - 1:MB].rearrange("(a n) -> a n", a=1).to_broadcast([P, 1]))\
                    .then_inc(loaded, 16)
                tg_of = lambda s: M["c_d"][:, :, bass.ds(s * MB, MB), :].rearrange("b h k n -> (b h) k n")
                sp.dma_start(tgt[:, :], tg_of(0)).then_inc(tgt_in, 16)
                sp.wait_ge(primed_a, 2)
                with sp.Fori(0, STEPS // SPT) as sc:
                    sp.wait_ge(*act.at("B1", sc * SPT))
                    sp.dma_start(M["W_d"][bass.ds(sc, 1)].rearrange("a p h b e -> (a p) (h b e)"),
                                 Wsb[:, :, :, :].rearrange("p h b e -> p (h b e)")).then_inc(snapped, 16)
                    sp.dma_start(M["B_d"][bass.ds(sc, 1)].rearrange("a p n -> (a p) n"), Bsb[:, :]).then_inc(snapped, 16)
                    with sp.Fori(0, SPT) as j:
                        s = sc * SPT + j
                        sp.wait_ge(*dve.at("gx1", s))
                        sp.dma_start(tgt[:, :], tg_of((s + 1) % STEPS)).then_inc(tgt_in, 16)
                        sp.wait_ge(*dve.at("g1", s))
                        sp.dma_start(M["g_d"][:, :, bass.ds(s * MB, MB), :].rearrange("b h k n -> (b h) k n"), gr[:, :]).then_inc(gr_out, 16)
                sp.wait_ge(gr_out, 16 * STEPS + 1)
                sp.wait_ge(tgt_in, 16 * (STEPS + 1))
                sp.wait_ge(snapped, 32 * (STEPS // SPT))

            @block.tensor
            def _(t_):
                pe.open(t_)
                t_.wait_ge(primed_d, 4)
                for i in range(HP // 2):
                    t_.matmul(ps[i].rearrange("p (h b e) -> p h b e", h=2, b=B), ident[:, :],
                              b3(W0[:, 2 * i * E1:(2 * i + 2) * E1]).unsqueeze(2).to_broadcast([P, 2, B, E1]),
                              start=True, stop=True, skip_group_check=True)
                t_.matmul(BZ[:, 0:HALF], ident[:, :], B0[:, :], start=True, stop=True, skip_group_check=True)\
                    .then_inc(primed_p, 1)

                def read_out(g):
                    for b in range(B):
                        for i in range(GP):
                            last = t_.matmul(Zps[g][32 * b:32 * b + 32, i * E1:(i + 1) * E1],
                                             KTz[:, g * GP + i, b, :, :].rearrange("p h k -> p (h k)"),
                                             Wsb[:, g * GP + i, b, :], start=True, stop=True)
                    return last

                t_.wait_ge(primed_a, 2)
                read_out(0).then_inc(primed_p, 1)
                with t_.Fori(0, STEPS // SPT) as sc:
                    with t_.Fori(0, SPT) as j:
                        s = sc * SPT + j
                        for g in range(G):
                            t_.wait_ge(*act.at("kz1", s, 1))
                            for i in range(GP):
                                last = t_.transpose(TK[g][:, i * P:(i + 1) * P],
                                                    KTz[:, g * GP + i, :, :, :].rearrange("p b h k -> p (b h k)"), ident[:, :])
                            last.then_inc(*pe.did(f"T{g}"))
                        t_.wait_ge(*act.at("W1", s))
                        read_out(1).then_inc(*pe.did("Z1"))
                        for g in range(G):
                            t_.wait_ge(*act.at(f"d{g}", s))
                            t_.wait_ge(*dve.at(f"d{g}", s))
                            for i in range(GP):
                                p = g * GP + i
                                last = t_.matmul(wps[p], ek[:, p, :], grD[:, p, :, :].rearrange("p b e -> p (b e)"),
                                                 start=False, stop=False, skip_group_check=True)
                            last.then_inc(*pe.did(f"upd{g}"))
                            t_.matmul(BZ[:, g * GC:(g + 1) * GC], lastb[:, :], gr[:, g * GC:(g + 1) * GC],
                                      start=False, stop=False, skip_group_check=True).then_inc(*pe.did(f"bz{g}"))
                            if g == 0:
                                t_.wait_ge(*act.at("W0", s))
                                read_out(0).then_inc(*pe.did("Z0"))

            @block.vector
            def _(v):
                dve.open(v)
                v.memset(eps[:, :], LN_EPS)
                v.wait_ge(loaded, 16 * 18)
                v.tensor_reduce(mean0[:, 0, :], b3(W0[:, :]), AX.X, ALU.add)
                v.tensor_reduce(mean0[:, 1, :], b3(B0[:, :]), AX.X, ALU.add)
                v.tensor_scalar(t15[:, :], t15[:, :], 1.0 / MB, None, ALU.add)
                v.tensor_tensor(g2[:, :], g2[:, :], g2[:, :], ALU.mult).then_inc(primed_d, 1)
                v.wait_ge(primed_d, 1)
                v.tensor_scalar(mean0[:, :, :], mean0[:, :, :], 1.0 / E1, None, ALU.mult)
                v.tensor_scalar(t15[:, :], t15[:, :], 0.0, -1.0, ALU.max, ALU.mult).then_inc(primed_d, 1)
                v.wait_ge(primed_d, 2)
                v.tensor_tensor(b3(W0[:, :]), b3(W0[:, :]), bc(mean0[:, 0, :]), ALU.subtract)
                v.tensor_tensor(b3(B0[:, :]), b3(B0[:, :]), bc(mean0[:, 1, :]), ALU.subtract)
                v.tensor_scalar(lastb[:, :], blk[:, :], t15[:, 0:1], None, ALU.mult).then_inc(primed_d, 2)
                v.wait_ge(primed_p, 2)
                v.wait_ge(primed_g, 2)

                def op(o, g, s):
                    cols = slice(g * GC, (g + 1) * GC)
                    me = lambda n, back=0: v.wait_ge(*dve.at(f"{n}{g}", s, back))
                    done = dve.did(f"{o}{g}") if o not in ("t", "g", "d") else None
                    if o == "z":
                        v.wait_ge(*pe.at(f"Z{g}", s, 1 - g))
                        v.wait_ge(*act.at(f"B{g}", s, 1 - g))
                        me("g", 1)
                        v.tensor_tensor(z[g][:, :], Zps[g][:, 0:GC], Bsb[:, cols], ALU.add).then_inc(*done)
                    elif o == "sq":
                        me("z")
                        v.tensor_tensor(sq[g][:, :], z[g][:, :], z[g][:, :], ALU.mult).then_inc(*done)
                    elif o == "var":
                        me("sq")
                        v.tensor_reduce(var[g][:, :], b3(sq[g][:, :]), AX.X, ALU.add).then_inc(*done)
                    elif o == "rs":
                        v.wait_ge(*act.at(f"std{g}", s))
                        v.reciprocal(rs[g][:, :], std[g][:, :]).then_inc(*done)
                    elif o == "rl":
                        me("rs")
                        v.wait_ge(tgt_in, 16 * s + 16)
                        v.tensor_tensor(rl[g][:, :], rs[g][:, :], tgt[:, HALF + g * GP:HALF + (g + 1) * GP], ALU.mult)\
                            .then_inc(*done)
                    elif o == "xh":
                        v.tensor_tensor(b3(xh[g][:, :]), b3(z[g][:, :]), bc(rs[g][:, :]), ALU.mult).then_inc(*done)
                    elif o == "u":
                        me("xh")
                        v.tensor_tensor(u[g][:, :], xh[g][:, :], g2[:, cols], ALU.mult).then_inc(*done)
                    elif o == "gx":
                        me("u")
                        v.tensor_tensor(gx[g][:, :], u[g][:, :], tgt[:, cols], ALU.add).then_inc(*done)
                    elif o == "m1":
                        me("gx")
                        v.tensor_reduce(sums[g][:, 0, :], b3(gx[g][:, :]), AX.X, ALU.add).then_inc(*done)
                    elif o == "pr":
                        v.scalar_tensor_tensor(pr[g][:, :], gx[g][:, :], -1.0 / E1, xh[g][:, :], ALU.mult, ALU.mult).then_inc(*done)
                    elif o == "m2":
                        me("pr")
                        v.tensor_reduce(sums[g][:, 1, :], b3(pr[g][:, :]), AX.X, ALU.add).then_inc(*done)
                    elif o == "neg":
                        v.tensor_scalar(neg[g][:, :], sums[g][:, 0, :], -1.0 / E1, None, ALU.mult).then_inc(*done)
                    elif o == "t":
                        me("m2")
                        for i in range(GP):
                            c = slice(i * E1, (i + 1) * E1)
                            last = v.scalar_tensor_tensor(gx[g][:, c], xh[g][:, c], sums[g][:, 1, i:i + 1], gx[g][:, c],
                                                          ALU.mult, ALU.add)
                        last.then_inc(*dve.did(f"t{g}"))
                    elif o == "g":
                        me("t")
                        v.wait_ge(gr_out, 16 * s + 1)
                        v.wait_ge(*pe.at(f"bz{g}", s, 1))
                        for i in range(GP):
                            c = slice(i * E1, (i + 1) * E1)
                            last = v.tensor_scalar(gr[:, (g * GP + i) * E1:(g * GP + i + 1) * E1], gx[g][:, c],
                                                   neg[g][:, i:i + 1], rl[g][:, i:i + 1], ALU.add, ALU.mult)
                        last.then_inc(*dve.did(f"g{g}"))
                    else:
                        me("g")
                        for b in (0, 1):
                            last = v.tensor_copy(*diagonal(g, b))
                        last.then_inc(*dve.did(f"d{g}"))

                with v.Fori(0, STEPS // SPT) as sc:
                    with v.Fori(0, SPT) as j:
                        for o, g in ORDER:
                            op(o, g, sc * SPT + j)

            @block.scalar
            def _(a):
                act.open(a)

                def copy_w(g):
                    flat = [x[:, :, :].rearrange("p a n -> p (a n)") for x in ps2[0:2]]
                    dst = Wsb[:, :, :, :].rearrange("p h b e -> p (h b e)")
                    W = B * E1
                    for c0, c1 in ([(0, 3 * W)], [(3 * W, 4 * W), (4 * W, 6 * W)])[g]:
                        last = a.activation(dst[:, c0:c1], flat[c0 // 1024][:, c0 % 1024:c0 % 1024 + c1 - c0], ACT.Copy)
                    return last

                def copy_b(g):
                    cols = slice(g * GC, (g + 1) * GC)
                    return a.activation(Bsb[:, cols], BZ[:, cols], ACT.Copy)

                def keys(s, hh):
                    r = slice(hh * E1, (hh + 1) * E1)
                    return a.activation(KTz[r, :, :, hh, :].rearrange("p h b k -> p (h b) k"),
                                        kT_all[r, :, :, bass.ds(s * MB, MB)].rearrange("p h b k -> p (h b) k"), ACT.Copy)

                a.wait_ge(primed_d, 1)
                a.activation(std[0][:, 0:1], eps[:, 0:1], ACT.Sqrt).then_inc(primed_s, 1)
                a.wait_ge(primed_s, 1)
                a.wait_ge(primed_p, 1)
                for g in range(G):
                    copy_w(g)
                    copy_b(g)
                a.wait_ge(primed_g, 2)
                keys(0, 0)
                keys(0, 1).then_inc(primed_a, 2)
                with a.Fori(0, STEPS // SPT) as sc:
                    with a.Fori(0, SPT) as j:
                        s = sc * SPT + j

                        def root(g):
                            a.wait_ge(*dve.at(f"var{g}", s))
                            a.activation(std[g][:, :], var[g][:, :], ACT.Sqrt, bias=eps[:, 0:1], scale=1.0 / E1)\
                                .then_inc(*act.did(f"std{g}"))

                        def state(g):
                            a.wait_ge(*pe.at(f"bz{g}", s, g))
                            copy_w(g).then_inc(*act.did(f"W{g}"))
                            copy_b(g).then_inc(*act.did(f"B{g}"))

                        def spread(g):
                            a.wait_ge(*dve.at(f"g{g}", s))
                            for b in (2, 3):
                                last = a.activation(*diagonal(g, b), ACT.Copy)
                            last.then_inc(*act.did(f"d{g}"))

                        root(0)
                        state(1)
                        for g in range(G):
                            a.wait_ge(*pe.at(f"T{g}", s))
                            a.activation(ek[:, g * GP:(g + 1) * GP, :].rearrange("p h c -> p (h c)"), TK[g][:, 0:GP * P],
                                         ACT.Identity, scale=t15[:, 0:1]).then_inc(*act.did(f"ek{g}"))
                        a.wait_ge(*pe.at("Z1", s))
                        for hh in range(2):
                            keys((s + 1) % STEPS, hh).then_inc(*act.did(f"kz{hh}"))
                        spread(0)
                        root(1)
                        a.wait_ge(snapped, 32 * sc + 32)
                        state(0)
                        spread(1)

            @block.gpsimd
            def _(g):
                g.memset(KTz[:, :, :, :, :], 0.0).then_inc(primed_g, 1)
                g.memset(grD[:, :, :, :], 0.0).then_inc(primed_g, 1)


def ttt_output(nc, M, ins):
    with ExitStack() as ctx:
        sb = lambda n, s, d=F32: ctx.enter_context(nc.sbuf_tensor(n, s, d))
        sem = lambda n: ctx.enter_context(nc.semaphore(n))
        qk = [sb(f"o_qk{r}", [P, 2, HP, P]) for r in range(2)]
        Ws, Gs, brow = ([sb(f"o_{n}{r}", s) for r in range(2)] for n, s in
                        (("W", [P, HALF]), ("G", [P, 2, HALF]), ("b", [1, CH])))
        xT = sb("o_xT", [DC, KC, N])
        wg, wo = sb("o_wg", [DC, KC, CH]), sb("o_wo", [P, HP, D])
        gB, bB = sb("o_gB", [P, CH]), sb("o_bB", [P, CH])
        psc, pbc = sb("o_ps", [P, HP]), sb("o_pb", [P, HP])
        idx, same, prev = sb("o_idx", [P, P]), sb("o_same", [P, P]), sb("o_prev", [P, P])
        inv, i15 = sb("o_inv", [P, P]), sb("o_i15", [P, 1])
        ones = sb("o_ones", [1, P])
        eps = sb("o_eps", [P, 1])
        Sm = sb("o_Sm", [P, 2, HP, P])
        sq, zn = sb("o_sq", [P, CH]), sb("o_zn", [P, CH])
        var, std, rs = sb("o_var", [P, H1]), sb("o_std", [P, H1]), sb("o_rs", [P, H1])
        st, mv, std2, rs2 = sb("o_st", [P, 2, 6]), sb("o_mv", [P, 2]), sb("o_std2", [P, 1]), sb("o_rs2", [P, 1])
        gate, yT = sb("o_gate", [P, TB, HP, P]), sb("o_yT", [P, HP, P])
        tick = sb("o_tick", [P, 1])
        h, ident, ps, ps2 = M["h"], M["ident"], M["ps"], M["ps2"]
        loaded, ready, masked = sem("o_loaded"), sem("o_ready"), sem("o_masked")
        tiles_in, xs_in = [sem(f"o_in{r}") for r in range(2)], sem("o_xin")
        R = range(TB)
        OUT = ps[3][:, 256:256 + D]
        prog = []
        for i in range(TB + 1):
            if i < TB:
                prog += [f"S{i}"]
            if i:
                prog += []
            if i < TB:
                prog += [f"Z{i}"]
            if i:
                prog += [f"T{i - 1}"]
            if i < TB:
                prog += [f"q{i}"]
            if i:
                prog += [f"y{i - 1}"]
        pe = Steps(sem("o_pe"), [f"gate{t}" for t in R] + prog)
        late = ["var", "rs", "zn", "zq", "stats", "aggr", "rs2", "nrm", "sc", "res"]
        dve = Steps(sem("o_dve"), [n for i in range(TB + 1) for n in
                                   ([f"Sm{i}"] if i < TB else []) + ([f"{o}{i - 1}" for o in late] if i else [])])
        act = Steps(sem("o_act"), [f"gate{t}" for t in R] + [n for t in R for n in (f"sq{t}", f"std{t}", f"std2{t}")])
        pool = Steps(sem("o_pool"), [n for t in R for n in (f"g{t}", f"b{t}", f"y{t}")])
        LOADS = 16 * 7

        with nc.Block() as block:
            @block.sync
            def _(sp):
                for dst, src in ((wg[:, :, :], ins["t_wg"].rearrange("(k p) n -> p k n", p=DC)),
                                 (wo[:, :, :], ins["t_wo"].rearrange("(c p) n -> p c n", p=P)),
                                 (gB[:, :], ins["t_g"].rearrange("(a n) -> a n", a=1).to_broadcast([P, CH])),
                                 (bB[:, :], ins["t_b"].rearrange("(a n) -> a n", a=1).to_broadcast([P, CH])),
                                 (psc[:, :], ins["t_ps"]), (pbc[:, :], ins["t_pb"]),
                                 (same[:, :], ins["c_same"]), (prev[:, :], ins["c_prev"]), (inv[:, :], ins["c_inv"]),
                                 (idx[:, :], ins["t_idx8"].rearrange("(a n) -> a n", a=1).to_broadcast([P, P]))):
                    sp.dma_start(dst, src).then_inc(loaded, 16)
                with sp.Fori(0, B) as b:
                    sp.wait_ge(*pe.at("gate3", b, 1))
                    sp.dma_start(xT[:, :, :], M["xT_d"][bass.ds(b, 1)].rearrange("a p k n -> (a p) k n")).then_inc(xs_in, 16)
                    for t in R:
                        r = t % 2
                        sp.wait_ge(*pe.at(f"q{(t - 2) % TB}", b, 1 if t < 2 else 0))
                        for w_ in range(2):
                            sp.dma_start(qk[r][:, w_, :, :], M["qk1_d"][bass.ds(b * TB + t, 1), w_].rearrange("a p h n -> (a p) h n"))\
                                .then_inc(tiles_in[r], 16)
                        sp.dma_start(Ws[r][:, :].rearrange("p (h e) -> p h e", e=E1),
                                     M["W_d"][t, :, :, bass.ds(b, 1), :].rearrange("p h b e -> p (h b) e")).then_inc(tiles_in[r], 16)
                        for hh in range(2):
                            sp.dma_start(Gs[r][:, hh, :], M["g_d"][bass.ds(b, 1), hh, t * P:(t + 1) * P, :]
                                         .rearrange("a k n -> (a k) n")).then_inc(tiles_in[r], 16)
                            sp.dma_start(brow[r][:, hh * HALF:(hh + 1) * HALF],
                                         M["B_d"].rearrange("s (b h k) n -> s b h k n", b=B, h=2)[t, bass.ds(b, 1), hh, 0, :])\
                                .then_inc(tiles_in[r], 16)
                for r in range(2):
                    sp.wait_ge(tiles_in[r], LOADS * 2 * B)
                sp.wait_ge(xs_in, 16 * B)

            @block.tensor
            def _(t_):
                pe.open(t_)
                t_.wait_ge(loaded, 160)
                t_.wait_ge(ready, 2)
                with t_.Fori(0, B) as b:
                    t_.wait_ge(xs_in, 16 * b + 16)
                    t_.wait_ge(*dve.at("sc3", b, 1))
                    for t in R:
                        if t:
                            t_.wait_ge(*act.at(f"gate{t - 1}", b))
                        for c in range(HP):
                            for kc in range(KC):
                                last = t_.matmul(ps[6 + c // 4][:, (c % 4) * P:(c % 4 + 1) * P], wg[:, kc, c * P:(c + 1) * P],
                                                 xT[:, kc, t * P:(t + 1) * P], start=(kc == 0), stop=(kc == 1))
                        last.then_inc(*pe.did(f"gate{t}"))
                    for i in range(TB + 1):
                        r = i % 2
                        if i < TB:
                            t_.wait_ge(tiles_in[r], b * (2 * LOADS) + LOADS * (i // 2 + 1))
                            t_.wait_ge(*(dve.at(f"res{i - 2}", b) if i >= 2 else dve.at("Sm0", b) if i else dve.at("res3", b, 1)))
                            for hh in range(2):
                                rr = slice(hh * E1, (hh + 1) * E1)
                                for p in range(HP):
                                    last = t_.matmul(ps[2 * hh + p // 4][:, (p % 4) * P:(p % 4 + 1) * P], qk[r][rr, 1, p, :],
                                                     qk[r][rr, 0, p, :], start=True, stop=True)
                            last.then_inc(*pe.did(f"S{i}"))
                            t_.wait_ge(*(dve.at(f"zn{i - 1}", b) if i else dve.at("zn3", b, 1)))
                            t_.wait_ge(*(act.at(f"sq{i - 1}", b) if i else act.at("sq3", b, 1)))
                            for hh in range(2):
                                rr = slice(hh * E1, (hh + 1) * E1)
                                t_.matmul(ps[4 + hh][:, 0:HALF], ones[:, :], brow[r][:, hh * HALF:(hh + 1) * HALF],
                                          start=True, stop=False, skip_group_check=True)
                                for p in range(HP):
                                    t_.matmul(ps[4 + hh][:, p * E1:(p + 1) * E1], qk[r][rr, 0, p, :],
                                              Ws[r][rr, p * E1:(p + 1) * E1], start=False, stop=False, skip_group_check=True)
                            t_.wait_ge(*dve.at(f"Sm{i}", b))
                            for hh in range(2):
                                for p in range(HP):
                                    last = t_.matmul(ps[4 + hh][:, p * E1:(p + 1) * E1], Sm[:, hh, p, :],
                                                     Gs[r][:, hh, p * E1:(p + 1) * E1], start=False, stop=True,
                                                     skip_group_check=True)
                            last.then_inc(*pe.did(f"Z{i}"))
                        if i:
                            t_.wait_ge(*dve.at(f"nrm{i - 1}", b))
                            t_.wait_ge(*act.at("gate3", b))
                            for c in range(HP):
                                last = t_.transpose(ps[6 + c // 4][:, (c % 4) * P:(c % 4 + 1) * P], zn[:, c * P:(c + 1) * P],
                                                    ident[:, :])
                            last.then_inc(*pe.did(f"T{i - 1}"))
                        if i < TB:
                            t_.wait_ge(*(dve.at(f"sc{i - 1}", b) if i else act.at("gate3", b)))
                            for p in range(HP):
                                last = t_.transpose(ps[6 + p // 4][:, (p % 4) * P:(p % 4 + 1) * P], qk[r][:, 0, p, :], ident[:, :])
                            last.then_inc(*pe.did(f"q{i}"))
                        if i:
                            t_.wait_ge(*pool.at(f"y{i - 1}", b))
                            for c in range(HP):
                                last = t_.matmul(OUT, yT[:, c, :], wo[:, c, :], start=(c == 0), stop=(c == HP - 1))
                            last.then_inc(*pe.did(f"y{i - 1}"))

            @block.vector
            def _(v):
                dve.open(v)
                v.memset(eps[:, :], LN_EPS)
                v.memset(ones[:, :], 1.0)
                v.wait_ge(loaded, 160)
                v.tensor_tensor(idx[:, :], idx[:, :], inv[:, :], ALU.add).then_inc(ready, 1)
                v.wait_ge(ready, 1)
                v.tensor_scalar(inv[:, :], idx[:, :], 0.0, -1.0, ALU.max, ALU.mult).then_inc(masked, 1)
                v.wait_ge(masked, 1)
                v.tensor_tensor(same[:, :], same[:, :], inv[:, :], ALU.mult)
                v.tensor_copy(i15[:, :], inv[:, P - 1:P]).then_inc(masked, 1)
                v.wait_ge(masked, 2)
                v.scalar_tensor_tensor(idx[:, :], prev[:, :], i15[:, 0:1], same[:, :], ALU.mult, ALU.add).then_inc(ready, 1)
                v.wait_ge(ready, 2)
                with v.Fori(0, B) as b:
                    for i in range(TB + 1):
                        if i < TB:
                            v.wait_ge(*pe.at(f"S{i}", b))
                            for hh in range(2):
                                for p0, n in ((0, 4), (4, 2)):
                                    last = v.scalar_tensor_tensor(
                                        Sm[:, hh, p0:p0 + n, :], ps[2 * hh + p0 // 4][:, 0:n * P].rearrange("p (h n) -> p h n", n=P),
                                        1.0, idx[:, :].unsqueeze(1).to_broadcast([P, n, P]), ALU.add, ALU.mult)
                            last.then_inc(*dve.did(f"Sm{i}"))
                        if not i:
                            continue
                        t = i - 1
                        me = lambda n: v.wait_ge(*dve.at(f"{n}{t}", b))
                        h3 = lambda ap: ap.rearrange("p (h e) -> p h e", e=E1)
                        v.wait_ge(*act.at(f"sq{t}", b))
                        v.tensor_reduce(var[:, :], h3(sq[:, :]), AX.X, ALU.add).then_inc(*dve.did(f"var{t}"))
                        v.wait_ge(*act.at(f"std{t}", b))
                        v.reciprocal(rs[:, :], std[:, :]).then_inc(*dve.did(f"rs{t}"))
                        me("rs")
                        v.wait_ge(*(pe.at(f"T{t - 1}", b) if t else pe.at("T3", b, 1)))
                        for hh in range(2):
                            last = v.tensor_tensor(h3(zn[:, hh * HALF:(hh + 1) * HALF]), h3(ps[4 + hh][:, 0:HALF]),
                                                   rs[:, hh * HP:(hh + 1) * HP].unsqueeze(2).to_broadcast([P, HP, E1]), ALU.mult)
                        last.then_inc(*dve.did(f"zn{t}"))
                        v.wait_ge(*pool.at(f"b{t}", b))
                        v.wait_ge(*pe.at(f"q{t}", b))
                        for p0, n in ((0, 4), (4, 2)):
                            dst = zn[:, :].rearrange("p (a h e) -> p h a e", a=2, e=E1)[:, p0:p0 + n, :, :]
                            last = v.tensor_tensor(dst, dst, ps[6 + p0 // 4][:, 0:n * P].rearrange("p (h a e) -> p h a e", a=2, e=E1),
                                                   ALU.add)
                        last.then_inc(*dve.did(f"zq{t}"))
                        me("zq")
                        for hh in range(2):
                            last = v.bn_stats(st[:, hh, :], zn[:, hh * HALF:(hh + 1) * HALF])
                        last.then_inc(*dve.did(f"stats{t}"))
                        me("stats")
                        v.memset(tick[:, :], 0.0)
                        v.bn_aggr(mv[:, :], st[:, :, :]).then_inc(*dve.did(f"aggr{t}"))
                        v.wait_ge(*act.at(f"std2{t}", b))
                        v.reciprocal(rs2[:, :], std2[:, :]).then_inc(*dve.did(f"rs2{t}"))
                        me("rs2")
                        v.tensor_scalar(zn[:, :], zn[:, :], mv[:, 0:1], rs2[:, 0:1], ALU.subtract, ALU.mult)\
                            .then_inc(*dve.did(f"nrm{t}"))
                        v.wait_ge(*pe.at(f"T{t}", b))
                        for c in range(HP):
                            last = v.tensor_scalar(yT[:, c, :], ps[6 + c // 4][:, (c % 4) * P:(c % 4 + 1) * P],
                                                   psc[:, c:c + 1], pbc[:, c:c + 1], ALU.mult, ALU.add)
                        last.then_inc(*dve.did(f"sc{t}"))
                        v.wait_ge(*pe.at(f"y{t}", b))
                        v.tensor_tensor(row(h, b * TB + t), row(h, b * TB + t), OUT, ALU.add).then_inc(*dve.did(f"res{t}"))

            @block.scalar
            def _(a):
                act.open(a)
                a.wait_ge(loaded, 160)
                a.wait_ge(ready, 2)
                with a.Fori(0, B) as b:
                    for t in R:
                        a.wait_ge(*pe.at(f"gate{t}", b))
                        a.wait_ge(*pool.at("y3", b, 1))
                        a.activation(gate[:, t, :, :].rearrange("p c n -> p (c n)"),
                                     ps2[3][:, :, :].rearrange("p a n -> p (a n)")[:, 0:CH], ACT.Gelu_apprx_tanh)\
                            .then_inc(*act.did(f"gate{t}"))
                    for t in R:
                        a.wait_ge(*pe.at(f"Z{t}", b))
                        a.wait_ge(*(dve.at(f"var{t - 1}", b) if t else dve.at("var3", b, 1)))
                        a.activation(sq[:, :].rearrange("p (a n) -> p a n", a=2), ps2[2][:, :, 0:HALF], ACT.Square)\
                            .then_inc(*act.did(f"sq{t}"))
                        a.wait_ge(*dve.at(f"var{t}", b))
                        a.activation(std[:, :], var[:, :], ACT.Sqrt, bias=eps[:, 0:1], scale=1.0 / E1).then_inc(*act.did(f"std{t}"))
                        a.wait_ge(*dve.at(f"aggr{t}", b))
                        a.activation(std2[:, :], mv[:, 1:2], ACT.Sqrt, bias=eps[:, 0:1]).then_inc(*act.did(f"std2{t}"))

            @block.gpsimd
            def _(g):
                pool.open(g)
                g.wait_ge(loaded, 160)
                with g.Fori(0, B) as b:
                    for t in R:
                        g.wait_ge(*dve.at(f"zn{t}", b))
                        g.tensor_tensor(zn[:, :], zn[:, :], gB[:, :], ALU.mult).then_inc(*pool.did(f"g{t}"))
                        g.wait_ge(*pool.at(f"g{t}", b))
                        g.tensor_tensor(zn[:, :], zn[:, :], bB[:, :], ALU.add).then_inc(*pool.did(f"b{t}"))
                        g.wait_ge(*dve.at(f"sc{t}", b))
                        g.wait_ge(*act.at("gate3", b))
                        g.tensor_tensor(yT[:, :, :], yT[:, :, :], gate[:, t, :, :], ALU.mult).then_inc(*pool.did(f"y{t}"))


E2, S2, H2 = 32, 32, 768
SL = E2 * S2
CJ = SL // P
HC = H2 // P
XE = 4
W2C = HC * D + HC
FLOOR = 1e-12


def load_expert(sp, M, ins, r, e):
    sp.dma_start(M["w1"][r][:, :, :], ins["m_w1"][bass.ds(e, 1)].rearrange("a p k n -> (a p) k n")).then_inc(M["w_in"][r], 16)
    sp.dma_start(M["w2"][r][:, :], ins["m_w2"][bass.ds(e, 1)].rearrange("a p n -> (a p) n")).then_inc(M["w_in"][r], 16)
    sp.dma_start(M["b2"][r][:, :], ins["m_b2"][bass.ds(e, 1), :]).then_inc(M["w_in"][r], 16)


def moe_dispatch(nc, M, ins):
    with ExitStack() as ctx:
        sb = lambda n, s, d=F32: ctx.enter_context(nc.sbuf_tensor(n, s, d))
        sem = lambda n: ctx.enter_context(nc.semaphore(n))
        L = ln_buffers(sb, "m_")
        phi, scale = sb("m_phi", [DC, KC, SL]), sb("m_scale", [P, 1])
        ones = sb("m_ones", [DC, P])
        xT = sb("m_xT", [DC, KC, N])
        Ed = [sb(f"m_E{i}", [P, SL]) for i in range(2)]
        dw, cw = sb("m_dw", [P, SL]), sb("m_cw", [P, SL])
        ss, nn, nr = sb("m_ss", [P, TB]), sb("m_nn", [P, TB]), sb("m_nr", [P, TB])
        mx, dm, f = ([sb(f"m_{n}{i}", [P, E2]) for i in range(2)] for n in ("mx", "dm", "f"))
        gm, se, rse, w = sb("m_gm", [P, 1]), sb("m_se", [P, E2]), sb("m_rse", [P, E2]), sb("m_w", [P, E2])
        tot, rtot = sb("m_tot", [P, 1]), sb("m_rtot", [P, 1])
        h, ident, ps, ps2 = M["h"], M["ident"], M["ps"], M["ps2"]
        cT, slT = M["cT"], M["slT"]
        xs = L["xn"]
        R = range(TB)
        loaded, prep, normed = sem("m_loaded"), sem("m_prep"), sem("m_normed")
        skew = lambda now, late: [n for i in range(TB + 1) for n in
                                  ([f"{o}{i}" for o in now] if i < TB else []) + ([f"{o}{i - 1}" for o in late] if i else [])]
        pe = Steps(sem("m_pe"), ["T0", "T1"] + skew(["L"], ["S", "C0", "C1"]))
        act = Steps(sem("m_act"), ["std", "nrm", "xT0", "xT1"] + skew(["E", "ex"], ["cT0", "cT1"]) + [f"sl{j}" for j in range(4)])
        dve = Steps(sem("m_dve"), LN_DVE + ["ss", "nx", "nr", "xs"]
                    + skew(["mx", "sb", "gm", "dm"], ["se", "rse", "w", "tot", "rtot", "f", "dw"]))
        pool = Steps(sem("m_pool"), ["sq"] + [f"cw{t}" for t in R])
        e3 = lambda ap: ap.rearrange("p (e s) -> p e s", s=S2)
        bc = lambda ap: ap.unsqueeze(2).to_broadcast([P, E2, S2])
        logits = ps2[0][:, :, :].rearrange("p a n -> p (a n)")
        sq4 = dw[:, 0:TB * D].rearrange("p (t d) -> p t d", t=TB)

        with nc.Block() as block:
            @block.sync
            def _(sp):
                sp.dma_start(phi[:, :, :], ins["m_phi"].rearrange("(k p) n -> p k n", p=DC)).then_inc(loaded, 16)
                sp.dma_start(scale[:, :], ins["m_scale"].rearrange("(a n) -> a n", a=1).to_broadcast([P, 1])).then_inc(loaded, 16)
                for r in range(XE):
                    load_expert(sp, M, ins, r, r)
                sp.wait_ge(loaded, 32)

            @block.tensor
            def _(t_):
                pe.open(t_)
                t_.wait_ge(prep, 2)
                for half in range(2):
                    for kc in range(KC):
                        last = t_.matmul(ps[half], ones[:, :], Ed[kc][0:DC, half * 512:(half + 1) * 512],
                                         start=(kc == 0), stop=(kc == 1))
                last.then_inc(normed, 1)
                t_.wait_ge(normed, 5)
                with t_.Fori(0, B) as b:
                    for c in range(KC):
                        t_.wait_ge(*dve.at("xs", b))
                        for t in R:
                            last = t_.transpose(ps[c][0:DC, t * P:(t + 1) * P], xs[:, t, c * DC:(c + 1) * DC], ident[:, :])
                        last.then_inc(*pe.did(f"T{c}"))
                    for i in range(TB + 1):
                        if i < TB:
                            t_.wait_ge(*(dve.at(f"sb{i - 1}", b) if i else act.at("xT1", b)))
                            for half in range(2):
                                for kc in range(KC):
                                    last = t_.matmul(ps[half], xT[:, kc, i * P:(i + 1) * P], phi[:, kc, half * 512:(half + 1) * 512],
                                                     start=(kc == 0), stop=(kc == 1))
                            last.then_inc(*pe.did(f"L{i}"))
                        if i:
                            t = i - 1
                            t_.wait_ge(*dve.at(f"dw{t}", b))
                            if t == 0:
                                t_.wait_ge(*act.at("sl3", b, 1))
                            for kc in range(KC):
                                for half in range(2):
                                    last = t_.matmul(ps[2 + 2 * kc + half][0:DC, :], xs[:, t, kc * DC:(kc + 1) * DC],
                                                     dw[:, half * 512:(half + 1) * 512], start=(t == 0), stop=(t == TB - 1),
                                                     skip_group_check=True)
                            last.then_inc(*pe.did(f"S{t}"))
                            for k in range(2):
                                t_.wait_ge(*pool.at(f"cw{t}", b))
                                t_.wait_ge(*(act.at(f"cT{k}{t - 1}", b) if t else act.at(f"cT{k}{TB - 1}", b, 1)))
                                for j in range(4):
                                    last = t_.transpose(ps[6 + k][:, j * P:(j + 1) * P], cw[:, (4 * k + j) * P:(4 * k + j + 1) * P],
                                                        ident[:, :])
                                last.then_inc(*pe.did(f"C{k}{t}"))

            @block.vector
            def _(v):
                dve.open(v)
                v.memset(L["eps"][:, :], LN_EPS)
                v.memset(ones[:, :], 1.0).then_inc(prep, 1)
                v.wait_ge(normed, 3)
                v.tensor_scalar(cw[0:DC, :], cw[0:DC, :], FLOOR, None, ALU.max).then_inc(prep, 1)
                v.wait_ge(prep, 3)
                v.reciprocal(dw[0:DC, :], cw[0:DC, :]).then_inc(prep, 1)
                v.wait_ge(prep, 4)
                v.tensor_scalar(dw[0:DC, :], dw[0:DC, :], scale[0:DC, 0:1], None, ALU.mult).then_inc(prep, 1)
                v.wait_ge(prep, 5)
                for kc in range(KC):
                    v.tensor_tensor(phi[:, kc, :], phi[:, kc, :], dw[0:DC, :], ALU.mult).then_inc(normed, 1)
                v.wait_ge(normed, 5)
                with v.Fori(0, B) as b:
                    ln_dve(v, L, h, b, dve, act, pe)
                    v.wait_ge(*pool.at("sq", b))
                    v.tensor_reduce(ss[:, :], sq4, AX.X, ALU.add).then_inc(*dve.did("ss"))
                    v.wait_ge(*act.at("nrm", b))
                    v.tensor_scalar(nn[:, :], nn[:, :], FLOOR, None, ALU.max).then_inc(*dve.did("nx"))
                    v.wait_ge(*dve.at("nx", b))
                    v.reciprocal(nr[:, :], nn[:, :]).then_inc(*dve.did("nr"))
                    v.wait_ge(*dve.at("nr", b))
                    for t in R:
                        last = v.tensor_scalar(xs[:, t, :], xs[:, t, :], nr[:, t:t + 1], None, ALU.mult)
                    last.then_inc(*dve.did("xs"))
                    for i in range(TB + 1):
                        if i < TB:
                            q = i % 2
                            v.wait_ge(*pe.at(f"L{i}", b))
                            v.tensor_reduce(mx[q][:, :], e3(logits), AX.X, ALU.max).then_inc(*dve.did(f"mx{i}"))
                            v.wait_ge(*dve.at(f"mx{i}", b))
                            v.wait_ge(*pool.at(f"cw{(i - 2) % TB}", b, 1 if i < 2 else 0))
                            v.tensor_tensor(e3(Ed[q][:, :]), e3(logits), bc(mx[q][:, :]), ALU.subtract).then_inc(*dve.did(f"sb{i}"))
                            v.tensor_reduce(gm[:, :], mx[q][:, :], AX.X, ALU.max).then_inc(*dve.did(f"gm{i}"))
                            v.wait_ge(*dve.at(f"gm{i}", b))
                            v.tensor_scalar(dm[q][:, :], mx[q][:, :], gm[:, 0:1], None, ALU.subtract).then_inc(*dve.did(f"dm{i}"))
                        if i:
                            t, q = i - 1, (i - 1) % 2
                            me = lambda n: v.wait_ge(*dve.at(f"{n}{t}", b))
                            v.wait_ge(*act.at(f"ex{t}", b))
                            v.tensor_reduce(se[:, :], e3(Ed[q][:, :]), AX.X, ALU.add).then_inc(*dve.did(f"se{t}"))
                            me("se")
                            v.reciprocal(rse[:, :], se[:, :]).then_inc(*dve.did(f"rse{t}"))
                            v.tensor_tensor(w[:, :], se[:, :], dm[q][:, :], ALU.mult).then_inc(*dve.did(f"w{t}"))
                            me("w")
                            v.tensor_reduce(tot[:, :], w[:, :], AX.X, ALU.add).then_inc(*dve.did(f"tot{t}"))
                            me("tot")
                            v.reciprocal(rtot[:, :], tot[:, :]).then_inc(*dve.did(f"rtot{t}"))
                            me("rtot")
                            v.tensor_scalar(f[q][:, :], dm[q][:, :], rtot[:, 0:1], None, ALU.mult).then_inc(*dve.did(f"f{t}"))
                            v.wait_ge(*(pe.at(f"S{t - 1}", b) if t else pe.at("S3", b, 1)))
                            v.tensor_tensor(e3(dw[:, :]), e3(Ed[q][:, :]), bc(rse[:, :]), ALU.mult).then_inc(*dve.did(f"dw{t}"))

            @block.scalar
            def _(a):
                act.open(a)
                a.wait_ge(loaded, 32)
                for kc in range(KC):
                    last = a.activation(Ed[kc][0:DC, :], phi[:, kc, :], ACT.Square)
                last.then_inc(prep, 1)
                a.wait_ge(normed, 1)
                for half in range(2):
                    a.activation(cw[0:DC, half * 512:(half + 1) * 512], ps[half][0:DC, :], ACT.Sqrt).then_inc(normed, 1)
                a.wait_ge(normed, 5)
                with a.Fori(0, B) as b:
                    ln_std(a, L, b, dve, act)
                    a.wait_ge(*dve.at("ss", b))
                    a.activation(nn[:, :], ss[:, :], ACT.Sqrt).then_inc(*act.did("nrm"))
                    for c in range(KC):
                        a.wait_ge(*pe.at(f"T{c}", b))
                        a.activation(xT[:, c, :], ps[c][0:DC, :], ACT.Copy).then_inc(*act.did(f"xT{c}"))
                    for i in range(TB + 1):
                        if i < TB:
                            q = i % 2
                            a.wait_ge(*dve.at(f"sb{i}", b))
                            a.activation(Ed[q][:, :], Ed[q][:, :], ACT.Exp).then_inc(*act.did(f"E{i}"))
                            a.wait_ge(*dve.at(f"dm{i}", b))
                            a.activation(dm[q][:, :], dm[q][:, :], ACT.Exp).then_inc(*act.did(f"ex{i}"))
                        if i:
                            for k in range(2):
                                a.wait_ge(*pe.at(f"C{k}{i - 1}", b))
                                a.activation(cT[:, bass.ds(b * TB + i - 1, 1), 4 * k:4 * k + 4, :].rearrange("p a c n -> p (a c n)"),
                                             ps[6 + k], ACT.Copy).then_inc(*act.did(f"cT{k}{i - 1}"))
                    for kc in range(KC):
                        for half in range(2):
                            a.activation(slT[:, kc, 16 * half:16 * half + 16, bass.ds(b * S2, S2)],
                                         e3(ps[2 + 2 * kc + half][0:DC, :]), ACT.Copy).then_inc(*act.did(f"sl{2 * kc + half}"))

            @block.gpsimd
            def _(g):
                pool.open(g)
                with g.Fori(0, B) as b:
                    g.wait_ge(*dve.at("xn3", b))
                    g.wait_ge(*pe.at("S3", b, 1))
                    g.tensor_tensor(sq4, L["xn"][:, :, :], L["xn"][:, :, :], ALU.mult).then_inc(*pool.did("sq"))
                    for t in R:
                        g.wait_ge(*dve.at(f"f{t}", b))
                        g.wait_ge(*(pe.at(f"C1{t - 1}", b) if t else pe.at("C13", b, 1)))
                        g.tensor_tensor(e3(cw[:, :]), e3(Ed[t % 2][:, :]), bc(f[t % 2][:, :]), ALU.mult).then_inc(*pool.did(f"cw{t}"))


def moe_experts(nc, M, ins):
    with ExitStack() as ctx:
        sb = lambda n, s, d=F32: ctx.enter_context(nc.sbuf_tensor(n, s, d))
        sem = lambda n: ctx.enter_context(nc.semaphore(n))
        gT = [sb(f"x_g{i}", [P, HC, P]) for i in range(2)]
        eo = [sb(f"x_eo{r}", [P, D]) for r in range(XE)]
        ones = sb("x_ones", [1, P])
        ps, ps2, slT, eo_all = M["ps"], M["ps2"], M["slT"], M["eo_all"]
        w1, w2, b2, w_in = M["w1"], M["w2"], M["b2"], M["w_in"]
        prep = sem("x_prep")
        moved = [sem(f"x_moved{r}") for r in range(XE)]
        R = range(XE)
        pe = Steps(sem("x_pe"), ["H0"] + [n for r in range(1, XE) for n in (f"H{r}", f"E{r - 1}")] + [f"E{XE - 1}"])
        act = Steps(sem("x_act"), [f"G{r}{k}" for r in R for k in range(2)])
        dve = Steps(sem("x_dve"), [f"c{r}" for r in R])
        TURNS = E2 // XE

        def move(sp, q, r):
            sp.wait_ge(*dve.at(f"c{r}", q))
            for b in range(B):
                sp.dma_start(eo_all[r * S2:(r + 1) * S2, b, bass.ds(q, 1), :].rearrange("p a n -> p (a n)"),
                             eo[r][b * S2:(b + 1) * S2, :]).then_inc(moved[r], 16)

        with nc.Block() as block:
            @block.sync
            def _(sp):
                for r in R:
                    sp.sem_inc(moved[r], 1)
                with sp.Fori(0, TURNS - 1) as q:
                    for r in R:
                        sp.wait_ge(*pe.at(f"E{r}", q))
                        load_expert(sp, M, ins, r, q * XE + XE + r)
                        move(sp, q, r)
                for r in R:
                    move(sp, TURNS - 1, r)
                for r in R:
                    sp.wait_ge(moved[r], 16 * B * TURNS + 1)

            @block.tensor
            def _(t_):
                pe.open(t_)
                t_.wait_ge(prep, 1)
                with t_.Fori(0, TURNS) as q:
                    for i in range(XE + 1):
                        if i < XE:
                            t_.wait_ge(w_in[i], q * 48 + 48)
                            t_.wait_ge(*(act.at(f"G{i - 2}1", q) if i >= 2 else act.at(f"G{XE - 2 + i}1", q, 1)))
                            for c in range(HC):
                                for kc in range(KC):
                                    last = t_.matmul(ps[2 * (i % 2) + c // 3][:, (c % 3) * P:(c % 3 + 1) * P],
                                                     w1[i][:, kc, c * P:(c + 1) * P],
                                                     slT[:, kc, bass.ds(q * XE + i, 1), :].rearrange("p a n -> p (a n)"),
                                                     start=(kc == 0), stop=(kc == 1))
                            last.then_inc(*pe.did(f"H{i}"))
                        if i:
                            r = i - 1
                            bank = ps[4 + r % 2][:, 0:D]
                            t_.wait_ge(*(dve.at(f"c{r - 2}", q) if r >= 2 else dve.at(f"c{XE - 2 + r}", q, 1)))
                            t_.matmul(bank, ones[:, :], b2[r][:, :], start=True, stop=False)
                            t_.wait_ge(*act.at(f"G{r}1", q))
                            for c in range(HC):
                                last = t_.matmul(bank, gT[r % 2][:, c, :], w2[r][:, c * D:(c + 1) * D], start=False,
                                                 stop=(c == HC - 1))
                            last.then_inc(*pe.did(f"E{r}"))

            @block.scalar
            def _(a):
                act.open(a)
                with a.Fori(0, TURNS) as q:
                    for r in R:
                        a.wait_ge(*pe.at(f"H{r}", q))
                        for c in range(HC):
                            last = a.activation(gT[r % 2][:, c, :], ps[2 * (r % 2) + c // 3][:, (c % 3) * P:(c % 3 + 1) * P],
                                                ACT.Gelu, bias=w2[r][:, HC * D + c:HC * D + c + 1])
                            if c % 3 == 2:
                                last.then_inc(*act.did(f"G{r}{c // 3}"))

            @block.vector
            def _(v):
                dve.open(v)
                v.memset(ones[:, :], 1.0).then_inc(prep, 1)
                with v.Fori(0, TURNS) as q:
                    for r in R:
                        v.wait_ge(*pe.at(f"E{r}", q))
                        v.wait_ge(moved[r], q * (16 * B) + 1)
                        v.tensor_copy(eo[r][:, :], ps[4 + r % 2][:, 0:D]).then_inc(*dve.did(f"c{r}"))


def moe_combine(nc, M, ins, out):
    with ExitStack() as ctx:
        sb = lambda n, s, d=F32: ctx.enter_context(nc.sbuf_tensor(n, s, d))
        sem = lambda n: ctx.enter_context(nc.semaphore(n))
        cb = [sb(f"y_c{i}", [P, CJ, P]) for i in range(2)]
        h, ps, cT, eo_all = M["h"], M["ps"], M["cT"], M["eo_all"]
        R = range(TB)
        pe = Steps(sem("y_pe"), [f"y{t}" for t in R])
        act = Steps(sem("y_act"), [f"c{t}" for t in R])
        dve = Steps(sem("y_dve"), [f"add{t}" for t in R])
        stored = sem("y_stored")

        with nc.Block() as block:
            @block.sync
            def _(sp):
                with sp.Fori(0, B) as b:
                    sp.wait_ge(*dve.at(f"add{TB - 1}", b))
                    sp.dma_start(out[bass.ds(b, 1)].rearrange("a (t p) d -> p (a t) d", p=P), rows(h, b * TB, TB)).then_inc(stored, 16)
                sp.wait_ge(stored, 16 * B)

            @block.scalar
            def _(a):
                act.open(a)
                with a.Fori(0, B) as b:
                    for t in R:
                        a.wait_ge(*(pe.at(f"y{t - 2}", b) if t >= 2 else pe.at(f"y{TB - 2 + t}", b, 1)))
                        a.activation(cb[t % 2][:, :, :].rearrange("p c n -> p (c n)"),
                                     cT[:, bass.ds(b * TB + t, 1), :, :].rearrange("p a c n -> p (a c n)"), ACT.Copy)\
                            .then_inc(*act.did(f"c{t}"))

            @block.tensor
            def _(t_):
                pe.open(t_)
                with t_.Fori(0, B) as b:
                    for t in R:
                        t_.wait_ge(*act.at(f"c{t}", b))
                        t_.wait_ge(*(dve.at(f"add{t - 2}", b) if t >= 2 else dve.at(f"add{TB - 2 + t}", b, 1)))
                        for c in range(CJ):
                            last = t_.matmul(ps[t % 2][:, 0:D], cb[t % 2][:, c, :],
                                             eo_all[:, bass.ds(b, 1), c, :].rearrange("p a n -> p (a n)"),
                                             start=(c == 0), stop=(c == CJ - 1))
                        last.then_inc(*pe.did(f"y{t}"))

            @block.vector
            def _(v):
                dve.open(v)
                with v.Fori(0, B) as b:
                    for t in R:
                        v.wait_ge(*pe.at(f"y{t}", b))
                        v.tensor_tensor(row(h, b * TB + t), row(h, b * TB + t), ps[t % 2][:, 0:D], ALU.add)\
                            .then_inc(*dve.did(f"add{t}"))


def soft_experts(nc, M, ins, out):
    with ExitStack() as ctx:
        sb = lambda n, s, d=F32: ctx.enter_context(nc.sbuf_tensor(n, s, d))
        M["cT"], M["slT"] = sb("cT", [P, TILES, CJ, P]), sb("slT", [DC, KC, E2, P])
        M["w1"] = [sb(f"w1_{r}", [DC, KC, H2]) for r in range(XE)]
        M["w2"] = [sb(f"w2_{r}", [P, W2C]) for r in range(XE)]
        M["b2"] = [sb(f"b2_{r}", [1, D]) for r in range(XE)]
        M["w_in"] = [ctx.enter_context(nc.semaphore(f"w_in{r}")) for r in range(XE)]
        moe_dispatch(nc, M, ins)
        M["eo_all"] = sb("eo_all", [P, B, CJ, D])
        moe_experts(nc, M, ins)
        moe_combine(nc, M, ins, out)


def program(nc, ins, out):
    with ExitStack() as ctx:
        sb = lambda n, s, d=F32: ctx.enter_context(nc.sbuf_tensor(n, s, d))
        M = {"h": sb("h", [P, TILES, D]), "ident": sb("ident", [P, P]), "pair": sb("pair", [P, P]),
             "blk": sb("blk", [P, P])}
        bank = [ctx.enter_context(nc.psum_tensor(f"bank{i}", [P, 2, 512], F32)) for i in range(4)]
        M["ps2"] = bank
        M["ps"] = [bank[i // 2][:, i % 2, :] for i in range(8)]
        embed(nc, M, ins)
        with ExitStack() as c1:
            M["V1"] = c1.enter_context(nc.sbuf_tensor("V1", [P, TILES, HA, VP], F32))
            M["qk_d"] = nc.dram_tensor("qk_d", (B, QUADS, 2, SPLIT, 4 * DH, N), BF16, kind="Internal").ap()
            qkv(nc, M, ins)
            attention(nc, M, ins)
        switch_ffn(nc, M, ins)
        for n, s_ in (("qk1_d", (TILES, 2, P, HP, P)), ("c_d", (B, 2, N, CL)), ("g_d", (B, 2, N, HALF)),
                      ("W_d", (STEPS // SPT, P, HP, B, E1)), ("B_d", (STEPS // SPT, P, HALF)), ("xT_d", (B, DC, KC, N))):
            M[n] = nc.dram_tensor(n, s_, F32, kind="Internal").ap()
        with ExitStack() as c1:
            M["kT_all"] = c1.enter_context(nc.sbuf_tensor("kT_all", [P, HP, B, N], F32))
            ttt_prepare(nc, M, ins)
            ttt_recur(nc, M, ins)
        ttt_output(nc, M, ins)
        soft_experts(nc, M, ins, out)


def host_constants():
    i = np.arange(P)
    ident = np.eye(P, dtype=np.float32)
    pair = np.zeros((P, P), np.float32)
    pair[i ^ 1, i] = 1.0
    blk = (i[:, None] // 16 == i[None, :] // 16).astype(np.float32)
    spread = np.zeros((E0, CE, 2, R0), np.float32)
    for e in range(E0):
        spread[e, e // 2, e % 2] = 1.0
    rank8 = np.broadcast_to(np.arange(E0, 0, -1, dtype=np.float32), (P, TB, E0)).reshape(P, TB * E0)
    s_, t_ = i[:, None], i[None, :]
    same = ((s_ // MB == t_ // MB) & (s_ <= t_)).astype(np.float32)
    prev = (s_ // MB < t_ // MB).astype(np.float32)
    inv = np.broadcast_to((np.float32(1.0) / np.arange(1, MB + 1, dtype=np.float32)), (P, SPT, MB)).reshape(P, P)
    freq = (1.0 / np.float32(10000.0) ** (np.arange(0, E1, 2, dtype=np.float32) / np.float32(E1))).astype(np.float32)
    ang = np.arange(N, dtype=np.float32)[None, :] * freq[:, None]
    c, s = np.repeat(np.cos(ang), 2, 0), np.repeat(np.sin(ang), 2, 0)
    s[0::2] *= -1
    rope = np.stack([np.tile(c, (2, 1)), np.tile(s, (2, 1))], 1).astype(np.float32)
    return {"c_same": same, "c_prev": prev, "c_inv": inv, "c_rope": rope, "c_spread": spread.reshape(E0, CE * P), "c_rank8": rank8, "c_ident": ident, "c_pair": pair, "c_blk": blk}


def layout(inputs):
    g = {k: np.asarray(v) for k, v in inputs.items()}
    kv = g["L0_attn_Wkv"].reshape(HA, 2, DH, D)
    a = {
        "x": g["x"], "tune_ids": g["L0_tok_tune_ids"], "base_weight": g["L0_tok_base_weight"],
        "train_weight": g["L0_tok_train_weight"],
        "WqT": g["L0_attn_Wq"].T, "WkT": kv[:, 0].reshape(D, D).T, "WvT": kv[:, 1].reshape(D, D).T,
        "WprojT": g["L0_attn_Wproj"].T,
        "enc_w": g["L0_ffn_enc_w"], "enc_b": g["L0_ffn_enc_b"], "sw_w": g["L0_ffn_sw_w"], "sw_b": g["L0_ffn_sw_b"],
        "f_w1": g["L0_ffn_w1"].transpose(1, 0, 2).reshape(D, E0 * R0), "f_b1": g["L0_ffn_b1"].reshape(CE, P).T,
        "f_w2": g["L0_ffn_w2"].reshape(E0 * R0, D), "f_b2": g["L0_ffn_b2"],
    }
    halves = lambda w: w.reshape(-1, 2, HP, E1)
    chan = lambda w: halves(w).transpose(1, 3, 2, 0).reshape(P, HP, -1)
    a.update({
        "t_wq": halves(g["L1_attn_wq"]).transpose(0, 2, 1, 3).reshape(D, CH), "t_wv": g["L1_attn_wv"],
        "t_wg": g["L1_attn_wg"], "t_wo": g["L1_attn_wo"], "t_lrw": g["L1_attn_lr_w"].T, "t_lrb": g["L1_attn_lr_b"],
        "t_cwq": chan(g["L1_attn_conv_q_w"]), "t_cwk": chan(g["L1_attn_conv_k_w"]),
        "t_cbq": chan(g["L1_attn_conv_q_b"][None])[:, :, 0], "t_cbk": chan(g["L1_attn_conv_k_b"][None])[:, :, 0],
        "t_g": g["L1_attn_ttt_norm_scale"].reshape(CH), "t_b": g["L1_attn_ttt_norm_bias"].reshape(CH),
        "t_idx": g["L1_attn_learnable_token_idx"], "t_idx8": np.tile(g["L1_attn_learnable_token_idx"], SPT),
        "t_ps": g["L1_attn_post_norm_scale"].reshape(HP, P).T, "t_pb": g["L1_attn_post_norm_bias"].reshape(HP, P).T,
        "t_W1": g["L1_attn_W1"].reshape(2, HP, E1, E1).transpose(0, 2, 1, 3).reshape(P, HALF),
        "t_b1": g["L1_attn_b1"].reshape(CH),
    })
    up = lambda w, p: w.reshape(E2, -1, p, w.shape[-1]).transpose(0, 2, 1, 3)
    b1 = g["L1_ffn_b1"].reshape(E2, HC, P).transpose(0, 2, 1)
    a.update({
        "m_phi": g["L1_ffn_phi"].reshape(D, SL), "m_scale": g["L1_ffn_scale"], "m_w1": up(g["L1_ffn_w1"], DC),
        "m_w2": np.concatenate([up(g["L1_ffn_w2"], P).reshape(E2, P, HC * D), b1], axis=2), "m_b2": g["L1_ffn_b2"],
    })
    a.update(host_constants())
    return {k: np.ascontiguousarray(v) for k, v in a.items()}


def kernel(**inputs):
    import concourse.bacc as bacc
    from concourse.bass_utils import run_bass_kernel_spmd

    nc = bacc.Bacc("TRN2", target_bir_lowering=False, num_devices=1)
    arrays = {f"in_{k}": v for k, v in layout(inputs).items()}
    ins = {k[3:]: nc.dram_tensor(k, v.shape, mybir.dt.from_np(v.dtype), kind="ExternalInput").ap()
           for k, v in arrays.items()}
    out = nc.dram_tensor("out_0", (B, N, D), F32, kind="ExternalOutput").ap()
    program(nc, ins, out)
    r = run_bass_kernel_spmd(nc, [arrays], core_ids=[0])
    return r.results[0]["out_0"]
```

```python
from contextlib import ExitStack

import numpy as np

import concourse.bass as bass
from concourse import mybir

F32 = mybir.dt.float32
BF16 = mybir.dt.bfloat16
I32 = mybir.dt.int32
U32 = mybir.dt.uint32
ALU = mybir.AluOpType
ACT = mybir.ActivationFunctionType
AX = mybir.AxisListType

P = 128
B, N, D = 4, 512, 192
TILES = B * N // P
TB = N // P
KC, DC = 2, 96
LN_EPS = 1e-5
FLOOR = 1e-12

HA, DH = 12, 16
VP = 32
QUADS = HA // 4
SPLIT = 3
PAIRS = [(0, 0), (0, 1), (1, 0), (0, 2), (2, 0), (1, 1)]
MASK_ROW = len(PAIRS) * DH
MAX_ROW = MASK_ROW + 1
NEG = -3.0e38


class Steps:

    def __init__(self, sem, names):
        self.sem, self.names, self.k, self.pos = sem, list(names), len(names), 0
        assert len(set(self.names)) == self.k

    def open(self, eng):
        eng.sem_inc(self.sem, self.k)

    def did(self, name):
        assert self.names[self.pos % self.k] == name, (name, self.names[self.pos % self.k])
        self.pos += 1
        return self.sem, 1

    def at(self, name, turn=0, back=0):
        return self.sem, turn * self.k + (self.k * (1 - back) + self.names.index(name) + 1)


def row(ap, i):
    return ap[:, bass.ds(i, 1), :].rearrange("p a n -> p (a n)")


def rows(ap, i, n):
    return ap[:, bass.ds(i, n), :]


def embed(nc, M, ins):
    NT = ins["tune_ids"].shape[0]
    with ExitStack() as ctx:
        sb = lambda n, s, d=F32: ctx.enter_context(nc.sbuf_tensor(n, s, d))
        sem = lambda n: ctx.enter_context(nc.semaphore(n))
        ids16, ids16f = sb("ids16", [TILES, P], I32), sb("ids16f", [TILES, P])
        tune_i, tune_f = sb("tune_i", [P, NT], I32), sb("tune_f", [P, NT])
        rank_i, rank_f = sb("rank_i", [P, NT], I32), sb("rank_f", [P, NT])
        ids_f, ids_u = sb("ids_f", [P, TILES]), sb("ids_u", [P, TILES], U32)
        hit = sb("hit", [P, TILES, NT])
        best, none = sb("best", [P, TILES]), sb("none", [P, TILES])
        tuned_u = sb("tuned_u", [P, TILES], U32)
        h, ident, psT = M["h"], M["ident"], M["ps"][0]
        loaded, consts, gathered, laid = sem("e_loaded"), sem("e_consts"), sem("e_gathered"), sem("e_laid")
        dve = Steps(sem("e_dve"), ["idsf", "ids", "tune", "rank", "hits", "best", "none", "tuned"])
        turned, ranked = sem("e_turned"), sem("e_ranked")

        with nc.Block() as block:
            @block.sync
            def _(sp):
                sp.dma_start(ids16[:, :], ins["x"].rearrange("b (t p) -> (b t) p", p=P)).then_inc(loaded, 16)
                sp.dma_start(tune_i[:, :], ins["tune_ids"].rearrange("(a n) -> a n", a=1).to_broadcast([P, NT]))\
                    .then_inc(loaded, 16)
                sp.dma_start(M["ident"][:, :], ins["c_ident"]).then_inc(consts, 16)
                sp.dma_start(M["pair"][:, :], ins["c_pair"]).then_inc(consts, 16)
                sp.dma_start(M["blk"][:, :], ins["c_blk"]).then_inc(consts, 16)
                sp.wait_ge(consts, 48)

            @block.tensor
            def _(pe):
                pe.wait_ge(consts, 48)
                pe.wait_ge(*dve.at("idsf"))
                pe.transpose(psT[:, 0:TILES], ids16f[:, :], ident[0:TILES, 0:TILES]).then_inc(turned, 1)

            @block.vector
            def _(v):
                dve.open(v)
                v.wait_ge(loaded, 32)
                v.tensor_copy(ids16f[:, :], ids16[:, :]).then_inc(*dve.did("idsf"))
                v.wait_ge(turned, 1)
                v.tensor_copy(ids_f[:, :], psT[:, 0:TILES])
                v.tensor_copy(ids_u[:, :], psT[:, 0:TILES]).then_inc(*dve.did("ids"))
                v.tensor_copy(tune_f[:, :], tune_i[:, :]).then_inc(*dve.did("tune"))
                v.wait_ge(ranked, 1)
                v.tensor_copy(rank_f[:, :], rank_i[:, :]).then_inc(*dve.did("rank"))
                v.wait_ge(*dve.at("rank"))
                for t in range(TILES):
                    last = v.scalar_tensor_tensor(hit[:, t, :], tune_f[:, :], ids_f[:, t:t + 1], rank_f[:, :],
                                                  ALU.is_equal, ALU.mult)
                last.then_inc(*dve.did("hits"))
                v.wait_ge(*dve.at("hits"))
                v.tensor_reduce(best[:, :], hit[:, :, :], AX.X, ALU.max).then_inc(*dve.did("best"))
                v.wait_ge(*dve.at("best"))
                v.tensor_scalar(none[:, :], best[:, :], 0.0, 70000.0, ALU.is_equal, ALU.mult)\
                    .then_inc(*dve.did("none"))
                v.wait_ge(*dve.at("none"))
                v.scalar_tensor_tensor(tuned_u[:, :], best[:, :], 1.0, none[:, :], ALU.subtract, ALU.add,)\
                    .then_inc(*dve.did("tuned"))

            @block.gpsimd
            def _(g):
                g.iota(rank_i[:, :], pattern=[[1, NT]], base=1, channel_multiplier=0).then_inc(ranked, 1)
                g.wait_ge(*dve.at("ids"))
                for t in range(TILES):
                    g.indirect_dma_start(out=h[:, t, :], out_offset=None, in_=ins["base_weight"],
                                         in_offset=bass.IndirectOffsetOnAxis(ap=ids_u[:, t:t + 1], axis=0))\
                        .then_inc(gathered, 16)
                g.wait_ge(gathered, 16 * TILES)
                g.wait_ge(*dve.at("tuned"))
                for t in range(TILES):
                    g.indirect_dma_start(out=h[:, t, :], out_offset=None, in_=ins["train_weight"],
                                         in_offset=bass.IndirectOffsetOnAxis(ap=tuned_u[:, t:t + 1], axis=0),
                                         bounds_check=NT - 1, oob_is_err=False).then_inc(laid, 16)
                g.wait_ge(laid, 16 * TILES)


LN_DVE = ["stats", "aggr", "rstd", "xn0", "xn1", "xn2", "xn3"]


def ln_buffers(sb, pre=""):
    return {"stats": sb(pre + "ln_stats", [P, TB, 6]), "mv": sb(pre + "ln_mv", [P, TB, 2]), "std": sb(pre + "ln_std", [P, TB]),
            "rstd": sb(pre + "ln_rstd", [P, TB]), "xn": sb(pre + "ln_xn", [P, TB, D]), "eps": sb(pre + "ln_eps", [P, 1]),
            "gate": sb(pre + "ln_gate", [P, 1])}


def ln_dve(v, L, h, b, dve, act, pe):
    v.wait_ge(*dve.at("xn3", b, 1))
    for t in range(TB):
        last = v.bn_stats(L["stats"][:, t, :], row(h, b * TB + t))
    last.then_inc(*dve.did("stats"))
    v.wait_ge(*dve.at("stats", b))
    v.memset(L["gate"][:, :], 0.0)
    for t in range(TB):
        last = v.bn_aggr(L["mv"][:, t, :], L["stats"][:, t, :])
    last.then_inc(*dve.did("aggr"))
    v.wait_ge(*act.at("std", b))
    v.reciprocal(L["rstd"][:, :], L["std"][:, :]).then_inc(*dve.did("rstd"))
    v.wait_ge(*dve.at("rstd", b))
    v.wait_ge(*pe.at("T1", b, 1))
    for t in range(TB):
        v.tensor_scalar(L["xn"][:, t, :], row(h, b * TB + t), L["mv"][:, t, 0:1], L["rstd"][:, t:t + 1],
                        ALU.subtract, ALU.mult).then_inc(*dve.did(f"xn{t}"))


def ln_std(a, L, b, dve, act):
    a.wait_ge(*dve.at("aggr", b))
    a.activation(L["std"][:, :], L["mv"][:, :, 1], ACT.Sqrt, bias=L["eps"][:, 0:1]).then_inc(*act.did("std"))


def ln_turn(t_, L, ident, banks, b, dve, act, pe):
    for c in range(KC):
        t_.wait_ge(*act.at(f"xT{c}", b, 1))
        for t in range(TB):
            if c == 0:
                t_.wait_ge(*dve.at(f"xn{t}", b))
            last = t_.transpose(banks[c][0:DC, t * P:(t + 1) * P], L["xn"][:, t, c * DC:(c + 1) * DC], ident[:, :])
        last.then_inc(*pe.did(f"T{c}"))


def normalise(nc, M, pre, xn, xT, unit=False):
    with ExitStack() as ctx:
        sb = lambda n, s, d=F32: ctx.enter_context(nc.sbuf_tensor(pre + n, s, d))
        sem = lambda n: ctx.enter_context(nc.semaphore(pre + n))
        stats, mv = sb("stats", [P, TILES, 6]), sb("mv", [P, TILES, 2])
        std, rstd, eps, gate = sb("std", [P, TILES]), sb("rstd", [P, TILES]), sb("eps", [P, 1]), sb("gate", [P, 1])
        sq, ss = (sb("sq", [P, TILES, D]), sb("ss", [P, TILES])) if unit else (None, None)
        h, ident, ps = M["h"], M["ident"], M["ps"]
        ready, scaled, squared, rooted, turned, out_a, out_d = (
            sem(n) for n in ("ready", "scaled", "squared", "rooted", "turned", "out_a", "out_d"))
        SB = range(B)
        of = lambda b: slice(b * TB, (b + 1) * TB)
        scales = B * (2 if unit else 1)

        with nc.Block() as block:
            @block.tensor
            def _(t_):
                for b in SB:
                    t_.wait_ge(scaled, scales - B + b + 1)
                    for c in range(KC):
                        for t in range(TB):
                            last = t_.transpose(ps[2 * b + c][0:DC, t * P:(t + 1) * P], xn[:, b * TB + t, c * DC:(c + 1) * DC],
                                                ident[:, :])
                        last.then_inc(turned, 1)

            @block.vector
            def _(v):
                v.memset(eps[:, :], LN_EPS)
                for t in range(TILES):
                    last = v.bn_stats(stats[:, t, :], h[:, t, :])
                last.then_inc(ready, 1)
                v.wait_ge(ready, 1)
                v.memset(gate[:, :], 0.0)
                for t in range(TILES):
                    last = v.bn_aggr(mv[:, t, :], stats[:, t, :])
                last.then_inc(ready, 1)
                v.wait_ge(rooted, 1)
                v.reciprocal(rstd[:, :], std[:, :]).then_inc(ready, 1)
                v.wait_ge(ready, 3)
                for b in SB:
                    for t in range(b * TB, (b + 1) * TB):
                        last = v.tensor_scalar(xn[:, t, :], h[:, t, :], mv[:, t, 0:1], rstd[:, t:t + 1], ALU.subtract, ALU.mult)
                    last.then_inc(scaled, 1)
                if unit:
                    for b in SB:
                        v.wait_ge(squared, b + 1)
                        last = v.tensor_reduce(ss[:, of(b)], sq[:, of(b), :], AX.X, ALU.add)
                    last.then_inc(ready, 1)
                    v.wait_ge(rooted, 2)
                    v.tensor_scalar(std[:, :], std[:, :], FLOOR, None, ALU.max).then_inc(ready, 1)
                    v.wait_ge(ready, 5)
                    v.reciprocal(rstd[:, :], std[:, :]).then_inc(ready, 1)
                    v.wait_ge(ready, 6)
                    for b in SB:
                        for t in range(b * TB, (b + 1) * TB):
                            last = v.tensor_scalar(xn[:, t, :], xn[:, t, :], rstd[:, t:t + 1], None, ALU.mult)
                        last.then_inc(scaled, 1)
                for b in SB:
                    v.wait_ge(turned, 2 * b + 2)
                    v.tensor_copy(xT[:, 1, b * N:(b + 1) * N], ps[2 * b + 1][0:DC, :]).then_inc(out_d, 1)
                v.wait_ge(out_d, B)

            @block.scalar
            def _(a):
                a.wait_ge(ready, 2)
                a.activation(std[:, :], mv[:, :, 1], ACT.Sqrt, bias=eps[:, 0:1]).then_inc(rooted, 1)
                if unit:
                    for b in SB:
                        a.wait_ge(scaled, b + 1)
                        a.activation(sq[:, of(b), :], xn[:, of(b), :], ACT.Square).then_inc(squared, 1)
                    a.wait_ge(ready, 4)
                    a.activation(std[:, :], ss[:, :], ACT.Sqrt).then_inc(rooted, 1)
                for b in SB:
                    a.wait_ge(turned, 2 * b + 1)
                    a.activation(xT[:, 0, b * N:(b + 1) * N], ps[2 * b][0:DC, :], ACT.Copy).then_inc(out_a, 1)
                a.wait_ge(out_a, B)


def qkv(nc, M, ins):
    with ExitStack() as ctx:
        sb = lambda n, s, d=F32: ctx.enter_context(nc.sbuf_tensor(n, s, d))
        sem = lambda n: ctx.enter_context(nc.semaphore(n))
        L = ln_buffers(sb, "a_")
        w = [sb("wq_a", [DC, KC, D]), sb("wk_a", [DC, KC, D]), sb("wv_a", [DC, KC, D])]
        xT = sb("a_xT", [DC, KC, N])
        parts = sb("qk_parts", [DC, 2, KC, SPLIT, N], BF16)
        rest = sb("qk_rest", [DC, 2, KC, N])
        h, ident, ps, V1 = M["h"], M["ident"], M["ps"], M["V1"]
        loaded, ones, stored = sem("a_loaded"), sem("a_ones"), sem("a_stored")
        WC = [(w_, c) for w_ in range(2) for c in range(KC)]
        dve = Steps(sem("a_dve"), LN_DVE + [f"rest{w_}{c}" for w_, c in WC])
        pe = Steps(sem("a_pe"), ["T0", "T1"] + [f"qk{w_}{c}" for w_, c in WC] + ["v0", "v1"])
        act = Steps(sem("a_act"), ["std", "xT0", "xT1"] + [f"hi{w_}{c}" for w_, c in WC] + ["v0", "v1"]
                    + [f"mid{w_}{c}" for w_, c in WC])
        pool = Steps(sem("a_pool"), [f"lo{w_}{c}" for w_, c in WC])
        qk_d = M["qk_d"]
        PER = 16 * 8

        with nc.Block() as block:
            @block.sync
            def _(sp):
                sp.sem_inc(stored, 1)
                for t, name in zip(w, ("WqT", "WkT", "WvT")):
                    sp.dma_start(t[:, :, :], ins[name].rearrange("(k p) n -> p k n", p=DC)).then_inc(loaded, 16)
                with sp.Fori(0, B) as b:
                    for w_, c in WC:
                        sp.wait_ge(*pool.at(f"lo{w_}{c}", b))
                        for r0, r1, q, d0 in ([(0, 64, 0, 0), (64, 96, 1, 0)], [(0, 32, 1, 32), (32, 96, 2, 0)])[c]:
                            sp.dma_start(
                                qk_d[bass.ds(b, 1), q, w_, :, d0:d0 + r1 - r0, :].rearrange("a s r n -> r (a s) n"),
                                parts[r0:r1, w_, c, :, :]).then_inc(stored, 16)
                sp.wait_ge(stored, PER * B + 1)

            @block.tensor
            def _(t_):
                pe.open(t_)
                t_.wait_ge(loaded, 48)
                with t_.Fori(0, B) as b:
                    ln_turn(t_, L, ident, ps[0:2], b, dve, act, pe)
                    t_.wait_ge(*act.at("xT1", b))
                    for w_, c in WC:
                        bank = ps[2 + 2 * w_ + c]
                        t_.wait_ge(*dve.at(f"rest{w_}{c}", b, 1))
                        for kc in range(KC):
                            last = t_.matmul(bank[0:DC, :], w[w_][:, kc, c * DC:(c + 1) * DC], xT[:, kc, :],
                                             start=(kc == 0), stop=(kc == KC - 1))
                        last.then_inc(*pe.did(f"qk{w_}{c}"))
                    for t in range(TB):
                        if t % 2 == 0:
                            t_.wait_ge(*act.at(f"v{t // 2}", b, 1))
                        for kc in range(KC):
                            last = t_.matmul(ps[6 + t // 2][:, (t % 2) * D:(t % 2 + 1) * D], xT[:, kc, t * P:(t + 1) * P],
                                             w[2][:, kc, :], start=(kc == 0), stop=(kc == KC - 1))
                        if t % 2:
                            last.then_inc(*pe.did(f"v{t // 2}"))

            @block.vector
            def _(v):
                dve.open(v)
                v.memset(L["eps"][:, :], LN_EPS)
                with v.Fori(0, B) as b:
                    ln_dve(v, L, h, b, dve, act, pe)
                    for w_, c in WC:
                        v.wait_ge(*act.at(f"hi{w_}{c}", b))
                        v.wait_ge(*pool.at(f"lo{w_}{c}", b, 1))
                        v.tensor_tensor(rest[:, w_, c, :], ps[2 + 2 * w_ + c][0:DC, :], parts[:, w_, c, 0, :],
                                        ALU.subtract).then_inc(*dve.did(f"rest{w_}{c}"))

            @block.scalar
            def _(a):
                act.open(a)
                with a.Fori(0, B) as b:
                    ln_std(a, L, b, dve, act)
                    for c in range(KC):
                        a.wait_ge(*pe.at(f"T{c}", b))
                        a.wait_ge(*pe.at("v1", b, 1))
                        a.activation(xT[:, c, :], ps[c][0:DC, :], ACT.Copy).then_inc(*act.did(f"xT{c}"))
                    for w_, c in WC:
                        a.wait_ge(*pe.at(f"qk{w_}{c}", b))
                        a.wait_ge(stored, b * PER + 1)
                        a.activation(parts[:, w_, c, 0, :], ps[2 + 2 * w_ + c][0:DC, :], ACT.Copy)\
                            .then_inc(*act.did(f"hi{w_}{c}"))
                    for j in range(2):
                        a.wait_ge(*pe.at(f"v{j}", b))
                        a.wait_ge(ones, 2)
                        a.activation(V1[:, bass.ds(b * TB + 2 * j, 2), :, 0:DH],
                                     ps[6 + j][:, 0:2 * D].rearrange("p (t h d) -> p t h d", t=2, h=HA), ACT.Copy)\
                            .then_inc(*act.did(f"v{j}"))
                    for w_, c in WC:
                        a.wait_ge(*dve.at(f"rest{w_}{c}", b))
                        a.activation(parts[:, w_, c, 1, :], rest[:, w_, c, :], ACT.Copy).then_inc(*act.did(f"mid{w_}{c}"))

            @block.gpsimd
            def _(g):
                pool.open(g)
                g.memset(V1[:, :, :, DH:DH + 1], 1.0).then_inc(ones, 1)
                g.memset(V1[:, :, :, DH + 1:VP], 0.0).then_inc(ones, 1)
                with g.Fori(0, B) as b:
                    for w_, c in WC:
                        g.wait_ge(*act.at(f"mid{w_}{c}", b))
                        g.tensor_tensor(parts[:, w_, c, 2, :], rest[:, w_, c, :], parts[:, w_, c, 1, :], ALU.subtract)\
                            .then_inc(*pool.did(f"lo{w_}{c}"))


def attention(nc, M, ins):
    with ExitStack() as ctx:
        sb = lambda n, s, d=F32: ctx.enter_context(nc.sbuf_tensor(n, s, d))
        sem = lambda n: ctx.enter_context(nc.semaphore(n))
        RA, RB = MASK_ROW + 1, MAX_ROW + 2
        Q = [sb(f"Q{r}", [RB, 4, N], BF16) for r in range(QUADS)]
        K = [sb(f"K{r}", [RB, 4, N], BF16) for r in range(QUADS)]
        PT = [sb(f"PT{r}", [P, 2, N]) for r in range(2)]
        mx = sb("mx", [P, 4, TB])
        mparts, mrest = sb("mparts", [16, 2, P], BF16), sb("mrest", [16, P])
        rec, AO = sb("rec", [P, TB, 4]), sb("AO", [P, TB, D])
        AOT = sb("AOT", [DC, KC, N])
        OT = sb("OT", [P, N])
        Vb = sb("Vb", [P, TB, HA * VP])
        wp = sb("wp", [DC, KC, D])
        h, ident, V1, qk_d = M["h"], M["ident"], M["V1"], M["qk_d"]
        ps = M["ps"]
        AB, STB = M["ps2"][0], [M["ps2"][1], M["ps2"][2]]
        OB, XB = ps[6], ps[7]
        O = XB.rearrange("p (t h e) -> p t h e", t=TB, h=4)
        WHEN = {0: [0, 1], 1: [2], 2: [3, 4], 3: [5], 4: [6, 7]}
        loaded = [sem(f"t_loaded{r}") for r in range(QUADS)]
        consts, rowed = sem("t_consts"), sem("t_rowed")
        UQ = range(QUADS)
        MXS = [f"max{j}" for j in range(8)]
        dve = Steps(sem("t_dve"), [f"{s}/{q}" for q in UQ for s in MXS + ["m0", "m0r", "m1", "rec", "AO"]]
                    + ["res0", "res1", "Vb"])
        act = Steps(sem("t_act"), [f"exp{s}/{q}" for q in UQ for s in list(range(8)) + ["O"]] + ["AOT0", "AOT1"])
        pe = Steps(sem("t_pe"), [x for q in UQ for x in
                                 [y for s in range(8) for y in [f"ST{s}/{q}"] + [f"A{j}/{q}" for j in WHEN.get(s, [])]
                                  + ([f"mxT/{q}"] if s == 5 else []) + ([f"PV{s - 1}/{q}"] if s else [])]
                                 + [f"PV7/{q}", f"Oq/{q}"]] + ["OT0", "OT1", "proj0", "proj1"])
        first_pe, first_dve = sem("t_first_pe"), sem("t_first_dve")
        masks, laid = sem("t_masks"), sem("t_laid")
        NL = 12

        def load(sp, r, b, q):
            for g, pq in enumerate(PAIRS):
                for w_, dst in ((0, Q[r]), (1, K[r])):
                    sp.dma_start(dst[g * DH:(g + 1) * DH, :, :],
                                 qk_d[bass.ds(b, 1), q, w_, pq[w_], :, :].rearrange("a (h d) n -> (a d) h n", d=DH))\
                        .then_inc(loaded[r], 16)

        def max_scores(t_, r, j):
            hd, qt = j // 2, 2 * (j % 2)
            for i in range(2):
                last = t_.matmul(AB[:, i, :], Q[r][0:RA, hd, (qt + i) * P:(qt + i + 1) * P], K[r][0:RA, hd, :],
                                 start=True, stop=True)
            return last

        def take_max(v, j):
            hd, qt = j // 2, 2 * (j % 2)
            return v.tensor_reduce(mx[:, hd, qt:qt + 2], AB[:, :, :], AX.X, ALU.max)

        MXT = AB[0:16, 0, 0:P]

        def neg_max(v, wait, done):
            v.tensor_scalar(mparts[:, 0, :], MXT, -1.0, None, ALU.mult).then_inc(*done("m0"))
            wait("m0")
            v.scalar_tensor_tensor(mrest[:, :], MXT, -1.0, mparts[:, 0, :], ALU.mult, ALU.subtract)\
                .then_inc(*done("m0r"))
            wait("m0r")
            v.tensor_copy(mparts[:, 1, :], mrest[:, :]).then_inc(*done("m1"))

        def store_rows(sp, r):
            for j in range(2):
                sp.dma_start(Q[r][MAX_ROW + j:MAX_ROW + j + 1, :, :].rearrange("a h (t n) -> a (h t) n", t=TB),
                             mparts[:, j, :]).then_inc(rowed, 16)

        with nc.Block() as block:
            @block.sync
            def _(sp):
                sp.dma_start(wp[:, :, :], ins["WprojT"].rearrange("(k p) n -> p k n", p=DC)).then_inc(consts, 16)
                for r in UQ:
                    load(sp, r, 0, r)
                sp.wait_ge(first_dve, 11)
                store_rows(sp, 0)
                with sp.Fori(0, B) as b:
                    for q in UQ:
                        sp.wait_ge(*dve.at(f"m1/{q}", b))
                        store_rows(sp, (q + 1) % 3)
                        sp.wait_ge(*pe.at(f"PV7/{q}", b))
                        load(sp, q, (b + 1) % B, q)
                for r in UQ:
                    sp.wait_ge(loaded[r], 16 * NL * (B + 1))
                sp.wait_ge(rowed, 32 * (QUADS * B + 1))

            @block.tensor
            def _(t_):
                pe.open(t_)
                t_.wait_ge(consts, 16)
                t_.wait_ge(masks, QUADS)
                t_.wait_ge(loaded[0], 16 * NL)
                for j in range(8):
                    if j:
                        t_.wait_ge(first_dve, j)
                    max_scores(t_, 0, j).then_inc(first_pe, 1)
                t_.wait_ge(first_dve, 8)
                t_.transpose(MXT, mx[:, :, :].rearrange("p h t -> p (h t)"), ident[:, :]).then_inc(first_pe, 1)
                with t_.Fori(0, B) as b:
                    for q in UQ:
                        nxt = (q + 1) % 3
                        t_.wait_ge(rowed, b * (32 * QUADS) + 32 * (q + 1))

                        def pv(s):
                            t_.wait_ge(*act.at(f"exp{s}/{q}", b))
                            for i in range(2):
                                hd, kt = s // 2, 2 * (s % 2) + i
                                last = t_.matmul(OB[hd * VP:(hd + 1) * VP, :], Vb[:, kt, (4 * q + hd) * VP:(4 * q + hd + 1) * VP],
                                                 PT[s % 2][:, i, :], start=(kt == 0), stop=(kt == TB - 1))
                            last.then_inc(*pe.did(f"PV{s}/{q}"))

                        for s in range(8):
                            hd, kt = s // 2, 2 * (s % 2)
                            if s >= 2:
                                t_.wait_ge(*act.at(f"exp{s - 2}/{q}", b))
                            elif q:
                                t_.wait_ge(*act.at(f"exp{6 + s}/{q - 1}", b))
                            else:
                                t_.wait_ge(*act.at(f"exp{6 + s}/2", b, 1))
                            for i in range(2):
                                last = t_.matmul(STB[s % 2][:, i, :], K[q][0:RB, hd, (kt + i) * P:(kt + i + 1) * P],
                                                 Q[q][0:RB, hd, :], start=True, stop=True)
                            last.then_inc(*pe.did(f"ST{s}/{q}"))
                            for j in WHEN.get(s, []):
                                if j:
                                    t_.wait_ge(*dve.at(f"max{j - 1}/{q}", b))
                                else:
                                    t_.wait_ge(*dve.at(f"m0r/{(q - 1) % 3}", b, 1 if q == 0 else 0))
                                    t_.wait_ge(loaded[nxt], b * (16 * NL) + 16 * NL * (2 if q == 2 else 1))
                                    if q == 0:
                                        t_.wait_ge(*act.at("AOT1", b, 1))
                                        t_.wait_ge(*dve.at("res1", b, 1))
                                max_scores(t_, nxt, j).then_inc(*pe.did(f"A{j}/{q}"))
                            if s == 5:
                                t_.wait_ge(*dve.at(f"max7/{q}", b))
                                t_.transpose(MXT, mx[:, :, :].rearrange("p h t -> p (h t)"), ident[:, :])\
                                    .then_inc(*pe.did(f"mxT/{q}"))
                            if s:
                                if s == 1 and q == 0:
                                    t_.wait_ge(first_dve, 12)
                                    t_.wait_ge(*dve.at("Vb", b, 1))
                                pv(s - 1)
                        pv(7)
                        t_.wait_ge(*act.at(f"expO/{q}", b))
                        t_.wait_ge(*dve.at("res1", b, 1) if q == 0 else dve.at(f"AO/{q - 1}", b))
                        for t in range(TB):
                            last = t_.transpose(XB[:, t * P:(t + 1) * P], OT[:, t * P:(t + 1) * P], ident[:, :])
                        last.then_inc(*pe.did(f"Oq/{q}"))
                    t_.wait_ge(*dve.at("AO/2", b))
                    for c in range(KC):
                        for t in range(TB):
                            last = t_.transpose(AB[0:DC, c, t * P:(t + 1) * P], AO[:, t, c * DC:(c + 1) * DC], ident[:, :])
                        last.then_inc(*pe.did(f"OT{c}"))
                    t_.wait_ge(*act.at("AOT1", b))
                    for t in range(TB):
                        bank = XB if t < 2 else AB[:, 0, :]
                        for kc in range(KC):
                            last = t_.matmul(bank[:, (t % 2) * D:(t % 2 + 1) * D], AOT[:, kc, t * P:(t + 1) * P],
                                             wp[:, kc, :], start=(kc == 0), stop=(kc == KC - 1))
                        if t % 2:
                            last.then_inc(*pe.did(f"proj{t // 2}"))

            @block.vector
            def _(v):
                dve.open(v)
                def stage_values(b):
                    return v.tensor_copy(Vb[:, :, :], V1[:, bass.ds(b * TB, TB), :, :].rearrange("p t h e -> p t (h e)"))

                for j in range(8):
                    v.wait_ge(first_pe, j + 1)
                    take_max(v, j).then_inc(first_dve, 1)
                v.wait_ge(first_pe, 9)
                neg_max(v, lambda n: v.wait_ge(first_dve, {"m0": 9, "m0r": 10}[n]), lambda n: (first_dve, 1))
                stage_values(0).then_inc(first_dve, 1)
                with v.Fori(0, B) as b:
                    for q in UQ:
                        for j in range(8):
                            if j == 0:
                                v.wait_ge(*pe.at(f"mxT/{(q - 1) % 3}", b, 1 if q == 0 else 0))
                            v.wait_ge(*pe.at(f"A{j}/{q}", b))
                            take_max(v, j).then_inc(*dve.did(f"max{j}/{q}"))
                        v.wait_ge(*pe.at(f"mxT/{q}", b))
                        v.wait_ge(rowed, b * (32 * QUADS) + 32 * (q + 1))
                        neg_max(v, lambda n: v.wait_ge(*dve.at(f"{n}/{q}", b)), lambda n: dve.did(f"{n}/{q}"))
                        v.wait_ge(*pe.at(f"Oq/{q}", b))
                        v.wait_ge(*dve.at(f"AO/{(q - 1) % 3}", b, 1 if q == 0 else 0))
                        v.reciprocal(rec[:, :, :], O[:, :, :, DH]).then_inc(*dve.did(f"rec/{q}"))
                        v.wait_ge(*dve.at(f"rec/{q}", b))
                        if q == 0:
                            v.wait_ge(*pe.at("OT1", b, 1))
                        v.tensor_tensor(AO[:, :, q * 64:(q + 1) * 64].rearrange("p t (h d) -> p t h d", d=DH),
                                        O[:, :, :, 0:DH], rec[:, :, :].unsqueeze(3).to_broadcast([P, TB, 4, DH]),
                                        ALU.mult).then_inc(*dve.did(f"AO/{q}"))
                    for j in range(2):
                        v.wait_ge(*pe.at(f"proj{j}", b))
                        bank = XB if j == 0 else AB[:, 0, :]
                        v.tensor_tensor(rows(h, b * TB + 2 * j, 2), rows(h, b * TB + 2 * j, 2),
                                        bank[:, 0:2 * D].rearrange("p (t n) -> p t n", t=2), ALU.add)\
                            .then_inc(*dve.did(f"res{j}"))
                    stage_values((b + 1) % B).then_inc(*dve.did("Vb"))

            @block.scalar
            def _(a):
                act.open(a)
                with a.Fori(0, B) as b:
                    for q in UQ:
                        for s in range(8):
                            a.wait_ge(*pe.at(f"ST{s}/{q}", b))
                            if s >= 2:
                                a.wait_ge(*pe.at(f"PV{s - 2}/{q}", b))
                            elif q:
                                a.wait_ge(*pe.at(f"PV{6 + s}/{q - 1}", b))
                            else:
                                a.wait_ge(*pe.at(f"PV{6 + s}/2", b, 1))
                            a.activation(PT[s % 2][:, :, :], STB[s % 2][:, :, :], ACT.Exp, scale=DH ** -0.5)\
                                .then_inc(*act.did(f"exp{s}/{q}"))
                        a.wait_ge(*pe.at(f"PV7/{q}", b))
                        a.wait_ge(*pe.at(f"Oq/{(q - 1) % 3}", b, 1 if q == 0 else 0))
                        a.activation(OT[:, :], OB, ACT.Copy).then_inc(*act.did(f"expO/{q}"))
                    for c in range(KC):
                        a.wait_ge(*pe.at(f"OT{c}", b))
                        a.wait_ge(*pe.at("proj1", b, 1))
                        a.activation(AOT[:, c, :], AB[0:DC, c, :], ACT.Copy).then_inc(*act.did(f"AOT{c}"))

            @block.gpsimd
            def _(g):
                for n, r in enumerate(UQ):
                    g.memset(Q[r][MASK_ROW:MASK_ROW + 1, :, :], NEG)
                    g.memset(K[r][MASK_ROW:RB, :, :], 1.0).then_inc(laid, 1)
                    g.wait_ge(laid, n + 1)
                    g.memset(Q[r][MASK_ROW:MASK_ROW + 1, :, 0:1], 0.0)
                    g.memset(K[r][MASK_ROW:MASK_ROW + 1, :, 1:N], 0.0).then_inc(masks, 1)


E0, R0 = 8, 64
CE = E0 * R0 // P


def switch_ffn(nc, M, ins):
    with ExitStack() as ctx:
        sb = lambda n, s, d=F32: ctx.enter_context(nc.sbuf_tensor(n, s, d))
        sem = lambda n: ctx.enter_context(nc.semaphore(n))
        L = ln_buffers(sb, "f_")
        xT = sb("f_xT", [DC, KC, N])
        enc_w, enc_b = sb("enc_w", [DC, KC, R0]), sb("enc_b", [R0, 1])
        sw = sb("sw", [R0 + 1, E0])
        w1, b1 = sb("f_w1", [DC, KC, E0 * R0]), sb("f_b1", [P, CE])
        w2, b2 = sb("f_w2", [P, CE, D]), sb("f_b2", [E0, D])
        spread, rank = sb("f_spread", [E0, CE, P]), sb("f_rank", [P, TB, E0])
        xe = sb("f_xe", [R0 + 1, N])
        top, lg, ex = sb("f_top", [P, TB]), sb("f_lg", [P, TB, E0]), sb("f_ex", [P, TB, E0])
        den, prob = sb("f_den", [P, TB]), sb("f_prob", [P, TB])
        ranked, first, hot = sb("f_ranked", [P, TB, E0]), sb("f_first", [P, TB]), sb("f_hot", [P, TB, E0])
        spreadb = sb("f_spreadb", [E0, CE, P], BF16)
        hotT, hotTb = sb("f_hotT", [E0, N]), sb("f_hotTb", [E0, N], BF16)
        act_h, hid = sb("f_act", [P, 2, N]), sb("f_hid", [P, CE, N])
        h, ident, ps = M["h"], M["ident"], M["ps"]
        loaded, cast = sem("f_loaded"), sem("f_cast")
        dve = Steps(sem("f_dve"), LN_DVE + ["top", "lg", "ranked", "first", "hot", "den", "prob"]
                    + [f"hid{c}" for c in range(CE)] + ["res0", "res1"])
        act = Steps(sem("f_act_s"), ["std", "xT0", "xT1", "xe", "ex", "hotT", "hotTb"] + [f"gelu{c}" for c in range(CE)])
        pe = Steps(sem("f_pe"), ["T0", "T1", "enc", "logits"] + ["hotT"]
                   + [f"{x}{c}" for c in range(CE) for x in ("mask", "h")] + ["y0", "y1"])
        lg_ps = ps[3][:, 0:TB * E0].rearrange("p (t e) -> p t e", t=TB)

        def bc(ap, n):
            return ap.unsqueeze(2).to_broadcast([P, ap.shape[1], n])

        with nc.Block() as block:
            @block.sync
            def _(sp):
                for dst, src in ((enc_w[:, :, :], ins["enc_w"].rearrange("(k p) n -> p k n", p=DC)),
                                 (enc_b[:, :], ins["enc_b"].rearrange("(p a) -> p a", a=1)),
                                 (sw[0:R0, :], ins["sw_w"]), (sw[R0:R0 + 1, :], ins["sw_b"].rearrange("(a e) -> a e", a=1)),
                                 (w1[:, :, :], ins["f_w1"].rearrange("(k p) n -> p k n", p=DC)),
                                 (b1[:, :], ins["f_b1"]), (w2[:, :, :], ins["f_w2"].rearrange("(c p) d -> p c d", p=P)),
                                 (b2[:, :], ins["f_b2"]), (spread[:, :, :], ins["c_spread"].rearrange("e (c p) -> e c p", p=P)),
                                 (rank[:, :, :], ins["c_rank8"].rearrange("p (t e) -> p t e", e=E0))):
                    sp.dma_start(dst, src).then_inc(loaded, 16)
                sp.wait_ge(loaded, 160)

            @block.tensor
            def _(t_):
                pe.open(t_)
                t_.wait_ge(loaded, 160)
                t_.wait_ge(cast, 1)
                with t_.Fori(0, B) as b:
                    t_.wait_ge(*dve.at("res1", b, 1))
                    ln_turn(t_, L, ident, ps[0:2], b, dve, act, pe)
                    t_.wait_ge(*act.at("xT1", b))
                    t_.wait_ge(*act.at("hotTb", b, 1))
                    for kc in range(KC):
                        last = t_.matmul(ps[2][0:R0, :], enc_w[:, kc, :], xT[:, kc, :], start=(kc == 0), stop=(kc == 1))
                    last.then_inc(*pe.did("enc"))
                    t_.wait_ge(*act.at("xe", b))
                    t_.wait_ge(*dve.at("lg", b, 1))
                    for t in range(TB):
                        last = t_.matmul(lg_ps[:, t, :], xe[:, t * P:(t + 1) * P], sw[:, :], start=True, stop=True)
                    last.then_inc(*pe.did("logits"))
                    t_.wait_ge(*dve.at("hot", b))
                    for t in range(TB):
                        last = t_.transpose(ps[2][0:E0, t * P:(t + 1) * P], hot[:, t, :], ident[:, :])
                    last.then_inc(*pe.did("hotT"))
                    t_.wait_ge(*act.at("hotTb", b))
                    for c in range(CE):
                        t_.wait_ge(*dve.at(f"hid{(c - 2) % CE}", b, 1 if c < 2 else 0))
                        t_.matmul(ps[6 + c % 2], spreadb[:, c, :], hotTb[:, :], start=True, stop=True)\
                            .then_inc(*pe.did(f"mask{c}"))
                        for kc in range(KC):
                            last = t_.matmul(ps[4 + c % 2], w1[:, kc, c * P:(c + 1) * P], xT[:, kc, :],
                                             start=(kc == 0), stop=(kc == 1))
                        last.then_inc(*pe.did(f"h{c}"))
                    t_.wait_ge(*dve.at(f"hid{CE - 1}", b))
                    for t in range(TB):
                        y = ps[t // 2][:, (t % 2) * D:(t % 2 + 1) * D]
                        for c in range(CE):
                            t_.matmul(y, hid[:, c, t * P:(t + 1) * P], w2[:, c, :], start=(c == 0), stop=False)
                        last = t_.matmul(y, hotT[:, t * P:(t + 1) * P], b2[:, :], start=False, stop=True)
                        if t % 2:
                            last.then_inc(*pe.did(f"y{t // 2}"))

            @block.vector
            def _(v):
                dve.open(v)
                v.memset(L["eps"][:, :], LN_EPS)
                v.memset(xe[R0:R0 + 1, :], 1.0)
                v.wait_ge(loaded, 160)
                v.tensor_copy(spreadb[:, :, :], spread[:, :, :]).then_inc(cast, 1)
                with v.Fori(0, B) as b:
                    ln_dve(v, L, h, b, dve, act, pe)
                    v.wait_ge(*pe.at("logits", b))
                    v.tensor_reduce(top[:, :], lg_ps, AX.X, ALU.max).then_inc(*dve.did("top"))
                    v.wait_ge(*dve.at("top", b))
                    v.wait_ge(*act.at("ex", b, 1))
                    v.tensor_tensor(lg[:, :, :], lg_ps, bc(top[:, :], E0), ALU.subtract).then_inc(*dve.did("lg"))
                    v.wait_ge(*dve.at("lg", b))
                    v.scalar_tensor_tensor(ranked[:, :, :], lg[:, :, :], 0.0, rank[:, :, :], ALU.is_equal, ALU.mult)\
                        .then_inc(*dve.did("ranked"))
                    v.wait_ge(*dve.at("ranked", b))
                    v.tensor_reduce(first[:, :], ranked[:, :, :], AX.X, ALU.max).then_inc(*dve.did("first"))
                    v.wait_ge(*dve.at("first", b))
                    v.wait_ge(*pe.at("hotT", b, 1))
                    v.tensor_tensor(hot[:, :, :], rank[:, :, :], bc(first[:, :], E0), ALU.is_equal)\
                        .then_inc(*dve.did("hot"))
                    v.wait_ge(*act.at("ex", b))
                    v.wait_ge(*dve.at("res1", b, 1))
                    v.tensor_reduce(den[:, :], ex[:, :, :], AX.X, ALU.add).then_inc(*dve.did("den"))
                    v.wait_ge(*dve.at("den", b))
                    v.reciprocal(prob[:, :], den[:, :]).then_inc(*dve.did("prob"))
                    for c in range(CE):
                        v.wait_ge(*act.at(f"gelu{c}", b))
                        if c == 0:
                            v.wait_ge(*pe.at("y1", b, 1))
                        v.tensor_tensor(hid[:, c, :], ps[6 + c % 2], act_h[:, c % 2, :], ALU.mult)\
                            .then_inc(*dve.did(f"hid{c}"))
                    for j in range(2):
                        v.wait_ge(*pe.at(f"y{j}", b))
                        for t in (2 * j, 2 * j + 1):
                            last = v.scalar_tensor_tensor(row(h, b * TB + t), ps[j][:, (t % 2) * D:(t % 2 + 1) * D],
                                                          prob[:, t:t + 1], row(h, b * TB + t), ALU.mult, ALU.add)
                        last.then_inc(*dve.did(f"res{j}"))

            @block.scalar
            def _(a):
                act.open(a)
                a.wait_ge(loaded, 160)
                with a.Fori(0, B) as b:
                    ln_std(a, L, b, dve, act)
                    for c in range(KC):
                        a.wait_ge(*pe.at(f"T{c}", b))
                        a.activation(xT[:, c, :], ps[c][0:DC, :], ACT.Copy).then_inc(*act.did(f"xT{c}"))
                    a.wait_ge(*pe.at("enc", b))
                    a.wait_ge(*dve.at("xn0", b))
                    a.activation(xe[0:R0, :], ps[2][0:R0, :], ACT.Identity, bias=enc_b[:, 0:1]).then_inc(*act.did("xe"))
                    a.wait_ge(*dve.at("lg", b))
                    a.wait_ge(*dve.at("den", b, 1))
                    a.activation(ex[:, :, :], lg[:, :, :], ACT.Exp).then_inc(*act.did("ex"))
                    a.wait_ge(*pe.at("hotT", b))
                    a.activation(hotT[:, :], ps[2][0:E0, :], ACT.Copy).then_inc(*act.did("hotT"))
                    a.activation(hotTb[:, :], ps[2][0:E0, :], ACT.Copy).then_inc(*act.did("hotTb"))
                    for c in range(CE):
                        a.wait_ge(*pe.at(f"h{c}", b))
                        a.wait_ge(*dve.at(f"hid{(c - 2) % CE}", b, 1 if c < 2 else 0))
                        a.activation(act_h[:, c % 2, :], ps[4 + c % 2], ACT.Gelu, bias=b1[:, c:c + 1])\
                            .then_inc(*act.did(f"gelu{c}"))

            @block.gpsimd
            def _(g):
                g.wait_ge(loaded, 160)


H1, E1, MB, KW = 12, 64, 16, 4
HP = H1 // 2
CH = H1 * E1
HALF = CH // 2
STEPS = N // MB
SPT = P // MB
CL = HALF + 8


def ttt_prepare(nc, M, ins, xT):
    with ExitStack() as ctx:
        sb = lambda n, s, d=F32: ctx.enter_context(nc.sbuf_tensor(n, s, d))
        sem = lambda n: ctx.enter_context(nc.semaphore(n))
        wq, wv = sb("p_wq", [DC, KC, CH]), sb("p_wv", [DC, KC, CH])
        lrw, lrb = sb("p_lrw", [DC, KC, P]), sb("p_lrb", [H1, 1])
        cw, cb = [sb("cw_q", [P, HP, KW]), sb("cw_k", [P, HP, KW])], [sb("cb_q", [P, HP]), sb("cb_k", [P, HP])]
        rope = sb("rope", [P, 2, N])
        gC, bC = sb("gC", [P, HP]), sb("bC", [P, HP])
        XP = sb("XP", [P, 2, KW + N])
        y, r1, r2 = (sb(n, [P, 2, 2, N]) for n in ("cy", "rope_c", "rope_s"))
        qT = sb("p_qT", [P, HP, N])
        tT, rows_ = sb("p_tT", [P, 2, N]), sb("p_rows", [P, TB, 2, CL])
        lrT = sb("p_lr", [P, N])
        ident, pair, ps, kT_all = M["ident"], M["pair"], M["ps"], M["kT_all"]
        loaded, padded, prep = sem("p_loaded"), sem("p_padded"), sem("p_prep")
        kept, kst, qst, cst = sem("p_kept"), sem("p_kstored"), sem("p_qstored"), sem("p_cstored")
        prime_p, prime_a = sem("p_prime_p"), sem("p_prime_a")
        PR = range(HP)
        nxt = lambda i: (i + 1) % HP
        late = lambda i, n, back: [f"{n}{i - back}"] if i >= back else []
        dve = Steps(sem("p_dve"), [n for i in PR for n in
                                   [f"c11{i}", f"c10{i}"] + ([f"s1{i - 1}", f"s0{i - 1}"] if i else [])
                                   + [f"c21{i}", f"c20{i}", f"c31{i}", f"c30{i}"]] + [f"s1{HP - 1}", f"s0{HP - 1}", "lr"])
        act = Steps(sem("p_act"), [n for i in PR for n in [f"XP{nxt(i)}", f"y1{nxt(i)}", f"y0{nxt(i)}"]
                                   + late(i, "tt", 1) + late(i, "rw", 2)] + [f"tt{HP - 1}", f"rw{HP - 2}", "sig", f"rw{HP - 1}"])
        pe = Steps(sem("p_pe"), [n for i in PR for n in [f"x{nxt(i)}", f"r1{i}", f"r0{i}"] + late(i, "V", 1) + late(i, "TR", 2)]
                   + [f"V{HP - 1}", f"TR{HP - 2}", "lr", f"TR{HP - 1}", "lt"])
        pool = Steps(sem("p_pool"), [n for i in PR for n in ([f"z1{i - 1}", f"z0{i - 1}"] if i else []) + [f"c1{i}", f"c0{i}"]]
                     + [f"z1{HP - 1}", f"z0{HP - 1}"])
        LOADS = 16 * 11
        of = lambda b: bass.ds(b * N, N)
        kT = lambda p, b: kT_all[:, p, bass.ds(b, 1), :].rearrange("p a n -> p (a n)")

        with nc.Block() as block:
            @block.sync
            def _(sp):
                for stores in (kst, qst, cst):
                    sp.sem_inc(stores, 1)
                for dst, src in ((wq[:, :, :], ins["t_wq"].rearrange("(k p) n -> p k n", p=DC)),
                                 (cw[1][:, :, :], ins["t_cwk"]), (cw[0][:, :, :], ins["t_cwq"]),
                                 (cb[0][:, :], ins["t_cbq"]), (cb[1][:, :], ins["t_cbk"]),
                                 (rope[:, :, :], ins["c_rope"]),
                                 (wv[:, :, :], ins["t_wv"].rearrange("(k p) n -> p k n", p=DC)),
                                 (lrb[:, :], ins["t_lrb"].rearrange("(n a) -> n a", a=1)),
                                 (gC[:, :], ins["t_gc"]), (bC[:, :], ins["t_bc"])):
                    sp.dma_start(dst, src).then_inc(loaded, 16)
                sp.wait_ge(padded, 3)
                sp.dma_start(lrw[:, :, 0:H1], ins["t_lrw"].rearrange("(k p) n -> p k n", p=DC)).then_inc(loaded, 16)
                sp.dma_start(M["xT_d"], xT[:, :, :]).then_inc(kept, 16)
                with sp.Fori(0, B) as b:
                    for p in PR:
                        sp.wait_ge(*pool.at(f"z0{p}", b))
                        for w_, src, done in ((0, qT[:, p, :], qst), (1, kT(p, b), kst)):
                            sp.dma_start(M["qk1_d"][bass.ds(b * TB, TB), w_, :, p, :].rearrange("t c n -> c t n"),
                                         src.rearrange("c (t n) -> c t n", t=TB)).then_inc(done, 16)
                    sp.wait_ge(*act.at(f"rw{HP - 1}", b))
                    sp.wait_ge(*dve.at("lr", b))
                    for t in range(TB):
                        for hh in range(2):
                            sp.dma_start(M["c_d"][bass.ds(b, 1), hh, t * P:(t + 1) * P, :].rearrange("a k n -> (a k) n"),
                                         rows_[:, t, hh, :]).then_inc(cst, 16)
                sp.wait_ge(kept, 16)
                sp.wait_ge(kst, 16 * HP * B + 1)
                sp.wait_ge(qst, 16 * HP * B + 1)
                sp.wait_ge(cst, 16 * 2 * TB * B + 1)

            @block.tensor
            def _(t_):
                pe.open(t_)
                t_.wait_ge(loaded, LOADS)
                t_.wait_ge(prep, 2)

                def project(p, b):
                    for kc in range(KC):
                        last = t_.matmul(ps[p % 2], wq[:, kc, p * P:(p + 1) * P], xT[:, kc, of(b)],
                                         start=(kc == 0), stop=(kc == 1))
                    return last

                def target(p, b):
                    t_.wait_ge(*act.at(f"tt{(p - 2) % HP}", b, 1 if p < 2 else 0))
                    for kc in range(KC):
                        t_.matmul(ps[4 + p % 2], wv[:, kc, p * P:(p + 1) * P], xT[:, kc, of(b)], start=(kc == 0), stop=False)
                    t_.wait_ge(*pool.at(f"z1{p}", b))
                    t_.matmul(ps[4 + p % 2], ident[:, :], kT(p, b), start=False, stop=True).then_inc(*pe.did(f"V{p}"))

                def turn(p, b):
                    t_.wait_ge(*(act.at(f"rw{p - 1}", b) if p else act.at("tt0", b)))
                    for t in range(TB):
                        last = t_.transpose(ps[6][:, t * P:(t + 1) * P], tT[:, p % 2, t * P:(t + 1) * P], ident[:, :])
                    last.then_inc(*pe.did(f"TR{p}"))

                project(0, 0).then_inc(prime_p, 1)
                with t_.Fori(0, B) as b:
                    for i in PR:
                        t_.wait_ge(*act.at(f"XP{(i - 1) % HP}", b, 1 if i < 2 else 0))
                        project(nxt(i), b if i < HP - 1 else (b + 1) % B).then_inc(*pe.did(f"x{nxt(i)}"))
                        for w_ in (1, 0):
                            t_.wait_ge(*dve.at(f"c3{w_}{i}", b))
                            t_.matmul(ps[2 + w_], pair[:, :], y[:, i % 2, w_, :], start=True, stop=True)\
                                .then_inc(*pe.did(f"r{w_}{i}"))
                        if i:
                            target(i - 1, b)
                        if i >= 2:
                            turn(i - 2, b)
                    target(HP - 1, b)
                    turn(HP - 2, b)
                    t_.wait_ge(*dve.at("lr", b, 1))
                    for kc in range(KC):
                        last = t_.matmul(ps[7], lrw[:, kc, :], xT[:, kc, of(b)], start=(kc == 0), stop=(kc == 1))
                    last.then_inc(*pe.did("lr"))
                    turn(HP - 1, b)
                    t_.wait_ge(*act.at("sig", b))
                    for t in range(TB):
                        last = t_.transpose(ps[7][:, t * P:(t + 1) * P], lrT[:, t * P:(t + 1) * P], ident[:, :])
                    last.then_inc(*pe.did("lt"))

            @block.vector
            def _(v):
                dve.open(v)
                v.wait_ge(loaded, LOADS)
                v.tensor_scalar(wv[:, :, :], wv[:, :, :], -1.0, None, ALU.mult).then_inc(prep, 1)
                v.tensor_tensor(bC[:, :], bC[:, :], gC[:, :], ALU.mult).then_inc(prep, 1)
                v.wait_ge(prime_a, 3)

                def tap(k, w_, i, b):
                    if k == 1:
                        v.wait_ge(*act.at(f"y{w_}{i}", b, 0 if i else 1))
                    else:
                        v.wait_ge(*dve.at(f"c{k - 1}{w_}{i}", b))
                    yy = y[:, i % 2, w_, :]
                    v.scalar_tensor_tensor(yy, XP[:, i % 2, k:k + N], cw[w_][:, i, k:k + 1], yy, ALU.mult, ALU.add)\
                        .then_inc(*dve.did(f"c{k}{w_}{i}"))

                def partner(w_, p, b):
                    v.wait_ge(*pe.at(f"r{w_}{p}", b))
                    v.wait_ge(*pool.at(f"z{w_}{(p - 2) % HP}", b, 1 if p < 2 else 0))
                    v.tensor_tensor(r2[:, p % 2, w_, :], ps[2 + w_], rope[:, 1, :], ALU.mult).then_inc(*dve.did(f"s{w_}{p}"))

                with v.Fori(0, B) as b:
                    for i in PR:
                        for k in range(1, KW):
                            for w_ in (1, 0):
                                tap(k, w_, i, b)
                            if k == 1 and i:
                                for w_ in (1, 0):
                                    partner(w_, i - 1, b)
                    for w_ in (1, 0):
                        partner(w_, HP - 1, b)
                    v.wait_ge(*pe.at("lt", b))
                    v.wait_ge(cst, b * (16 * 2 * TB) + 1)
                    v.tensor_scalar(rows_[:, :, :, HALF:HALF + HP],
                                    ps[7].rearrange("p (t n) -> p t n", t=TB)[:, :, 0:H1].rearrange("p t (a h) -> p t a h", a=2),
                                    1.0 / E1, None, ALU.mult).then_inc(*dve.did("lr"))

            @block.scalar
            def _(a):
                act.open(a)
                a.wait_ge(loaded, LOADS)
                a.wait_ge(padded, 4)
                a.wait_ge(prep, 2)
                a.activation(lrT[0:H1, 0:1], lrb[:, 0:1], ACT.Sigmoid).then_inc(prep, 1)
                a.wait_ge(prep, 3)

                def first_tap(p, w_):
                    return a.activation(y[:, p % 2, w_, :], XP[:, p % 2, 0:N], ACT.Identity, bias=cb[w_][:, p:p + 1],
                                        scale=cw[w_][:, p, 0:1])

                def scaled(p, b):
                    a.wait_ge(*pe.at(f"V{p}", b))
                    a.activation(tT[:, p % 2, :], ps[4 + p % 2], ACT.Identity, bias=bC[:, p:p + 1],
                                 scale=gC[:, p:p + 1]).then_inc(*act.did(f"tt{p}"))

                def into_rows(p, b):
                    a.wait_ge(*pe.at(f"TR{p}", b))
                    if p == 0:
                        a.wait_ge(cst, b * (16 * 2 * TB) + 1)
                    a.activation(rows_[:, :, :, p * E1:(p + 1) * E1], ps[6].rearrange("p (t a e) -> p t a e", t=TB, a=2),
                                 ACT.Copy).then_inc(*act.did(f"rw{p}"))

                a.wait_ge(prime_p, 1)
                a.activation(XP[:, 0, KW:KW + N], ps[0], ACT.Copy).then_inc(prime_a, 1)
                a.wait_ge(prime_a, 1)
                for w_ in (1, 0):
                    last = first_tap(0, w_)
                last.then_inc(prime_a, 2)
                with a.Fori(0, B) as b:
                    for i in PR:
                        p = nxt(i)
                        a.wait_ge(*pe.at(f"x{p}", b))
                        a.wait_ge(*dve.at(f"c30{(i - 1) % HP}", b, 0 if i else 1))
                        a.activation(XP[:, p % 2, KW:KW + N], ps[p % 2], ACT.Copy).then_inc(*act.did(f"XP{p}"))
                        a.wait_ge(*act.at(f"XP{p}", b))
                        for w_ in (1, 0):
                            a.wait_ge(*pe.at(f"r{w_}{(i - 1) % HP}", b, 0 if i else 1))
                            a.wait_ge(*pool.at(f"c{w_}{(i - 1) % HP}", b, 0 if i else 1))
                            first_tap(p, w_).then_inc(*act.did(f"y{w_}{p}"))
                        if i:
                            scaled(i - 1, b)
                        if i >= 2:
                            into_rows(i - 2, b)
                    scaled(HP - 1, b)
                    into_rows(HP - 2, b)
                    a.wait_ge(*pe.at("lr", b))
                    a.activation(lrT[0:H1, :], ps[7][0:H1, :], ACT.Sigmoid, bias=lrb[:, 0:1]).then_inc(*act.did("sig"))
                    into_rows(HP - 1, b)

            @block.gpsimd
            def _(g):
                pool.open(g)
                g.memset(XP[:, :, 0:KW], 0.0).then_inc(padded, 1)
                g.memset(rows_[:, :, :, HALF + HP:CL], 0.0).then_inc(padded, 1)
                g.memset(lrw[:, :, :], 0.0).then_inc(padded, 1)
                g.memset(lrT[:, :], 0.0).then_inc(padded, 1)
                g.wait_ge(loaded, LOADS)

                def rotated(w_, p, b):
                    g.wait_ge(*pool.at(f"c{w_}{p}", b))
                    g.wait_ge(*dve.at(f"s{w_}{p}", b))
                    if w_ == 0 and p == 0:
                        g.wait_ge(qst, b * (16 * HP) + 1)
                    g.tensor_tensor(kT(p, b) if w_ else qT[:, p, :], r1[:, p % 2, w_, :], r2[:, p % 2, w_, :], ALU.add)\
                        .then_inc(*pool.did(f"z{w_}{p}"))

                with g.Fori(0, B) as b:
                    for i in PR:
                        if i:
                            for w_ in (1, 0):
                                rotated(w_, i - 1, b)
                        for w_ in (1, 0):
                            g.wait_ge(*dve.at(f"c3{w_}{i}", b))
                            g.wait_ge(*pool.at(f"z{w_}{(i - 2) % HP}", b, 1 if i < 2 else 0))
                            g.tensor_tensor(r1[:, i % 2, w_, :], y[:, i % 2, w_, :], rope[:, 0, :], ALU.mult)\
                                .then_inc(*pool.did(f"c{w_}{i}"))
                    for w_ in (1, 0):
                        rotated(w_, HP - 1, b)


def ttt_recur(nc, M, ins):
    with ExitStack() as ctx:
        sb = lambda n, s, d=F32: ctx.enter_context(nc.sbuf_tensor(n, s, d))
        sem = lambda n: ctx.enter_context(nc.semaphore(n))
        G = 2
        GP, GC = HP // G, HALF // G
        Wsb, Bsb = sb("Wsb", [P, HP, B, E1]), sb("Bsb", [P, HALF])
        W0, B0 = sb("W0", [P, HALF]), sb("B0", [P, HALF])
        mean0 = sb("mean0", [P, 2, HP])
        KTz, ek = sb("KTz", [P, HP, B, 2, MB]), sb("ek", [P, HP, P])
        tgt, g2 = sb("tgt", [P, CL]), sb("g2", [P, HALF])
        t15, lastb = sb("t15", [P, 1]), sb("lastb", [P, P])
        eps = sb("r_eps", [P, 1])
        z, sq, xh, u, gx, pr = ([sb(f"{n}{g}", [P, GC]) for g in range(G)] for n in ("z_", "sq_", "xh_", "u_", "gx_", "pr_"))
        var, std, rs, rl, mm = ([sb(f"{n}{g}", [P, GP]) for g in range(G)] for n in ("var", "std_", "rs", "rl", "mm_"))
        sums = [sb(f"sums{g}", [P, 2, GP]) for g in range(G)]
        neg = [sb(f"neg{g}", [P, GP]) for g in range(G)]
        gr = sb("gr", [P, HALF])
        grD = sb("grD", [P, HP, B, E1])
        ident, blk, ps, ps2, kT_all = M["ident"], M["blk"], M["ps"], M["ps2"], M["kT_all"]
        BZ, Zps, TK = ps[3], ps[4:6], ps[6:8]
        loaded, primed_d, primed_p, primed_a, primed_g, primed_s = (sem("r_" + n) for n in ("loaded", "pr_d", "pr_p", "pr_a", "pr_g", "pr_s"))
        tgt_in, gr_out, snapped = sem("r_tgt"), sem("r_gr"), sem("r_snap")
        OPS = ["z", "sq", "var", "rs", "rl", "xh", "u", "gx", "m1", "pr", "m2", "neg", "t", "g", "d"]
        ORDER = [(o, g) for g in range(G) for o in OPS]
        dve = Steps(sem("r_dve"), [f"{o}{g}" for o, g in ORDER])
        act = Steps(sem("r_act"), ["std0", "W1", "B1", "ek0", "ek1", "kz0", "kz1", "d0", "std1", "W0", "B0", "d1"])
        pe = Steps(sem("r_pe"), ["T0", "T1", "Z1", "upd0", "bz0", "Z0", "upd1", "bz1"])
        b3 = lambda ap: ap.rearrange("p (h e) -> p h e", e=E1)
        bc = lambda ap: ap.unsqueeze(2).to_broadcast([P, ap.shape[1], E1])
        wps = [ps[p // 2][:, (p % 2) * B * E1:(p % 2 + 1) * B * E1] for p in range(HP)]

        def diagonal(g, b):
            r = slice(32 * b, 32 * b + 32)
            return grD[r, g * GP:(g + 1) * GP, b, :], b3(gr[r, g * GC:(g + 1) * GC])

        with nc.Block() as block:
            @block.sync
            def _(sp):
                sp.sem_inc(gr_out, 1)
                sp.dma_start(W0[:, :], ins["t_W1"]).then_inc(loaded, 16)
                for b in range(B):
                    for hh in range(2):
                        r0 = 32 * b + 16 * hh
                        for dst, src in ((B0, "t_b1"), (g2, "t_g")):
                            sp.dma_start(dst[r0:r0 + MB, :], ins[src][hh * HALF:(hh + 1) * HALF]
                                         .rearrange("(a n) -> a n", a=1).to_broadcast([MB, HALF])).then_inc(loaded, 16)
                sp.dma_start(t15[:, :], ins["t_idx"][MB - 1:MB].rearrange("(a n) -> a n", a=1).to_broadcast([P, 1]))\
                    .then_inc(loaded, 16)
                tg_of = lambda s: M["c_d"][:, :, bass.ds(s * MB, MB), :].rearrange("b h k n -> (b h) k n")
                sp.dma_start(tgt[:, :], tg_of(0)).then_inc(tgt_in, 16)
                sp.wait_ge(primed_a, 2)
                with sp.Fori(0, STEPS // SPT) as sc:
                    sp.wait_ge(*act.at("B1", sc * SPT))
                    sp.dma_start(M["W_d"][bass.ds(sc, 1)].rearrange("a p h b e -> (a p) (h b e)"),
                                 Wsb[:, :, :, :].rearrange("p h b e -> p (h b e)")).then_inc(snapped, 16)
                    sp.dma_start(M["B_d"][bass.ds(sc, 1)].rearrange("a p n -> (a p) n"), Bsb[:, :]).then_inc(snapped, 16)
                    with sp.Fori(0, SPT) as j:
                        s = sc * SPT + j
                        sp.wait_ge(*dve.at("gx1", s))
                        sp.dma_start(tgt[:, :], tg_of((s + 1) % STEPS)).then_inc(tgt_in, 16)
                        sp.wait_ge(*dve.at("g1", s))
                        sp.dma_start(M["g_d"][:, :, bass.ds(s * MB, MB), :].rearrange("b h k n -> (b h) k n"), gr[:, :]).then_inc(gr_out, 16)
                sp.wait_ge(gr_out, 16 * STEPS + 1)
                sp.wait_ge(tgt_in, 16 * (STEPS + 1))
                sp.wait_ge(snapped, 32 * (STEPS // SPT))

            @block.tensor
            def _(t_):
                pe.open(t_)
                t_.wait_ge(primed_d, 4)
                for i in range(HP // 2):
                    t_.matmul(ps[i].rearrange("p (h b e) -> p h b e", h=2, b=B), ident[:, :],
                              b3(W0[:, 2 * i * E1:(2 * i + 2) * E1]).unsqueeze(2).to_broadcast([P, 2, B, E1]),
                              start=True, stop=True, skip_group_check=True)
                t_.matmul(BZ[:, 0:HALF], ident[:, :], B0[:, :], start=True, stop=True, skip_group_check=True)\
                    .then_inc(primed_p, 1)

                def read_out(g):
                    for b in range(B):
                        for i in range(GP):
                            last = t_.matmul(Zps[g][32 * b:32 * b + 32, i * E1:(i + 1) * E1],
                                             KTz[:, g * GP + i, b, :, :].rearrange("p h k -> p (h k)"),
                                             Wsb[:, g * GP + i, b, :], start=True, stop=True)
                    return last

                t_.wait_ge(primed_a, 2)
                read_out(0).then_inc(primed_p, 1)
                with t_.Fori(0, STEPS // SPT) as sc:
                    with t_.Fori(0, SPT) as j:
                        s = sc * SPT + j
                        for g in range(G):
                            t_.wait_ge(*act.at("kz1", s, 1))
                            for i in range(GP):
                                last = t_.transpose(TK[g][:, i * P:(i + 1) * P],
                                                    KTz[:, g * GP + i, :, :, :].rearrange("p b h k -> p (b h k)"), ident[:, :])
                            last.then_inc(*pe.did(f"T{g}"))
                        t_.wait_ge(*act.at("W1", s))
                        read_out(1).then_inc(*pe.did("Z1"))
                        for g in range(G):
                            t_.wait_ge(*act.at(f"d{g}", s))
                            t_.wait_ge(*dve.at(f"d{g}", s))
                            for i in range(GP):
                                p = g * GP + i
                                last = t_.matmul(wps[p], ek[:, p, :], grD[:, p, :, :].rearrange("p b e -> p (b e)"),
                                                 start=False, stop=False, skip_group_check=True)
                            last.then_inc(*pe.did(f"upd{g}"))
                            t_.matmul(BZ[:, g * GC:(g + 1) * GC], lastb[:, :], gr[:, g * GC:(g + 1) * GC],
                                      start=False, stop=False, skip_group_check=True).then_inc(*pe.did(f"bz{g}"))
                            if g == 0:
                                t_.wait_ge(*act.at("W0", s))
                                read_out(0).then_inc(*pe.did("Z0"))

            @block.vector
            def _(v):
                dve.open(v)
                v.memset(eps[:, :], LN_EPS)
                v.wait_ge(loaded, 16 * 18)
                v.tensor_reduce(mean0[:, 0, :], b3(W0[:, :]), AX.X, ALU.add)
                v.tensor_reduce(mean0[:, 1, :], b3(B0[:, :]), AX.X, ALU.add)
                v.tensor_scalar(t15[:, :], t15[:, :], 1.0 / MB, None, ALU.add)
                v.tensor_tensor(g2[:, :], g2[:, :], g2[:, :], ALU.mult).then_inc(primed_d, 1)
                v.wait_ge(primed_d, 1)
                v.tensor_scalar(mean0[:, :, :], mean0[:, :, :], 1.0 / E1, None, ALU.mult)
                v.tensor_scalar(t15[:, :], t15[:, :], 0.0, -1.0, ALU.max, ALU.mult).then_inc(primed_d, 1)
                v.wait_ge(primed_d, 2)
                v.tensor_tensor(b3(W0[:, :]), b3(W0[:, :]), bc(mean0[:, 0, :]), ALU.subtract)
                v.tensor_tensor(b3(B0[:, :]), b3(B0[:, :]), bc(mean0[:, 1, :]), ALU.subtract)
                v.tensor_scalar(lastb[:, :], blk[:, :], t15[:, 0:1], None, ALU.mult).then_inc(primed_d, 2)
                v.wait_ge(primed_p, 2)
                v.wait_ge(primed_g, 2)

                def op(o, g, s):
                    cols = slice(g * GC, (g + 1) * GC)
                    me = lambda n, back=0: v.wait_ge(*dve.at(f"{n}{g}", s, back))
                    done = dve.did(f"{o}{g}") if o not in ("t", "g", "d") else None
                    if o == "z":
                        v.wait_ge(*pe.at(f"Z{g}", s, 1 - g))
                        v.wait_ge(*act.at(f"B{g}", s, 1 - g))
                        me("g", 1)
                        v.tensor_tensor(z[g][:, :], Zps[g][:, 0:GC], Bsb[:, cols], ALU.add).then_inc(*done)
                    elif o == "sq":
                        me("z")
                        v.tensor_tensor(sq[g][:, :], z[g][:, :], z[g][:, :], ALU.mult).then_inc(*done)
                    elif o == "var":
                        me("sq")
                        v.tensor_reduce(var[g][:, :], b3(sq[g][:, :]), AX.X, ALU.add).then_inc(*done)
                    elif o == "rs":
                        v.wait_ge(*act.at(f"std{g}", s))
                        v.reciprocal(rs[g][:, :], std[g][:, :]).then_inc(*done)
                    elif o == "rl":
                        me("rs")
                        v.wait_ge(tgt_in, 16 * s + 16)
                        v.tensor_tensor(rl[g][:, :], rs[g][:, :], tgt[:, HALF + g * GP:HALF + (g + 1) * GP], ALU.mult)\
                            .then_inc(*done)
                    elif o == "xh":
                        v.tensor_tensor(b3(xh[g][:, :]), b3(z[g][:, :]), bc(rs[g][:, :]), ALU.mult).then_inc(*done)
                    elif o == "u":
                        me("xh")
                        v.tensor_tensor(u[g][:, :], xh[g][:, :], g2[:, cols], ALU.mult).then_inc(*done)
                    elif o == "gx":
                        me("u")
                        v.tensor_tensor(gx[g][:, :], u[g][:, :], tgt[:, cols], ALU.add).then_inc(*done)
                    elif o == "m1":
                        me("gx")
                        v.tensor_reduce(sums[g][:, 0, :], b3(gx[g][:, :]), AX.X, ALU.add).then_inc(*done)
                    elif o == "pr":
                        v.scalar_tensor_tensor(pr[g][:, :], gx[g][:, :], -1.0 / E1, xh[g][:, :], ALU.mult, ALU.mult).then_inc(*done)
                    elif o == "m2":
                        me("pr")
                        v.tensor_reduce(sums[g][:, 1, :], b3(pr[g][:, :]), AX.X, ALU.add).then_inc(*done)
                    elif o == "neg":
                        v.tensor_scalar(neg[g][:, :], sums[g][:, 0, :], -1.0 / E1, None, ALU.mult).then_inc(*done)
                    elif o == "t":
                        me("m2")
                        for i in range(GP):
                            c = slice(i * E1, (i + 1) * E1)
                            last = v.scalar_tensor_tensor(gx[g][:, c], xh[g][:, c], sums[g][:, 1, i:i + 1], gx[g][:, c],
                                                          ALU.mult, ALU.add)
                        last.then_inc(*dve.did(f"t{g}"))
                    elif o == "g":
                        me("t")
                        v.wait_ge(gr_out, 16 * s + 1)
                        v.wait_ge(*pe.at(f"bz{g}", s, 1))
                        for i in range(GP):
                            c = slice(i * E1, (i + 1) * E1)
                            last = v.tensor_scalar(gr[:, (g * GP + i) * E1:(g * GP + i + 1) * E1], gx[g][:, c],
                                                   neg[g][:, i:i + 1], rl[g][:, i:i + 1], ALU.add, ALU.mult)
                        last.then_inc(*dve.did(f"g{g}"))
                    else:
                        me("g")
                        for b in (0, 1):
                            last = v.tensor_copy(*diagonal(g, b))
                        last.then_inc(*dve.did(f"d{g}"))

                with v.Fori(0, STEPS // SPT) as sc:
                    with v.Fori(0, SPT) as j:
                        for o, g in ORDER:
                            op(o, g, sc * SPT + j)

            @block.scalar
            def _(a):
                act.open(a)

                def copy_w(g):
                    flat = [x[:, :, :].rearrange("p a n -> p (a n)") for x in ps2[0:2]]
                    dst = Wsb[:, :, :, :].rearrange("p h b e -> p (h b e)")
                    W = B * E1
                    for c0, c1 in ([(0, 3 * W)], [(3 * W, 4 * W), (4 * W, 6 * W)])[g]:
                        last = a.activation(dst[:, c0:c1], flat[c0 // 1024][:, c0 % 1024:c0 % 1024 + c1 - c0], ACT.Copy)
                    return last

                def copy_b(g):
                    cols = slice(g * GC, (g + 1) * GC)
                    return a.activation(Bsb[:, cols], BZ[:, cols], ACT.Copy)

                def keys(s, hh):
                    r = slice(hh * E1, (hh + 1) * E1)
                    return a.activation(KTz[r, :, :, hh, :].rearrange("p h b k -> p (h b) k"),
                                        kT_all[r, :, :, bass.ds(s * MB, MB)].rearrange("p h b k -> p (h b) k"), ACT.Copy)

                a.wait_ge(primed_d, 1)
                a.activation(std[0][:, 0:1], eps[:, 0:1], ACT.Sqrt).then_inc(primed_s, 1)
                a.wait_ge(primed_s, 1)
                a.wait_ge(primed_p, 1)
                for g in range(G):
                    copy_w(g)
                    copy_b(g)
                a.wait_ge(primed_g, 2)
                keys(0, 0)
                keys(0, 1).then_inc(primed_a, 2)
                with a.Fori(0, STEPS // SPT) as sc:
                    with a.Fori(0, SPT) as j:
                        s = sc * SPT + j

                        def root(g):
                            a.wait_ge(*dve.at(f"var{g}", s))
                            a.activation(std[g][:, :], var[g][:, :], ACT.Sqrt, bias=eps[:, 0:1], scale=1.0 / E1)\
                                .then_inc(*act.did(f"std{g}"))

                        def state(g):
                            a.wait_ge(*pe.at(f"bz{g}", s, g))
                            copy_w(g).then_inc(*act.did(f"W{g}"))
                            copy_b(g).then_inc(*act.did(f"B{g}"))

                        def spread(g):
                            a.wait_ge(*dve.at(f"g{g}", s))
                            for b in (2, 3):
                                last = a.activation(*diagonal(g, b), ACT.Copy)
                            last.then_inc(*act.did(f"d{g}"))

                        root(0)
                        state(1)
                        for g in range(G):
                            a.wait_ge(*pe.at(f"T{g}", s))
                            a.activation(ek[:, g * GP:(g + 1) * GP, :].rearrange("p h c -> p (h c)"), TK[g][:, 0:GP * P],
                                         ACT.Identity, scale=t15[:, 0:1]).then_inc(*act.did(f"ek{g}"))
                        a.wait_ge(*pe.at("Z1", s))
                        for hh in range(2):
                            keys((s + 1) % STEPS, hh).then_inc(*act.did(f"kz{hh}"))
                        spread(0)
                        root(1)
                        a.wait_ge(snapped, 32 * sc + 32)
                        state(0)
                        spread(1)

            @block.gpsimd
            def _(g):
                g.memset(KTz[:, :, :, :, :], 0.0).then_inc(primed_g, 1)
                g.memset(grD[:, :, :, :], 0.0).then_inc(primed_g, 1)


def ttt_output(nc, M, ins):
    with ExitStack() as ctx:
        sb = lambda n, s, d=F32: ctx.enter_context(nc.sbuf_tensor(n, s, d))
        sem = lambda n: ctx.enter_context(nc.semaphore(n))
        TT, RING, SEQ = 8, 3, 8 // TB
        TURNS = TILES // TT
        qk = [sb(f"o_qk{r}", [P, 2, HP, P]) for r in range(RING)]
        Ws, Gs, brow = ([sb(f"o_{n}{r}", s) for r in range(RING)] for n, s in
                        (("W", [P, HALF]), ("G", [P, 2, HALF]), ("b", [1, CH])))
        xT = sb("o_xT", [DC, KC, SEQ * N])
        wg, wo = sb("o_wg", [DC, KC, CH]), sb("o_wo", [P, HP, D])
        gB, bB = sb("o_gB", [P, CH]), sb("o_bB", [P, CH])
        psc, pbc = sb("o_ps", [P, HP]), sb("o_pb", [P, HP])
        idx, same, prev = sb("o_idx", [P, P]), sb("o_same", [P, P]), sb("o_prev", [P, P])
        inv, i15 = sb("o_inv", [P, P]), sb("o_i15", [P, 1])
        ones = sb("o_ones", [1, P])
        eps = sb("o_eps", [P, 1])
        Sm = sb("o_Sm", [P, 2, HP, P])
        sq, zn = sb("o_sq", [P, CH]), [sb(f"o_zn{r}", [P, CH]) for r in range(2)]
        var, std, rs = sb("o_var", [P, H1]), sb("o_std", [P, H1]), sb("o_rs", [P, H1])
        st, mv, std2, rs2 = sb("o_st", [P, 2, 6]), sb("o_mv", [P, 2]), sb("o_std2", [P, 1]), sb("o_rs2", [P, 1])
        gate, yT = sb("o_gate", [P, HP, SEQ * N]), sb("o_yT", [P, HP, P])
        tick = sb("o_tick", [P, 1])
        h, ident, ps, ps2 = M["h"], M["ident"], M["ps"], M["ps2"]
        loaded, ready, masked = sem("o_loaded"), sem("o_ready"), sem("o_masked")
        tiles_in, xs_in = [sem(f"o_in{r}") for r in range(RING)], sem("o_xin")
        OUT = ps[7][:, 256:256 + D]
        steps = lambda *parts: [f"{n}{i - lag}" for i in range(TT + 3) for n, lag in parts if 0 <= i - lag < TT]
        GATES = [f"gate{k}" for k in range(SEQ * HP)]
        LASTG = GATES[-1]
        pe = Steps(sem("o_pe"), GATES + steps(("S", 0), ("q", 1), ("y", 3), ("Z", 0), ("T", 2)))
        dve = Steps(sem("o_dve"), steps(("Sm", 0), ("res", 3), ("zq", 1), ("stats", 1), ("aggr", 1), ("rp", 1), ("nrm", 1),
                                        ("var", 0), ("sc", 2), ("rs", 0), ("zn", 0)))
        act = Steps(sem("o_act"), GATES + steps(("sp", 1), ("sq", 0), ("std", 0)))
        pool = Steps(sem("o_pool"), steps(("g", 1), ("b", 1), ("y", 2)))
        LOADS = 16 * 7
        uses = [len(range(r, TT, RING)) for r in range(RING)]
        h3 = lambda ap: ap.rearrange("p (h e) -> p h e", e=E1)
        at = lambda i, lag: i - lag if 0 <= i - lag < TT else None

        with nc.Block() as block:
            @block.sync
            def _(sp):
                for dst, src in ((wg[:, :, :], ins["t_wg"].rearrange("(k p) n -> p k n", p=DC)),
                                 (wo[:, :, :], ins["t_wo"].rearrange("(c p) n -> p c n", p=P)),
                                 (gB[:, :], ins["t_g"].rearrange("(a n) -> a n", a=1).to_broadcast([P, CH])),
                                 (bB[:, :], ins["t_b"].rearrange("(a n) -> a n", a=1).to_broadcast([P, CH])),
                                 (psc[:, :], ins["t_ps"]), (pbc[:, :], ins["t_pb"]),
                                 (same[:, :], ins["c_same"]), (prev[:, :], ins["c_prev"]), (inv[:, :], ins["c_inv"]),
                                 (idx[:, :], ins["t_idx8"].rearrange("(a n) -> a n", a=1).to_broadcast([P, P]))):
                    sp.dma_start(dst, src).then_inc(loaded, 16)
                with sp.Fori(0, TURNS) as u:
                    sp.wait_ge(*pe.at(LASTG, u, 1))
                    sp.dma_start(xT[:, :, :], M["xT_d"][:, :, bass.ds(u * (SEQ * N), SEQ * N)]).then_inc(xs_in, 16)
                    for i in range(TT):
                        r, b, t = i % RING, u * SEQ + i // TB, i % TB
                        last = max(j for j in range(r, TT, RING))
                        sp.wait_ge(*(pe.at(f"q{i - RING}", u) if i >= RING else pe.at(f"q{last}", u, 1)))
                        for w_ in range(2):
                            sp.dma_start(qk[r][:, w_, :, :], M["qk1_d"][bass.ds(u * TT + i, 1), w_].rearrange("a p h n -> (a p) h n"))\
                                .then_inc(tiles_in[r], 16)
                        sp.dma_start(Ws[r][:, :].rearrange("p (h e) -> p h e", e=E1),
                                     M["W_d"][t, :, :, bass.ds(b, 1), :].rearrange("p h b e -> p (h b) e")).then_inc(tiles_in[r], 16)
                        for hh in range(2):
                            sp.dma_start(Gs[r][:, hh, :], M["g_d"][bass.ds(b, 1), hh, t * P:(t + 1) * P, :]
                                         .rearrange("a k n -> (a k) n")).then_inc(tiles_in[r], 16)
                            sp.dma_start(brow[r][:, hh * HALF:(hh + 1) * HALF],
                                         M["B_d"].rearrange("s (b h k) n -> s b h k n", b=B, h=2)[t, bass.ds(b, 1), hh, 0, :])\
                                .then_inc(tiles_in[r], 16)
                for r in range(RING):
                    sp.wait_ge(tiles_in[r], LOADS * uses[r] * TURNS)
                sp.wait_ge(xs_in, 16 * TURNS)

            @block.tensor
            def _(t_):
                pe.open(t_)
                t_.wait_ge(loaded, 160)
                t_.wait_ge(ready, 2)
                with t_.Fori(0, TURNS) as u:
                    t_.wait_ge(xs_in, 16 * u + 16)
                    t_.wait_ge(*dve.at(f"res{TT - 1}", u, 1))
                    for k in range(SEQ * HP):
                        s_, c = k // HP, k % HP
                        if k >= 2:
                            t_.wait_ge(*act.at(f"gate{k - 2}", u))
                        for kc in range(KC):
                            last = t_.matmul(ps[6 + k % 2], wg[:, kc, c * P:(c + 1) * P], xT[:, kc, s_ * N:(s_ + 1) * N],
                                             start=(kc == 0), stop=(kc == 1))
                        last.then_inc(*pe.did(f"gate{k}"))
                    for i in range(TT + 3):
                        if (n := at(i, 0)) is not None:
                            r = n % RING
                            t_.wait_ge(tiles_in[r], u * (LOADS * uses[r]) + LOADS * (n // RING + 1))
                            if n:
                                t_.wait_ge(*dve.at(f"Sm{n - 1}", u))
                            for hh in range(2):
                                rr = slice(hh * E1, (hh + 1) * E1)
                                for p in range(HP):
                                    last = t_.matmul(ps[2 * hh + p // 4][:, (p % 4) * P:(p % 4 + 1) * P], qk[r][rr, 1, p, :],
                                                     qk[r][rr, 0, p, :], start=True, stop=True)
                            last.then_inc(*pe.did(f"S{n}"))
                        if i >= 3:
                            t_.wait_ge(*dve.at(f"sc{i - 3}", u))
                        elif i:
                            t_.wait_ge(*(dve.at("zq0", u) if i == 2 else act.at(LASTG, u)))
                        if (n := at(i, 1)) is not None:
                            for p in range(HP):
                                last = t_.transpose(ps[6 + p // 4][:, (p % 4) * P:(p % 4 + 1) * P], qk[n % RING][:, 0, p, :],
                                                    ident[:, :])
                            last.then_inc(*pe.did(f"q{n}"))
                        if (n := at(i, 3)) is not None:
                            t_.wait_ge(*pool.at(f"y{n}", u))
                            for c in range(HP):
                                last = t_.matmul(OUT, yT[:, c, :], wo[:, c, :], start=(c == 0), stop=(c == HP - 1))
                            last.then_inc(*pe.did(f"y{n}"))
                        if (n := at(i, 0)) is not None:
                            r = n % RING
                            if n:
                                t_.wait_ge(*dve.at(f"zn{n - 1}", u))
                            for hh in range(2):
                                rr = slice(hh * E1, (hh + 1) * E1)
                                t_.matmul(ps[4 + hh][:, 0:HALF], ones[:, :], brow[r][:, hh * HALF:(hh + 1) * HALF],
                                          start=True, stop=False, skip_group_check=True)
                                for p in range(HP):
                                    t_.matmul(ps[4 + hh][:, p * E1:(p + 1) * E1], qk[r][rr, 0, p, :],
                                              Ws[r][rr, p * E1:(p + 1) * E1], start=False, stop=False, skip_group_check=True)
                            t_.wait_ge(*dve.at(f"Sm{n}", u))
                            for hh in range(2):
                                for p in range(HP):
                                    last = t_.matmul(ps[4 + hh][:, p * E1:(p + 1) * E1], Sm[:, hh, p, :],
                                                     Gs[r][:, hh, p * E1:(p + 1) * E1], start=False, stop=True,
                                                     skip_group_check=True)
                            last.then_inc(*pe.did(f"Z{n}"))
                        if (n := at(i, 2)) is not None:
                            t_.wait_ge(*(dve.at(f"zq{n + 1}", u) if n + 1 < TT else dve.at(f"res{n - 1}", u)))
                            for c in range(HP):
                                last = t_.transpose(ps[6 + c // 4][:, (c % 4) * P:(c % 4 + 1) * P],
                                                    zn[n % 2][:, c * P:(c + 1) * P], ident[:, :])
                            last.then_inc(*pe.did(f"T{n}"))

            @block.vector
            def _(v):
                dve.open(v)
                v.memset(eps[:, :], LN_EPS)
                v.memset(ones[:, :], 1.0)
                v.wait_ge(loaded, 160)
                v.tensor_tensor(idx[:, :], idx[:, :], inv[:, :], ALU.add).then_inc(ready, 1)
                v.wait_ge(ready, 1)
                v.tensor_scalar(inv[:, :], idx[:, :], 0.0, -1.0, ALU.max, ALU.mult).then_inc(masked, 1)
                v.wait_ge(masked, 1)
                v.tensor_tensor(same[:, :], same[:, :], inv[:, :], ALU.mult)
                v.tensor_copy(i15[:, :], inv[:, P - 1:P]).then_inc(masked, 1)
                v.wait_ge(masked, 2)
                v.scalar_tensor_tensor(idx[:, :], prev[:, :], i15[:, 0:1], same[:, :], ALU.mult, ALU.add).then_inc(ready, 1)
                v.wait_ge(ready, 2)
                with v.Fori(0, TURNS) as u:
                    for i in range(TT + 3):
                        if (n := at(i, 0)) is not None:
                            v.wait_ge(*pe.at(f"S{n}", u))
                            for hh in range(2):
                                for p0, m in ((0, 4), (4, 2)):
                                    last = v.scalar_tensor_tensor(
                                        Sm[:, hh, p0:p0 + m, :], ps[2 * hh + p0 // 4][:, 0:m * P].rearrange("p (h n) -> p h n", n=P),
                                        1.0, idx[:, :].unsqueeze(1).to_broadcast([P, m, P]), ALU.add, ALU.mult)
                            last.then_inc(*dve.did(f"Sm{n}"))
                        if (n := at(i, 3)) is not None:
                            v.wait_ge(*pe.at(f"y{n}", u))
                            v.tensor_tensor(row(h, u * TT + n), row(h, u * TT + n), OUT, ALU.add).then_inc(*dve.did(f"res{n}"))
                        if (n := at(i, 1)) is not None:
                            z = zn[n % 2]
                            v.wait_ge(*pool.at(f"b{n}", u))
                            v.wait_ge(*pe.at(f"q{n}", u))
                            for p0, m in ((0, 4), (4, 2)):
                                dst = z[:, :].rearrange("p (a h e) -> p h a e", a=2, e=E1)[:, p0:p0 + m, :, :]
                                last = v.tensor_tensor(dst, dst, ps[6 + p0 // 4][:, 0:m * P].rearrange("p (h a e) -> p h a e", a=2, e=E1),
                                                       ALU.add)
                            last.then_inc(*dve.did(f"zq{n}"))
                            v.wait_ge(*dve.at(f"zq{n}", u))
                            for hh in range(2):
                                last = v.bn_stats(st[:, hh, :], z[:, hh * HALF:(hh + 1) * HALF])
                            last.then_inc(*dve.did(f"stats{n}"))
                            v.wait_ge(*dve.at(f"stats{n}", u))
                            v.memset(tick[:, :], 0.0)
                            v.bn_aggr(mv[:, :], st[:, :, :]).then_inc(*dve.did(f"aggr{n}"))
                            v.wait_ge(*act.at(f"sp{n}", u))
                            v.reciprocal(rs2[:, :], std2[:, :]).then_inc(*dve.did(f"rp{n}"))
                            v.wait_ge(*dve.at(f"rp{n}", u))
                            v.tensor_scalar(z[:, :], z[:, :], mv[:, 0:1], rs2[:, 0:1], ALU.subtract, ALU.mult)\
                                .then_inc(*dve.did(f"nrm{n}"))
                        if (n := at(i, 0)) is not None:
                            v.wait_ge(*act.at(f"sq{n}", u))
                            v.tensor_reduce(var[:, :], h3(sq[:, :]), AX.X, ALU.add).then_inc(*dve.did(f"var{n}"))
                        if (n := at(i, 2)) is not None:
                            v.wait_ge(*pe.at(f"T{n}", u))
                            for c in range(HP):
                                last = v.tensor_scalar(yT[:, c, :], ps[6 + c // 4][:, (c % 4) * P:(c % 4 + 1) * P],
                                                       psc[:, c:c + 1], pbc[:, c:c + 1], ALU.mult, ALU.add)
                            last.then_inc(*dve.did(f"sc{n}"))
                        if (n := at(i, 0)) is not None:
                            v.wait_ge(*act.at(f"std{n}", u))
                            v.reciprocal(rs[:, :], std[:, :]).then_inc(*dve.did(f"rs{n}"))
                            v.wait_ge(*dve.at(f"rs{n}", u))
                            for hh in range(2):
                                last = v.tensor_tensor(h3(zn[n % 2][:, hh * HALF:(hh + 1) * HALF]), h3(ps[4 + hh][:, 0:HALF]),
                                                       rs[:, hh * HP:(hh + 1) * HP].unsqueeze(2).to_broadcast([P, HP, E1]), ALU.mult)
                            last.then_inc(*dve.did(f"zn{n}"))

            @block.scalar
            def _(a):
                act.open(a)
                a.wait_ge(loaded, 160)
                a.wait_ge(ready, 2)
                with a.Fori(0, TURNS) as u:
                    for k in range(SEQ * HP):
                        s_, c = k // HP, k % HP
                        a.wait_ge(*pe.at(f"gate{k}", u))
                        a.wait_ge(*pool.at(f"y{TT - 1}", u, 1))
                        a.activation(gate[:, c, s_ * N:(s_ + 1) * N], ps[6 + k % 2], ACT.Gelu_apprx_tanh)\
                            .then_inc(*act.did(f"gate{k}"))
                    for i in range(TT + 3):
                        if (n := at(i, 1)) is not None:
                            a.wait_ge(*dve.at(f"aggr{n}", u))
                            a.activation(std2[:, :], mv[:, 1:2], ACT.Sqrt, bias=eps[:, 0:1]).then_inc(*act.did(f"sp{n}"))
                        if (n := at(i, 0)) is not None:
                            a.wait_ge(*pe.at(f"Z{n}", u))
                            a.wait_ge(*(dve.at(f"var{n - 1}", u) if n else dve.at(f"var{TT - 1}", u, 1)))
                            a.activation(sq[:, :].rearrange("p (a n) -> p a n", a=2), ps2[2][:, :, 0:HALF], ACT.Square)\
                                .then_inc(*act.did(f"sq{n}"))
                            a.wait_ge(*dve.at(f"var{n}", u))
                            a.activation(std[:, :], var[:, :], ACT.Sqrt, bias=eps[:, 0:1], scale=1.0 / E1).then_inc(*act.did(f"std{n}"))

            @block.gpsimd
            def _(g):
                pool.open(g)
                g.wait_ge(loaded, 160)
                with g.Fori(0, TURNS) as u:
                    for i in range(TT + 3):
                        if (n := at(i, 1)) is not None:
                            z = zn[n % 2]
                            g.wait_ge(*dve.at(f"zn{n}", u))
                            g.tensor_tensor(z[:, :], z[:, :], gB[:, :], ALU.mult).then_inc(*pool.did(f"g{n}"))
                            g.wait_ge(*pool.at(f"g{n}", u))
                            g.tensor_tensor(z[:, :], z[:, :], bB[:, :], ALU.add).then_inc(*pool.did(f"b{n}"))
                        if (n := at(i, 2)) is not None:
                            g.wait_ge(*dve.at(f"sc{n}", u))
                            g.wait_ge(*act.at(LASTG, u))
                            g.tensor_tensor(yT[:, :, :], yT[:, :, :], gate[:, :, n * P:(n + 1) * P], ALU.mult)\
                                .then_inc(*pool.did(f"y{n}"))


E2, S2, H2 = 32, 32, 768
SL = E2 * S2
CJ = SL // P
HC = H2 // P
XE = 4
W2C = HC * D + HC


def load_expert(sp, M, ins, r, e):
    sp.dma_start(M["w1"][r][:, :, :], ins["m_w1"][bass.ds(e, 1)].rearrange("a p k n -> (a p) k n")).then_inc(M["w_in"][r], 16)
    sp.dma_start(M["w2"][r][:, :], ins["m_w2"][bass.ds(e, 1)].rearrange("a p n -> (a p) n")).then_inc(M["w_in"][r], 16)
    sp.dma_start(M["b2"][r][:, :], ins["m_b2"][bass.ds(e, 1), :]).then_inc(M["w_in"][r], 16)


def moe_dispatch(nc, M, ins):
    with ExitStack() as ctx:
        sb = lambda n, s, d=F32: ctx.enter_context(nc.sbuf_tensor(n, s, d))
        sem = lambda n: ctx.enter_context(nc.semaphore(n))
        L = ln_buffers(sb, "m_")
        phi, scale = sb("m_phi", [DC, KC, SL]), sb("m_scale", [P, 1])
        ones = sb("m_ones", [DC, P])
        xT = sb("m_xT", [DC, KC, N])
        Ed = [sb(f"m_E{i}", [P, SL]) for i in range(2)]
        dw, cw = sb("m_dw", [P, SL]), sb("m_cw", [P, SL])
        ss, nn, nr = sb("m_ss", [P, TB]), sb("m_nn", [P, TB]), sb("m_nr", [P, TB])
        mx, dm, f = ([sb(f"m_{n}{i}", [P, E2]) for i in range(2)] for n in ("mx", "dm", "f"))
        gm, se, rse, w = sb("m_gm", [P, 1]), sb("m_se", [P, E2]), sb("m_rse", [P, E2]), sb("m_w", [P, E2])
        tot, rtot = sb("m_tot", [P, 1]), sb("m_rtot", [P, 1])
        h, ident, ps, ps2 = M["h"], M["ident"], M["ps"], M["ps2"]
        cT, slT = M["cT"], M["slT"]
        xs = L["xn"]
        R = range(TB)
        loaded, prep, normed = sem("m_loaded"), sem("m_prep"), sem("m_normed")
        skew = lambda now, late: [n for i in range(TB + 1) for n in
                                  ([f"{o}{i}" for o in now] if i < TB else []) + ([f"{o}{i - 1}" for o in late] if i else [])]
        pe = Steps(sem("m_pe"), ["T0", "T1"] + skew(["L"], ["S", "C0", "C1"]))
        act = Steps(sem("m_act"), ["std", "nrm", "xT0", "xT1"] + skew(["E", "ex"], ["cT0", "cT1"]) + [f"sl{j}" for j in range(4)])
        dve = Steps(sem("m_dve"), LN_DVE + ["ss", "nx", "nr", "xs"]
                    + skew(["mx", "sb", "gm", "dm"], ["se", "rse", "w", "tot", "rtot", "f", "dw"]))
        pool = Steps(sem("m_pool"), ["sq"] + [f"cw{t}" for t in R])
        e3 = lambda ap: ap.rearrange("p (e s) -> p e s", s=S2)
        bc = lambda ap: ap.unsqueeze(2).to_broadcast([P, E2, S2])
        logits = ps2[0][:, :, :].rearrange("p a n -> p (a n)")
        sq4 = dw[:, 0:TB * D].rearrange("p (t d) -> p t d", t=TB)

        with nc.Block() as block:
            @block.sync
            def _(sp):
                sp.dma_start(phi[:, :, :], ins["m_phi"].rearrange("(k p) n -> p k n", p=DC)).then_inc(loaded, 16)
                sp.dma_start(scale[:, :], ins["m_scale"].rearrange("(a n) -> a n", a=1).to_broadcast([P, 1])).then_inc(loaded, 16)
                for r in range(XE):
                    load_expert(sp, M, ins, r, r)
                sp.wait_ge(loaded, 32)

            @block.tensor
            def _(t_):
                pe.open(t_)
                t_.wait_ge(prep, 2)
                for half in range(2):
                    for kc in range(KC):
                        last = t_.matmul(ps[half], ones[:, :], Ed[kc][0:DC, half * 512:(half + 1) * 512],
                                         start=(kc == 0), stop=(kc == 1))
                last.then_inc(normed, 1)
                t_.wait_ge(normed, 5)
                with t_.Fori(0, B) as b:
                    for c in range(KC):
                        t_.wait_ge(*dve.at("xs", b))
                        for t in R:
                            last = t_.transpose(ps[c][0:DC, t * P:(t + 1) * P], xs[:, t, c * DC:(c + 1) * DC], ident[:, :])
                        last.then_inc(*pe.did(f"T{c}"))
                    for i in range(TB + 1):
                        if i < TB:
                            t_.wait_ge(*(dve.at(f"sb{i - 1}", b) if i else act.at("xT1", b)))
                            for half in range(2):
                                for kc in range(KC):
                                    last = t_.matmul(ps[half], xT[:, kc, i * P:(i + 1) * P], phi[:, kc, half * 512:(half + 1) * 512],
                                                     start=(kc == 0), stop=(kc == 1))
                            last.then_inc(*pe.did(f"L{i}"))
                        if i:
                            t = i - 1
                            t_.wait_ge(*dve.at(f"dw{t}", b))
                            if t == 0:
                                t_.wait_ge(*act.at("sl3", b, 1))
                            for kc in range(KC):
                                for half in range(2):
                                    last = t_.matmul(ps[2 + 2 * kc + half][0:DC, :], xs[:, t, kc * DC:(kc + 1) * DC],
                                                     dw[:, half * 512:(half + 1) * 512], start=(t == 0), stop=(t == TB - 1),
                                                     skip_group_check=True)
                            last.then_inc(*pe.did(f"S{t}"))
                            for k in range(2):
                                t_.wait_ge(*pool.at(f"cw{t}", b))
                                t_.wait_ge(*(act.at(f"cT{k}{t - 1}", b) if t else act.at(f"cT{k}{TB - 1}", b, 1)))
                                for j in range(4):
                                    last = t_.transpose(ps[6 + k][:, j * P:(j + 1) * P], cw[:, (4 * k + j) * P:(4 * k + j + 1) * P],
                                                        ident[:, :])
                                last.then_inc(*pe.did(f"C{k}{t}"))

            @block.vector
            def _(v):
                dve.open(v)
                v.memset(L["eps"][:, :], LN_EPS)
                v.memset(ones[:, :], 1.0).then_inc(prep, 1)
                v.wait_ge(normed, 3)
                v.tensor_scalar(cw[0:DC, :], cw[0:DC, :], FLOOR, None, ALU.max).then_inc(prep, 1)
                v.wait_ge(prep, 3)
                v.reciprocal(dw[0:DC, :], cw[0:DC, :]).then_inc(prep, 1)
                v.wait_ge(prep, 4)
                v.tensor_scalar(dw[0:DC, :], dw[0:DC, :], scale[0:DC, 0:1], None, ALU.mult).then_inc(prep, 1)
                v.wait_ge(prep, 5)
                for kc in range(KC):
                    v.tensor_tensor(phi[:, kc, :], phi[:, kc, :], dw[0:DC, :], ALU.mult).then_inc(normed, 1)
                v.wait_ge(normed, 5)
                with v.Fori(0, B) as b:
                    ln_dve(v, L, h, b, dve, act, pe)
                    v.wait_ge(*pool.at("sq", b))
                    v.tensor_reduce(ss[:, :], sq4, AX.X, ALU.add).then_inc(*dve.did("ss"))
                    v.wait_ge(*act.at("nrm", b))
                    v.tensor_scalar(nn[:, :], nn[:, :], FLOOR, None, ALU.max).then_inc(*dve.did("nx"))
                    v.wait_ge(*dve.at("nx", b))
                    v.reciprocal(nr[:, :], nn[:, :]).then_inc(*dve.did("nr"))
                    v.wait_ge(*dve.at("nr", b))
                    for t in R:
                        last = v.tensor_scalar(xs[:, t, :], xs[:, t, :], nr[:, t:t + 1], None, ALU.mult)
                    last.then_inc(*dve.did("xs"))
                    for i in range(TB + 1):
                        if i < TB:
                            q = i % 2
                            v.wait_ge(*pe.at(f"L{i}", b))
                            v.tensor_reduce(mx[q][:, :], e3(logits), AX.X, ALU.max).then_inc(*dve.did(f"mx{i}"))
                            v.wait_ge(*dve.at(f"mx{i}", b))
                            v.wait_ge(*pool.at(f"cw{(i - 2) % TB}", b, 1 if i < 2 else 0))
                            v.tensor_tensor(e3(Ed[q][:, :]), e3(logits), bc(mx[q][:, :]), ALU.subtract).then_inc(*dve.did(f"sb{i}"))
                            v.tensor_reduce(gm[:, :], mx[q][:, :], AX.X, ALU.max).then_inc(*dve.did(f"gm{i}"))
                            v.wait_ge(*dve.at(f"gm{i}", b))
                            v.tensor_scalar(dm[q][:, :], mx[q][:, :], gm[:, 0:1], None, ALU.subtract).then_inc(*dve.did(f"dm{i}"))
                        if i:
                            t, q = i - 1, (i - 1) % 2
                            me = lambda n: v.wait_ge(*dve.at(f"{n}{t}", b))
                            v.wait_ge(*act.at(f"ex{t}", b))
                            v.tensor_reduce(se[:, :], e3(Ed[q][:, :]), AX.X, ALU.add).then_inc(*dve.did(f"se{t}"))
                            me("se")
                            v.reciprocal(rse[:, :], se[:, :]).then_inc(*dve.did(f"rse{t}"))
                            v.tensor_tensor(w[:, :], se[:, :], dm[q][:, :], ALU.mult).then_inc(*dve.did(f"w{t}"))
                            me("w")
                            v.tensor_reduce(tot[:, :], w[:, :], AX.X, ALU.add).then_inc(*dve.did(f"tot{t}"))
                            me("tot")
                            v.reciprocal(rtot[:, :], tot[:, :]).then_inc(*dve.did(f"rtot{t}"))
                            me("rtot")
                            v.tensor_scalar(f[q][:, :], dm[q][:, :], rtot[:, 0:1], None, ALU.mult).then_inc(*dve.did(f"f{t}"))
                            v.wait_ge(*(pe.at(f"S{t - 1}", b) if t else pe.at("S3", b, 1)))
                            v.tensor_tensor(e3(dw[:, :]), e3(Ed[q][:, :]), bc(rse[:, :]), ALU.mult).then_inc(*dve.did(f"dw{t}"))

            @block.scalar
            def _(a):
                act.open(a)
                a.wait_ge(loaded, 32)
                for kc in range(KC):
                    last = a.activation(Ed[kc][0:DC, :], phi[:, kc, :], ACT.Square)
                last.then_inc(prep, 1)
                a.wait_ge(normed, 1)
                for half in range(2):
                    a.activation(cw[0:DC, half * 512:(half + 1) * 512], ps[half][0:DC, :], ACT.Sqrt).then_inc(normed, 1)
                a.wait_ge(normed, 5)
                with a.Fori(0, B) as b:
                    ln_std(a, L, b, dve, act)
                    a.wait_ge(*dve.at("ss", b))
                    a.activation(nn[:, :], ss[:, :], ACT.Sqrt).then_inc(*act.did("nrm"))
                    for c in range(KC):
                        a.wait_ge(*pe.at(f"T{c}", b))
                        a.activation(xT[:, c, :], ps[c][0:DC, :], ACT.Copy).then_inc(*act.did(f"xT{c}"))
                    for i in range(TB + 1):
                        if i < TB:
                            q = i % 2
                            a.wait_ge(*dve.at(f"sb{i}", b))
                            a.activation(Ed[q][:, :], Ed[q][:, :], ACT.Exp).then_inc(*act.did(f"E{i}"))
                            a.wait_ge(*dve.at(f"dm{i}", b))
                            a.activation(dm[q][:, :], dm[q][:, :], ACT.Exp).then_inc(*act.did(f"ex{i}"))
                        if i:
                            for k in range(2):
                                a.wait_ge(*pe.at(f"C{k}{i - 1}", b))
                                a.activation(cT[:, bass.ds(b * TB + i - 1, 1), 4 * k:4 * k + 4, :].rearrange("p a c n -> p (a c n)"),
                                             ps[6 + k], ACT.Copy).then_inc(*act.did(f"cT{k}{i - 1}"))
                    for kc in range(KC):
                        for half in range(2):
                            a.activation(slT[:, kc, 16 * half:16 * half + 16, bass.ds(b * S2, S2)],
                                         e3(ps[2 + 2 * kc + half][0:DC, :]), ACT.Copy).then_inc(*act.did(f"sl{2 * kc + half}"))

            @block.gpsimd
            def _(g):
                pool.open(g)
                with g.Fori(0, B) as b:
                    g.wait_ge(*dve.at("xn3", b))
                    g.wait_ge(*pe.at("S3", b, 1))
                    g.tensor_tensor(sq4, L["xn"][:, :, :], L["xn"][:, :, :], ALU.mult).then_inc(*pool.did("sq"))
                    for t in R:
                        g.wait_ge(*dve.at(f"f{t}", b))
                        g.wait_ge(*(pe.at(f"C1{t - 1}", b) if t else pe.at("C13", b, 1)))
                        g.tensor_tensor(e3(cw[:, :]), e3(Ed[t % 2][:, :]), bc(f[t % 2][:, :]), ALU.mult).then_inc(*pool.did(f"cw{t}"))


def moe_experts(nc, M, ins):
    with ExitStack() as ctx:
        sb = lambda n, s, d=F32: ctx.enter_context(nc.sbuf_tensor(n, s, d))
        sem = lambda n: ctx.enter_context(nc.semaphore(n))
        gT = [sb(f"x_g{i}", [P, HC, P]) for i in range(2)]
        eo = [sb(f"x_eo{r}", [P, D]) for r in range(XE)]
        ones = sb("x_ones", [1, P])
        ps, ps2, slT, eo_all = M["ps"], M["ps2"], M["slT"], M["eo_all"]
        w1, w2, b2, w_in = M["w1"], M["w2"], M["b2"], M["w_in"]
        prep = sem("x_prep")
        moved = [sem(f"x_moved{r}") for r in range(XE)]
        R = range(XE)
        pe = Steps(sem("x_pe"), ["H0"] + [n for r in range(1, XE) for n in (f"H{r}", f"E{r - 1}")] + [f"E{XE - 1}"])
        act = Steps(sem("x_act"), [f"G{r}{k}" for r in R for k in range(2)])
        dve = Steps(sem("x_dve"), [f"c{r}" for r in R])
        TURNS = E2 // XE

        def move(sp, q, r):
            sp.wait_ge(*dve.at(f"c{r}", q))
            for b in range(B):
                sp.dma_start(eo_all[r * S2:(r + 1) * S2, b, bass.ds(q, 1), :].rearrange("p a n -> p (a n)"),
                             eo[r][b * S2:(b + 1) * S2, :]).then_inc(moved[r], 16)

        with nc.Block() as block:
            @block.sync
            def _(sp):
                for r in R:
                    sp.sem_inc(moved[r], 1)
                with sp.Fori(0, TURNS - 1) as q:
                    for r in R:
                        sp.wait_ge(*pe.at(f"E{r}", q))
                        load_expert(sp, M, ins, r, q * XE + XE + r)
                        move(sp, q, r)
                for r in R:
                    move(sp, TURNS - 1, r)
                for r in R:
                    sp.wait_ge(moved[r], 16 * B * TURNS + 1)

            @block.tensor
            def _(t_):
                pe.open(t_)
                t_.wait_ge(prep, 1)
                with t_.Fori(0, TURNS) as q:
                    for i in range(XE + 1):
                        if i < XE:
                            t_.wait_ge(w_in[i], q * 48 + 48)
                            t_.wait_ge(*(act.at(f"G{i - 2}1", q) if i >= 2 else act.at(f"G{XE - 2 + i}1", q, 1)))
                            for c in range(HC):
                                for kc in range(KC):
                                    last = t_.matmul(ps[2 * (i % 2) + c // 3][:, (c % 3) * P:(c % 3 + 1) * P],
                                                     w1[i][:, kc, c * P:(c + 1) * P],
                                                     slT[:, kc, bass.ds(q * XE + i, 1), :].rearrange("p a n -> p (a n)"),
                                                     start=(kc == 0), stop=(kc == 1))
                            last.then_inc(*pe.did(f"H{i}"))
                        if i:
                            r = i - 1
                            bank = ps[4 + r % 2][:, 0:D]
                            t_.wait_ge(*(dve.at(f"c{r - 2}", q) if r >= 2 else dve.at(f"c{XE - 2 + r}", q, 1)))
                            t_.matmul(bank, ones[:, :], b2[r][:, :], start=True, stop=False)
                            t_.wait_ge(*act.at(f"G{r}1", q))
                            for c in range(HC):
                                last = t_.matmul(bank, gT[r % 2][:, c, :], w2[r][:, c * D:(c + 1) * D], start=False,
                                                 stop=(c == HC - 1))
                            last.then_inc(*pe.did(f"E{r}"))

            @block.scalar
            def _(a):
                act.open(a)
                with a.Fori(0, TURNS) as q:
                    for r in R:
                        a.wait_ge(*pe.at(f"H{r}", q))
                        for c in range(HC):
                            last = a.activation(gT[r % 2][:, c, :], ps[2 * (r % 2) + c // 3][:, (c % 3) * P:(c % 3 + 1) * P],
                                                ACT.Gelu, bias=w2[r][:, HC * D + c:HC * D + c + 1])
                            if c % 3 == 2:
                                last.then_inc(*act.did(f"G{r}{c // 3}"))

            @block.vector
            def _(v):
                dve.open(v)
                v.memset(ones[:, :], 1.0).then_inc(prep, 1)
                with v.Fori(0, TURNS) as q:
                    for r in R:
                        v.wait_ge(*pe.at(f"E{r}", q))
                        v.wait_ge(moved[r], q * (16 * B) + 1)
                        v.tensor_copy(eo[r][:, :], ps[4 + r % 2][:, 0:D]).then_inc(*dve.did(f"c{r}"))


def moe_combine(nc, M, ins, out):
    with ExitStack() as ctx:
        sb = lambda n, s, d=F32: ctx.enter_context(nc.sbuf_tensor(n, s, d))
        sem = lambda n: ctx.enter_context(nc.semaphore(n))
        cb = [sb(f"y_c{i}", [P, CJ, P]) for i in range(2)]
        h, ps, cT, eo_all = M["h"], M["ps"], M["cT"], M["eo_all"]
        R = range(TB)
        pe = Steps(sem("y_pe"), [f"y{t}" for t in R])
        act = Steps(sem("y_act"), [f"c{t}" for t in R])
        dve = Steps(sem("y_dve"), [f"add{t}" for t in R])
        stored = sem("y_stored")

        with nc.Block() as block:
            @block.sync
            def _(sp):
                with sp.Fori(0, B) as b:
                    sp.wait_ge(*dve.at(f"add{TB - 1}", b))
                    sp.dma_start(out[bass.ds(b, 1)].rearrange("a (t p) d -> p (a t) d", p=P), rows(h, b * TB, TB)).then_inc(stored, 16)
                sp.wait_ge(stored, 16 * B)

            @block.scalar
            def _(a):
                act.open(a)
                with a.Fori(0, B) as b:
                    for t in R:
                        a.wait_ge(*(pe.at(f"y{t - 2}", b) if t >= 2 else pe.at(f"y{TB - 2 + t}", b, 1)))
                        a.activation(cb[t % 2][:, :, :].rearrange("p c n -> p (c n)"),
                                     cT[:, bass.ds(b * TB + t, 1), :, :].rearrange("p a c n -> p (a c n)"), ACT.Copy)\
                            .then_inc(*act.did(f"c{t}"))

            @block.tensor
            def _(t_):
                pe.open(t_)
                with t_.Fori(0, B) as b:
                    for t in R:
                        t_.wait_ge(*act.at(f"c{t}", b))
                        t_.wait_ge(*(dve.at(f"add{t - 2}", b) if t >= 2 else dve.at(f"add{TB - 2 + t}", b, 1)))
                        for c in range(CJ):
                            last = t_.matmul(ps[t % 2][:, 0:D], cb[t % 2][:, c, :],
                                             eo_all[:, bass.ds(b, 1), c, :].rearrange("p a n -> p (a n)"),
                                             start=(c == 0), stop=(c == CJ - 1))
                        last.then_inc(*pe.did(f"y{t}"))

            @block.vector
            def _(v):
                dve.open(v)
                with v.Fori(0, B) as b:
                    for t in R:
                        v.wait_ge(*pe.at(f"y{t}", b))
                        v.tensor_tensor(row(h, b * TB + t), row(h, b * TB + t), ps[t % 2][:, 0:D], ALU.add)\
                            .then_inc(*dve.did(f"add{t}"))


def soft_experts(nc, M, ins, out):
    with ExitStack() as ctx:
        sb = lambda n, s, d=F32: ctx.enter_context(nc.sbuf_tensor(n, s, d))
        M["cT"], M["slT"] = sb("cT", [P, TILES, CJ, P]), sb("slT", [DC, KC, E2, P])
        M["w1"] = [sb(f"w1_{r}", [DC, KC, H2]) for r in range(XE)]
        M["w2"] = [sb(f"w2_{r}", [P, W2C]) for r in range(XE)]
        M["b2"] = [sb(f"b2_{r}", [1, D]) for r in range(XE)]
        M["w_in"] = [ctx.enter_context(nc.semaphore(f"w_in{r}")) for r in range(XE)]
        moe_dispatch(nc, M, ins)
        M["eo_all"] = sb("eo_all", [P, B, CJ, D])
        moe_experts(nc, M, ins)
        moe_combine(nc, M, ins, out)


def program(nc, ins, out):
    with ExitStack() as ctx:
        sb = lambda n, s, d=F32: ctx.enter_context(nc.sbuf_tensor(n, s, d))
        M = {"h": sb("h", [P, TILES, D]), "ident": sb("ident", [P, P]), "pair": sb("pair", [P, P]),
             "blk": sb("blk", [P, P])}
        bank = [ctx.enter_context(nc.psum_tensor(f"bank{i}", [P, 2, 512], F32)) for i in range(4)]
        M["ps2"] = bank
        M["ps"] = [bank[i // 2][:, i % 2, :] for i in range(8)]
        embed(nc, M, ins)
        with ExitStack() as c1:
            M["V1"] = c1.enter_context(nc.sbuf_tensor("V1", [P, TILES, HA, VP], F32))
            M["qk_d"] = nc.dram_tensor("qk_d", (B, QUADS, 2, SPLIT, 4 * DH, N), BF16, kind="Internal").ap()
            qkv(nc, M, ins)
            attention(nc, M, ins)
        switch_ffn(nc, M, ins)
        for n, s_ in (("qk1_d", (TILES, 2, P, HP, P)), ("c_d", (B, 2, N, CL)), ("g_d", (B, 2, N, HALF)),
                      ("W_d", (STEPS // SPT, P, HP, B, E1)), ("B_d", (STEPS // SPT, P, HALF)), ("xT_d", (DC, KC, B * N))):
            M[n] = nc.dram_tensor(n, s_, F32, kind="Internal").ap()
        with ExitStack() as c1:
            M["kT_all"] = c1.enter_context(nc.sbuf_tensor("kT_all", [P, HP, B, N], F32))
            with ExitStack() as c2:
                xT = c2.enter_context(nc.sbuf_tensor("t_xT", [DC, KC, B * N], F32))
                with ExitStack() as c3:
                    normalise(nc, M, "tn_", c3.enter_context(nc.sbuf_tensor("t_xn", [P, TILES, D], F32)), xT)
                ttt_prepare(nc, M, ins, xT)
            ttt_recur(nc, M, ins)
        ttt_output(nc, M, ins)
        soft_experts(nc, M, ins, out)


def host_constants():
    i = np.arange(P)
    ident = np.eye(P, dtype=np.float32)
    pair = np.zeros((P, P), np.float32)
    pair[i ^ 1, i] = 1.0
    blk = (i[:, None] // 16 == i[None, :] // 16).astype(np.float32)
    spread = np.zeros((E0, CE, 2, R0), np.float32)
    for e in range(E0):
        spread[e, e // 2, e % 2] = 1.0
    rank8 = np.broadcast_to(np.arange(E0, 0, -1, dtype=np.float32), (P, TB, E0)).reshape(P, TB * E0)
    s_, t_ = i[:, None], i[None, :]
    same = ((s_ // MB == t_ // MB) & (s_ <= t_)).astype(np.float32)
    prev = (s_ // MB < t_ // MB).astype(np.float32)
    inv = np.broadcast_to((np.float32(1.0) / np.arange(1, MB + 1, dtype=np.float32)), (P, SPT, MB)).reshape(P, P)
    freq = (1.0 / np.float32(10000.0) ** (np.arange(0, E1, 2, dtype=np.float32) / np.float32(E1))).astype(np.float32)
    ang = np.arange(N, dtype=np.float32)[None, :] * freq[:, None]
    c, s = np.repeat(np.cos(ang), 2, 0), np.repeat(np.sin(ang), 2, 0)
    s[0::2] *= -1
    rope = np.stack([np.tile(c, (2, 1)), np.tile(s, (2, 1))], 1).astype(np.float32)
    return {"c_same": same, "c_prev": prev, "c_inv": inv, "c_rope": rope, "c_spread": spread.reshape(E0, CE * P), "c_rank8": rank8, "c_ident": ident, "c_pair": pair, "c_blk": blk}


def layout(inputs):
    g = {k: np.asarray(v) for k, v in inputs.items()}
    kv = g["L0_attn_Wkv"].reshape(HA, 2, DH, D)
    a = {
        "x": g["x"], "tune_ids": g["L0_tok_tune_ids"], "base_weight": g["L0_tok_base_weight"],
        "train_weight": g["L0_tok_train_weight"],
        "WqT": g["L0_attn_Wq"].T, "WkT": kv[:, 0].reshape(D, D).T, "WvT": kv[:, 1].reshape(D, D).T,
        "WprojT": g["L0_attn_Wproj"].T,
        "enc_w": g["L0_ffn_enc_w"], "enc_b": g["L0_ffn_enc_b"], "sw_w": g["L0_ffn_sw_w"], "sw_b": g["L0_ffn_sw_b"],
        "f_w1": g["L0_ffn_w1"].transpose(1, 0, 2).reshape(D, E0 * R0), "f_b1": g["L0_ffn_b1"].reshape(CE, P).T,
        "f_w2": g["L0_ffn_w2"].reshape(E0 * R0, D), "f_b2": g["L0_ffn_b2"],
    }
    halves = lambda w: w.reshape(-1, 2, HP, E1)
    chan = lambda w: halves(w).transpose(1, 3, 2, 0).reshape(P, HP, -1)
    a.update({
        "t_wq": halves(g["L1_attn_wq"]).transpose(0, 2, 1, 3).reshape(D, CH), "t_wv": halves(g["L1_attn_wv"]).transpose(0, 2, 1, 3).reshape(D, CH),
        "t_wg": g["L1_attn_wg"], "t_wo": g["L1_attn_wo"], "t_lrw": g["L1_attn_lr_w"].T, "t_lrb": g["L1_attn_lr_b"],
        "t_cwq": chan(g["L1_attn_conv_q_w"]), "t_cwk": chan(g["L1_attn_conv_k_w"]),
        "t_cbq": chan(g["L1_attn_conv_q_b"][None])[:, :, 0], "t_cbk": chan(g["L1_attn_conv_k_b"][None])[:, :, 0],
        "t_gc": chan(g["L1_attn_ttt_norm_scale"].reshape(1, CH))[:, :, 0],
        "t_bc": chan(g["L1_attn_ttt_norm_bias"].reshape(1, CH))[:, :, 0],
        "t_g": g["L1_attn_ttt_norm_scale"].reshape(CH), "t_b": g["L1_attn_ttt_norm_bias"].reshape(CH),
        "t_idx": g["L1_attn_learnable_token_idx"], "t_idx8": np.tile(g["L1_attn_learnable_token_idx"], SPT),
        "t_ps": g["L1_attn_post_norm_scale"].reshape(HP, P).T, "t_pb": g["L1_attn_post_norm_bias"].reshape(HP, P).T,
        "t_W1": g["L1_attn_W1"].reshape(2, HP, E1, E1).transpose(0, 2, 1, 3).reshape(P, HALF),
        "t_b1": g["L1_attn_b1"].reshape(CH),
    })
    up = lambda w, p: w.reshape(E2, -1, p, w.shape[-1]).transpose(0, 2, 1, 3)
    b1 = g["L1_ffn_b1"].reshape(E2, HC, P).transpose(0, 2, 1)
    a.update({
        "m_phi": g["L1_ffn_phi"].reshape(D, SL), "m_scale": g["L1_ffn_scale"], "m_w1": up(g["L1_ffn_w1"], DC),
        "m_w2": np.concatenate([up(g["L1_ffn_w2"], P).reshape(E2, P, HC * D), b1], axis=2), "m_b2": g["L1_ffn_b2"],
    })
    a.update(host_constants())
    return {k: np.ascontiguousarray(v) for k, v in a.items()}


def kernel(**inputs):
    import concourse.bacc as bacc
    from concourse.bass_utils import run_bass_kernel_spmd

    nc = bacc.Bacc("TRN2", target_bir_lowering=False, num_devices=1)
    arrays = {f"in_{k}": v for k, v in layout(inputs).items()}
    ins = {k[3:]: nc.dram_tensor(k, v.shape, mybir.dt.from_np(v.dtype), kind="ExternalInput").ap()
           for k, v in arrays.items()}
    out = nc.dram_tensor("out_0", (B, N, D), F32, kind="ExternalOutput").ap()
    program(nc, ins, out)
    r = run_bass_kernel_spmd(nc, [arrays], core_ids=[0])
    return r.results[0]["out_0"]
```
